# Optimizing a Trainium2 kernel written in Bass

```python
import numpy as np
import jax
import jax.numpy as jnp

def _softmax(x, axis=-1):
    return jax.nn.softmax(x, axis=axis)

def _gelu(x):
    return jax.nn.gelu(x, approximate=True)

def _silu(x):
    return jax.nn.silu(x)

def _sigmoid(x):
    return jax.nn.sigmoid(x)

def _layernorm(x, axis=-1, eps=1e-05):
    m = jnp.mean(x, axis=axis, keepdims=True)
    v = jnp.var(x, axis=axis, keepdims=True)
    return (x - m) / jnp.sqrt(v + eps)

def _scatter_add(tgt, idx, src, axis=0):
    return tgt.at[idx].add(src)

def _segment_sum(src, seg, n):
    return jax.ops.segment_sum(src, seg, n)
kernel_name = 'mk_adaln_d1_jaxref_r8_51ddaf'

def setup_inputs(seed: int=0):
    np.random.seed(seed)
    _w = jnp.asarray

    def _L0_attn_setup():
        import jax, jax.numpy as jnp
        import numpy as np
        import math
        B, T = (4, 128)
        D_MODEL = 256
        HEAD_DIM = 64
        N_HEADS = 32
        N_KV = 8
        Q_MULT = N_HEADS // N_KV
        SLIDING_WINDOW = 128
        CAUSAL = True
        SM_SCALE = 1.0 / math.sqrt(HEAD_DIM)
        ROPE_THETA = 150000.0
        SCALING = 32.0
        NTK_ALPHA = 1.0
        NTK_BETA = 32.0
        ICL = 128

        def _rope_cos_sin(t_len):
            d_half = HEAD_DIM // 2
            freq = ROPE_THETA ** (np.arange(0, HEAD_DIM, 2, dtype=np.float32) / HEAD_DIM)
            concentration = 0.1 * math.log(SCALING) + 1.0
            low = d_half * math.log(ICL / (NTK_BETA * 2 * math.pi)) / math.log(ROPE_THETA)
            high = d_half * math.log(ICL / (NTK_ALPHA * 2 * math.pi)) / math.log(ROPE_THETA)
            interpolation = 1.0 / (SCALING * freq)
            extrapolation = 1.0 / freq
            ramp = np.clip((np.arange(d_half, dtype=np.float32) - low) / (high - low), 0.0, 1.0)
            mask = 1.0 - ramp
            inv_freq = interpolation * (1.0 - mask) + extrapolation * mask
            freqs = np.outer(np.arange(t_len, dtype=np.float32), inv_freq)
            return (jnp.asarray(np.cos(freqs) * concentration, jnp.float32), jnp.asarray(np.sin(freqs) * concentration, jnp.float32))

        def _apply_rope(x, cos, sin):
            x1, x2 = jnp.split(x, 2, axis=-1)
            return jnp.concatenate([x1 * cos - x2 * sin, x2 * cos + x1 * sin], axis=-1)
        key = jax.random.key(seed)
        ks = jax.random.split(key, 6)
        qkv_dim = HEAD_DIM * (N_HEADS + 2 * N_KV)
        return {'x': jax.random.normal(ks[0], (B, T, D_MODEL), jnp.float32), 'qkv_w': jax.random.normal(ks[1], (qkv_dim, D_MODEL), jnp.float32) * 0.02, 'qkv_b': jax.random.normal(ks[2], (qkv_dim,), jnp.float32) * 0.02, 'out_w': jax.random.normal(ks[3], (D_MODEL, N_HEADS * HEAD_DIM), jnp.float32) * 0.02, 'out_b': jax.random.normal(ks[4], (D_MODEL,), jnp.float32) * 0.02, 'sinks': jax.random.normal(ks[5], (N_HEADS,), jnp.float32) * (1.0 / math.sqrt(HEAD_DIM))}
    _L0_attn_in = _L0_attn_setup()

    def _L0_ffn_setup():
        import jax, jax.numpy as jnp
        import numpy as np
        B, S, H = (1, 128, 256)
        NH, NKV, D = (32, 8, 64)
        GROUPS = NH // NKV
        E, F, TOPK = (8, 1024, 2)
        EPS = 1e-05

        def rmsnorm(x, w):
            return x * jax.lax.rsqrt(jnp.mean(x * x, axis=-1, keepdims=True) + EPS) * w

        def attention(h, wq, wk, wv, wo):
            b, s, _ = h.shape
            q = (h @ wq).reshape(b, s, NH, D).transpose(0, 2, 1, 3)
            k = (h @ wk).reshape(b, s, NKV, D).transpose(0, 2, 1, 3)
            v = (h @ wv).reshape(b, s, NKV, D).transpose(0, 2, 1, 3)
            k = jnp.repeat(k, GROUPS, axis=1)
            v = jnp.repeat(v, GROUPS, axis=1)
            scores = jnp.einsum('bhqd,bhkd->bhqk', q, k) / jnp.sqrt(jnp.float32(D))
            causal = jnp.tril(jnp.ones((s, s), bool))
            scores = jnp.where(causal, scores, jnp.finfo(scores.dtype).min)
            attn = jax.nn.softmax(scores, axis=-1)
            out = jnp.einsum('bhqk,bhkd->bhqd', attn, v)
            out = out.transpose(0, 2, 1, 3).reshape(b, s, NH * D)
            return out @ wo

        def moe(h, gate_w, w1, w2, w3):
            b, s, hd = h.shape
            t = h.reshape(-1, hd)
            T = t.shape[0]
            probs = jax.nn.softmax(t @ gate_w, axis=-1)
            topw, topi = jax.lax.top_k(probs, TOPK)
            topw = topw / jnp.sum(topw, axis=-1, keepdims=True)
            combine = jnp.zeros((T, E), t.dtype).at[jnp.arange(T)[:, None], topi].add(topw)
            up = jnp.einsum('th,ehf->etf', t, w1)
            gated = jax.nn.relu(up) * jnp.einsum('th,ehf->etf', t, w3)
            down = jnp.einsum('etf,efh->eth', gated, w2)
            out = jnp.einsum('eth,te->th', down, combine)
            return out.reshape(b, s, hd)
        key = jax.random.key(seed)
        ks = jax.random.split(key, 12)
        sc = 0.02
        return {'x': jax.random.normal(ks[0], (B, S, H), dtype=jnp.float32), 'ln1_w': jnp.ones((H,), jnp.float32), 'wq': jax.random.normal(ks[1], (H, NH * D), jnp.float32) * sc, 'wk': jax.random.normal(ks[2], (H, NKV * D), jnp.float32) * sc, 'wv': jax.random.normal(ks[3], (H, NKV * D), jnp.float32) * sc, 'wo': jax.random.normal(ks[4], (NH * D, H), jnp.float32) * sc, 'ln2_w': jnp.ones((H,), jnp.float32), 'gate_w': jax.random.normal(ks[5], (H, E), jnp.float32) * sc, 'w1': jax.random.normal(ks[6], (E, H, F), jnp.float32) * sc, 'w2': jax.random.normal(ks[7], (E, F, H), jnp.float32) * sc, 'w3': jax.random.normal(ks[8], (E, H, F), jnp.float32) * sc}
    _L0_ffn_in = _L0_ffn_setup()
    _L0_c = _w((lambda *s: np.random.randn(*s).astype(np.float32) * 0.05)(2, 256))
    _L0_wmod = _w((lambda *s: np.random.randn(*s).astype(np.float32) * 0.05)(256, 6 * 256) * 256 ** (-0.5))
    _d = {'L0_attn_x': _L0_attn_in['x'], 'L0_attn_qkv_w': _L0_attn_in['qkv_w'], 'L0_attn_qkv_b': _L0_attn_in['qkv_b'], 'L0_attn_out_w': _L0_attn_in['out_w'], 'L0_attn_out_b': _L0_attn_in['out_b'], 'L0_attn_sinks': _L0_attn_in['sinks'], 'L0_ffn_ln1_w': _L0_ffn_in['ln1_w'], 'L0_ffn_wq': _L0_ffn_in['wq'], 'L0_ffn_wk': _L0_ffn_in['wk'], 'L0_ffn_wv': _L0_ffn_in['wv'], 'L0_ffn_wo': _L0_ffn_in['wo'], 'L0_ffn_ln2_w': _L0_ffn_in['ln2_w'], 'L0_ffn_gate_w': _L0_ffn_in['gate_w'], 'L0_ffn_w1': _L0_ffn_in['w1'], 'L0_ffn_w2': _L0_ffn_in['w2'], 'L0_ffn_w3': _L0_ffn_in['w3'], 'L0_c': _L0_c, 'L0_wmod': _L0_wmod}
    _x0 = _d['L0_attn_x']
    _d['L0_attn_x'] = jax.random.normal(jax.random.fold_in(jax.random.key(seed), 1), (2, 512, 256), dtype=_x0.dtype)
    del _x0
    return _d

def reference(L0_attn_x, L0_attn_qkv_w, L0_attn_qkv_b, L0_attn_out_w, L0_attn_out_b, L0_attn_sinks, L0_ffn_ln1_w, L0_ffn_wq, L0_ffn_wk, L0_ffn_wv, L0_ffn_wo, L0_ffn_ln2_w, L0_ffn_gate_w, L0_ffn_w1, L0_ffn_w2, L0_ffn_w3, L0_c, L0_wmod):

    def _L0_attn_ref(x, qkv_w, qkv_b, out_w, out_b, sinks):
        import jax, jax.numpy as jnp
        import numpy as np
        import math
        B, T = (4, 128)
        D_MODEL = 256
        HEAD_DIM = 64
        N_HEADS = 32
        N_KV = 8
        Q_MULT = N_HEADS // N_KV
        SLIDING_WINDOW = 128
        CAUSAL = True
        SM_SCALE = 1.0 / math.sqrt(HEAD_DIM)
        ROPE_THETA = 150000.0
        SCALING = 32.0
        NTK_ALPHA = 1.0
        NTK_BETA = 32.0
        ICL = 128

        def _rope_cos_sin(t_len):
            d_half = HEAD_DIM // 2
            freq = ROPE_THETA ** (np.arange(0, HEAD_DIM, 2, dtype=np.float32) / HEAD_DIM)
            concentration = 0.1 * math.log(SCALING) + 1.0
            low = d_half * math.log(ICL / (NTK_BETA * 2 * math.pi)) / math.log(ROPE_THETA)
            high = d_half * math.log(ICL / (NTK_ALPHA * 2 * math.pi)) / math.log(ROPE_THETA)
            interpolation = 1.0 / (SCALING * freq)
            extrapolation = 1.0 / freq
            ramp = np.clip((np.arange(d_half, dtype=np.float32) - low) / (high - low), 0.0, 1.0)
            mask = 1.0 - ramp
            inv_freq = interpolation * (1.0 - mask) + extrapolation * mask
            freqs = np.outer(np.arange(t_len, dtype=np.float32), inv_freq)
            return (jnp.asarray(np.cos(freqs) * concentration, jnp.float32), jnp.asarray(np.sin(freqs) * concentration, jnp.float32))

        def _apply_rope(x, cos, sin):
            x1, x2 = jnp.split(x, 2, axis=-1)
            return jnp.concatenate([x1 * cos - x2 * sin, x2 * cos + x1 * sin], axis=-1)
        Bv, Tv, _ = x.shape
        qkv = x @ qkv_w.T + qkv_b
        q = qkv[..., :N_HEADS * HEAD_DIM].reshape(Bv, Tv, N_KV, Q_MULT, HEAD_DIM)
        k = qkv[..., N_HEADS * HEAD_DIM:(N_HEADS + N_KV) * HEAD_DIM].reshape(Bv, Tv, N_KV, HEAD_DIM)
        v = qkv[..., (N_HEADS + N_KV) * HEAD_DIM:].reshape(Bv, Tv, N_KV, HEAD_DIM)
        cos, sin = _rope_cos_sin(Tv)
        q = _apply_rope(q, cos[:, None, None, :], sin[:, None, None, :])
        k = _apply_rope(k, cos[:, None, :], sin[:, None, :])
        logits = jnp.einsum('bqhmd,bkhd->bhmqk', q, k) * SM_SCALE
        i = jnp.arange(Tv)[:, None]
        j = jnp.arange(Tv)[None, :]
        mask = jnp.zeros((Tv, Tv), dtype=bool)
        if CAUSAL:
            mask = mask | (j > i)
        if SLIDING_WINDOW > 0:
            mask = mask | (j <= i - SLIDING_WINDOW)
        logits = jnp.where(mask, -jnp.inf, logits)
        m = jnp.max(logits, axis=-1, keepdims=True)
        e = jnp.exp(logits - m)
        s = sinks.reshape(N_KV, Q_MULT)[None, :, :, None, None]
        exp_sink = jnp.exp(s - m)
        w = e / (jnp.sum(e, axis=-1, keepdims=True) + exp_sink)
        out = jnp.einsum('bhmqk,bkhd->bqhmd', w, v).reshape(Bv, Tv, N_HEADS * HEAD_DIM)
        return out @ out_w.T + out_b

    def _L0_ffn_ref(x, ln1_w, wq, wk, wv, wo, ln2_w, gate_w, w1, w2, w3):
        import jax, jax.numpy as jnp
        import numpy as np
        B, S, H = (1, 128, 256)
        NH, NKV, D = (32, 8, 64)
        GROUPS = NH // NKV
        E, F, TOPK = (8, 1024, 2)
        EPS = 1e-05

        def rmsnorm(x, w):
            return x * jax.lax.rsqrt(jnp.mean(x * x, axis=-1, keepdims=True) + EPS) * w

        def attention(h, wq, wk, wv, wo):
            b, s, _ = h.shape
            q = (h @ wq).reshape(b, s, NH, D).transpose(0, 2, 1, 3)
            k = (h @ wk).reshape(b, s, NKV, D).transpose(0, 2, 1, 3)
            v = (h @ wv).reshape(b, s, NKV, D).transpose(0, 2, 1, 3)
            k = jnp.repeat(k, GROUPS, axis=1)
            v = jnp.repeat(v, GROUPS, axis=1)
            scores = jnp.einsum('bhqd,bhkd->bhqk', q, k) / jnp.sqrt(jnp.float32(D))
            causal = jnp.tril(jnp.ones((s, s), bool))
            scores = jnp.where(causal, scores, jnp.finfo(scores.dtype).min)
            attn = jax.nn.softmax(scores, axis=-1)
            out = jnp.einsum('bhqk,bhkd->bhqd', attn, v)
            out = out.transpose(0, 2, 1, 3).reshape(b, s, NH * D)
            return out @ wo

        def moe(h, gate_w, w1, w2, w3):
            b, s, hd = h.shape
            t = h.reshape(-1, hd)
            T = t.shape[0]
            probs = jax.nn.softmax(t @ gate_w, axis=-1)
            topw, topi = jax.lax.top_k(probs, TOPK)
            topw = topw / jnp.sum(topw, axis=-1, keepdims=True)
            combine = jnp.zeros((T, E), t.dtype).at[jnp.arange(T)[:, None], topi].add(topw)
            up = jnp.einsum('th,ehf->etf', t, w1)
            gated = jax.nn.relu(up) * jnp.einsum('th,ehf->etf', t, w3)
            down = jnp.einsum('etf,efh->eth', gated, w2)
            out = jnp.einsum('eth,te->th', down, combine)
            return out.reshape(b, s, hd)
        h = x + attention(rmsnorm(x, ln1_w), wq, wk, wv, wo)
        return h + moe(rmsnorm(h, ln2_w), gate_w, w1, w2, w3)
    x = L0_attn_x
    mod = (_silu(L0_c) @ L0_wmod).reshape(L0_c.shape[0], 6, 1, -1)
    sa, ca, ga, sb, cb, gb = (mod[:, 0], mod[:, 1], mod[:, 2], mod[:, 3], mod[:, 4], mod[:, 5])
    ga = (2 * (ga >= 0) - 1) * jnp.maximum(jnp.abs(ga), 0.25)
    gb = (2 * (gb >= 0) - 1) * jnp.maximum(jnp.abs(gb), 0.25)
    h = _layernorm(x, axis=-1) * (1 + ca) + sa
    x = x + ga * _L0_attn_ref(h, L0_attn_qkv_w, L0_attn_qkv_b, L0_attn_out_w, L0_attn_out_b, L0_attn_sinks)
    h = _layernorm(x, axis=-1) * (1 + cb) + sb
    x = x + gb * _L0_ffn_ref(h, L0_ffn_ln1_w, L0_ffn_wq, L0_ffn_wk, L0_ffn_wv, L0_ffn_wo, L0_ffn_ln2_w, L0_ffn_gate_w, L0_ffn_w1, L0_ffn_w2, L0_ffn_w3)
    return x

_drawn_inputs = setup_inputs


def setup_inputs(seed=0):
    import zlib

    import numpy as np

    out = dict(_drawn_inputs(seed))
    spreads = {'L0_ffn_ln1_w': (1.0, 0.6), 'L0_ffn_ln2_w': (1.0, 0.6)}
    factors = {'L0_attn_qkv_w': 6.659,
     'L0_attn_qkv_b': 8.0,
     'L0_attn_out_w': 6.054,
     'L0_attn_out_b': 8.0,
     'L0_attn_sinks': 8.0,
     'L0_ffn_wq': 8.0,
     'L0_ffn_wk': 8.0,
     'L0_ffn_wv': 6.47,
     'L0_ffn_wo': 6.574,
     'L0_ffn_gate_w': 7.24,
     'L0_ffn_w1': 7.712,
     'L0_ffn_w2': 6.383,
     'L0_ffn_w3': 6.381}
    for name, (base, spread) in spreads.items():
        noise = np.random.default_rng([zlib.crc32(name.encode()), seed]).standard_normal(out[name].shape)
        drawn = base * np.exp(spread * noise) if base else spread * noise
        out[name] = jnp.asarray(drawn.astype(out[name].dtype))
    for name, factor in factors.items():
        out[name] = (out[name] * factor).astype(out[name].dtype)
    return out
```

```python
from contextlib import ExitStack

import concourse.bass as bass
from concourse import mybir

F32 = mybir.dt.float32
F32R = mybir.dt.float32r
U32 = mybir.dt.uint32
ALU = mybir.AluOpType
ACT = mybir.ActivationFunctionType

P = 128
BATCH, SEQ, D = 2, 512, 256
NT = BATCH * SEQ // P
TB = SEQ // P
KC = D // P
HD = 64
NKV, QM = 8, 4
HQ = QM * HD
QKV = HQ + 2 * HD
NE, FF = 8, 1024
NF = FF // P
EW = 2 * KC * P + D
SCALE = HD ** -0.5
NEG = -1e30
EPS = 1e-5
NMOD = 6 * D


class Layer:

    def __init__(self, window, unit_base, kt_base):
        self.window = window
        self.unit_base, self.kt_base = unit_base, kt_base
        self.keys = [min(t + 1, 2) if window else t + 1 for t in range(TB)]
        self.kt_round = sum(self.keys) * BATCH

    def ntiles(self, s):
        return self.keys[s % TB]

    def first_tile(self, s):
        s %= NT
        return s - self.ntiles(s) + 1

    def unit(self, g, s):
        return self.unit_base + NT * g + s + 1

    def head(self, g, s, j):
        return QM * (self.unit(g, s) - 1) + j + 1

    def kt(self, g, s, k):
        before = sum(self.keys[i % TB] for i in range(s % NT)) + s // NT * self.kt_round
        return self.kt_base + self.kt_round * g + before + k + 1

    def kt_all(self, g, s):
        return self.kt(g, s + 1, -1)

    def kt_slot(self, s, k):
        return (sum(self.keys[i % TB] for i in range(s % NT)) + k) % 2


def exists(g, s):
    return not isinstance(g, int) or 0 <= NT * g + s < NT * NKV


def wait(eng, sem, value):
    if not isinstance(value, int) or value > 0:
        eng.wait_ge(sem, value)


def rounds(eng, step):
    for s in range(-4, NT):
        step(0, s)
    with eng.Fori(1, NKV - 1) as g:
        for s in range(NT):
            step(g, s)
    for s in range(NT + 3):
        step(NKV - 1, s)


def build(nc, x, w_attn, wo_attn, b_attn, outb, sinks, w_ffn, wo_ffn, ln1, ln2, gate, w_moe,
          cT, wmod, rope_cos, rope_sin, mask_win, mask_causal, ident, expert_ids, out):
    LA, LB = Layer(True, 0, 0), Layer(False, NT * NKV, 0)
    LB.kt_base = LA.kt_round * NKV
    ctx = ExitStack()
    with ctx:
        def sb(name, shape, dt=F32):
            return ctx.enter_context(nc.sbuf_tensor(name, shape, dt))

        def sem(name):
            return ctx.enter_context(nc.semaphore(name))

        N_CONST = 13
        idn = sb("idn", [P, P])
        mwin = sb("mwin", [P, 2 * P])
        mcau = sb("mcau", [P, SEQ])
        cosw = sb("cosw", [P, TB, HD])
        sinw = sb("sinw", [P, TB, HD])
        sink_b = sb("sink_b", [P, NKV * QM])
        outb_b = sb("outb_b", [P, D])
        ln1_b = sb("ln1_b", [P, D])
        ln2_b = sb("ln2_b", [P, D])
        ids = sb("ids", [P, NE])
        modb = sb("modb", [P, BATCH, NMOD])
        xN = sb("xN", [P, NT, D])
        uN = sb("uN", [P, NT, D])
        yN = sb("yN", [P, NT, D])
        hb = sb("hb", [P, 2, D])
        hTh = sb("hTh", [P, KC, NT * P], F32R)
        hTl = sb("hTl", [P, KC, NT * P], F32R)
        wraw = sb("wraw", [P, KC * QKV])
        woraw = sb("woraw", [P, 2 * D])
        biasraw = sb("biasraw", [33, NKV * QKV])
        bias = sb("bias", [P, NKV * QKV], F32R)
        pick = sb("pick", [P, P], F32R)
        t1 = sb("t1", [P, QM + 1, HD])
        t2 = sb("t2", [P, QM + 1, HD])
        qk = sb("qk", [P, QM + 1, HD])
        qn = sb("qn", [P, 2, QM, 2, HD], F32R)
        kn = sb("kn", [P, 2, 2, 2, HD], F32R)
        wbufs = sb("wbufs", [P, 4 * KC * QKV], F32R)
        wh = wbufs[:, 0:2 * KC * QKV]
        wl = wbufs[:, 2 * KC * QKV:]
        woh = sb("woh", [P, 2 * 2 * D], F32R)
        wol = sb("wol", [P, 2 * 2 * D], F32R)
        bufA = sb("bufA", [P, NF * EW], F32R)
        bufB = sb("bufB", [P, NF * EW], F32R)
        qT = bufA[:, 0:NT * QM * P].rearrange("p (t n) -> p t n", t=NT)
        kT = bufA[:, NT * QM * P:].rearrange("p (c n) -> p c n", c=2)
        o = 0
        vpad = bufB[:, 0:2 * NT * 3 * HD].rearrange("p (c t n) -> p c t n", c=2, t=NT)
        o = 2 * NT * 3 * HD
        pTh = bufB[:, o:o + 2 * QM * P].rearrange("p (c n) -> p c n", c=2)
        o += 2 * QM * P
        pTl = bufB[:, o:o + 2 * QM * P].rearrange("p (c n) -> p c n", c=2)
        o += 2 * QM * P
        oh = bufB[:, o:o + 2 * 2 * P].rearrange("p (c n) -> p c n", c=2)
        o += 2 * 2 * P
        ol = bufB[:, o:o + 2 * 2 * P].rearrange("p (c n) -> p c n", c=2)
        pbuf = sb("pbuf", [P, 2 * QM * SEQ])
        probs = pbuf[:, :].rearrange("p (c h n) -> p c h n", c=2, h=QM)
        wmod_s = pbuf[:, 0:KC * NMOD].rearrange("p (k n) -> p k n", k=KC)
        relu_s = pbuf[:, 0:2 * SEQ].rearrange("p (c n) -> p c n", c=2)
        gated = pbuf[:, 2 * SEQ:4 * SEQ].rearrange("p (c n) -> p c n", c=2)
        gTh = wbufs[:, 0:2 * SEQ].rearrange("p (c n) -> p c n", c=2)
        gTl = wbufs[:, 2 * SEQ:4 * SEQ].rearrange("p (c n) -> p c n", c=2)
        mraw = sb("mraw", [P, 4, EW])
        nmax = sb("nmax", [P, 2, QM])
        sums = sb("sums", [P, 2, QM])
        esin = sb("esin", [P, 2, QM])
        esink = sb("esink", [P, 2, QM])
        den = sb("den", [P, 2, QM])
        rden = sb("rden", [P, 2, QM])
        cS = sb("cS", [P, KC * BATCH])
        cE = sb("cE", [P, KC * BATCH])
        cD = sb("cD", [P, KC * BATCH])
        cR = sb("cR", [P, KC * BATCH])
        ones = sb("ones", [P, P])
        cB = sb("cB", [P, KC * BATCH, P])
        gsign = sb("gsign", [P, BATCH, D])
        stats = sb("stats", [P, NT, 6])
        mv = sb("mv", [P, NT, 2])
        vare = sb("vare", [P, NT])
        sd = sb("sd", [P, NT])
        rs = sb("rs", [P, NT])
        sq = sb("sq", [P, D])
        graw = sb("graw", [P, KC, NE])
        gwh = sb("gwh", [P, KC, NE], F32R)
        gwl = sb("gwl", [P, KC, NE], F32R)
        lmax = sb("lmax", [P, NT])
        pr = sb("pr", [P, NT, NE])
        prs = sb("prs", [P, NT])
        prr = sb("prr", [P, NT])
        top = sb("top", [P, NT, 8])
        topi = sb("topi", [P, NT, 8], U32)
        topf = sb("topf", [P, NT, 8])
        tops = sb("tops", [P, NT])
        topr = sb("topr", [P, NT])
        topw = sb("topw", [P, NT, 2])
        c0 = sb("c0", [P, NT, NE])
        c1 = sb("c1", [P, NT, NE])
        comb = sb("comb", [P, NT, NE])

        def bank(name):
            return ctx.enter_context(nc.psum_tensor(name, [P, 512], F32))

        psS = [bank("psS0"), bank("psS1")]
        psX = [bank("psX0"), bank("psX1")]
        psO = bank("psO")
        psP = bank("psP")
        psT = bank("psT")
        psY = bank("psY")
        psD = [psO, psP, psT, psY]

        ld_c = sem("ld_c")
        ld_x = sem("ld_x")
        ld_k = sem("ld_k")
        ld_w = sem("ld_w")
        ld_wo = sem("ld_wo")
        ld_m = [sem(f"ld_m{i}") for i in range(4)]
        st_out = sem("st_out")
        v_seq = sem("v_seq")
        v_zero = sem("v_zero")
        v_cb = sem("v_cb")
        v_mod = sem("v_mod")
        v_gate = sem("v_gate")
        v_stat = sem("v_stat")
        v_aggr = sem("v_aggr")
        v_var = sem("v_var")
        v_lmax = sem("v_lmax")
        v_out = sem("v_out")
        a_ec = sem("a_ec")
        a_root = sem("a_root")
        a_rt = sem("a_rt")
        p_init = sem("p_init")
        s_mod = sem("s_mod")
        s_ht = sem("s_ht")
        v_h = sem("v_h")
        a_hth = sem("a_hth")
        v_htl = sem("v_htl")
        g_hi = sem("g_hi")
        g_w = sem("g_w")
        s_proj = sem("s_proj")
        v_rope = sem("v_rope")
        g_add = sem("g_add")
        g_qh = sem("g_qh")
        qk_lo = sem("qk_lo")
        a_qh = sem("a_qh")
        a_vh = sem("a_vh")
        v_vl = sem("v_vl")
        s_tq = sem("s_tq")
        s_tk = sem("s_tk")
        a_tq = sem("a_tq")
        v_tk = sem("v_tk")
        s_S = sem("s_S")
        v_max = sem("v_max")
        a_exp = sem("a_exp")
        g_es = sem("g_es")
        a_es = sem("a_es")
        v_den = sem("v_den")
        v_rden = sem("v_rden")
        v_norm = sem("v_norm")
        s_X = sem("s_X")
        a_ph = sem("a_ph")
        v_pl = sem("v_pl")
        s_PV = sem("s_PV")
        a_oh = sem("a_oh")
        v_ol = sem("v_ol")
        s_Y = sem("s_Y")
        v_y = sem("v_y")
        s_rt = sem("s_rt")
        m_wh = sem("m_wh")
        m_w = sem("m_w")
        m_up = sem("m_up")
        m_relu = sem("m_relu")
        m_g = sem("m_g")
        m_gh = sem("m_gh")
        m_gl = sem("m_gl")
        m_dn = sem("m_dn")
        m_acc = sem("m_acc")

        block = ctx.enter_context(nc.Block())

        def apart(eng):
            eng.nop(nofuse=True)

        M_STEPS = 2 * NF

        def moe_rounds(eng, step, tail):
            for r in range(M_STEPS):
                step(0, r)
            with eng.Fori(1, NE) as e:
                for r in range(M_STEPS):
                    step(e, r)
            for r in range(tail):
                step(NE, r)

        def parity(g):
            return g % 2

        @block.sync
        def _(sp):
            sp.dma_start(cS[:, :], cT).then_inc(ld_c, 16)
            sp.dma_start(wmod_s, wmod).then_inc(ld_c, 16)
            sp.dma_start(xN[:, :, :], x.rearrange("b (t p) d -> p (b t) d", p=P)).then_inc(ld_x, 16)
            for dst, src in ((idn, ident), (mwin, mask_win), (mcau, mask_causal)):
                sp.dma_start(dst[:, :], src).then_inc(ld_k, 16)
            for dst, src in ((cosw, rope_cos), (sinw, rope_sin), (graw, gate)):
                sp.dma_start(dst[:, :, :], src).then_inc(ld_k, 16)
            for dst, src in ((sink_b, sinks), (outb_b, outb), (ln1_b, ln1), (ln2_b, ln2), (ids, expert_ids)):
                sp.dma_start(dst[:, :], src.partition_broadcast(P)).then_inc(ld_k, 16)
            sp.wait_ge(v_zero, 1)
            for row in (0, 32):
                sp.dma_start(biasraw[row:row + 1, :], b_attn.rearrange("(a n) -> a n", a=1)).then_inc(ld_k, 16)

            for n, (w_d, wo_d) in enumerate(((w_attn, wo_attn), (w_ffn, wo_ffn))):
                def load_round(g):
                    done = 3 * (NKV * n + g)
                    wait(sp, g_w, done)
                    sp.dma_start(wraw[:, :], w_d[bass.ds(g, 1)].rearrange("o p n -> (o p) n")).then_inc(ld_w, 16)
                    sp.dma_start(woraw[:, :], wo_d[bass.ds(g, 1)].rearrange("o p n -> (o p) n")).then_inc(ld_wo, 16)

                load_round(0)
                with sp.Fori(1, NKV) as g:
                    load_round(g)

            def load_chunk(e, f):
                wait(sp, m_w, NF * e + f + 1 - 4)
                sp.dma_start(mraw[:, f % 4, :], w_moe[bass.ds(e * NF + f, 1)].rearrange("o p n -> (o p) n"))\
                  .then_inc(ld_m[f % 4], 16)

            for f in range(NF):
                load_chunk(0, f)
            with sp.Fori(1, NE) as e:
                for f in range(NF):
                    load_chunk(e, f)
            sp.wait_ge(v_out, 1)
            sp.dma_start(out.rearrange("b (t p) d -> p (b t) d", p=P), xN[:, :, :]).then_inc(st_out, 16)
            sp.wait_ge(st_out, 16)

        @block.gpsimd
        def _(pool):
            nc.gpsimd.memset(bufB[:, 0:2 * NT * 3 * HD].bitcast(F32), 0.0).then_inc(p_init, 1)

            for L in (LA, LB):
                n = 0 if L is LA else 1

                def split_piece(g, piece, L=L, n=n):
                    r = NKV * n + g
                    if piece < 2:
                        wait(pool, ld_w, 16 * (r + 1))
                        wait(pool, s_proj, L.unit(g - 2, NT - 1))
                        at = parity(g) * (KC * QKV) + piece * QKV
                        hi, lo, raw = wh[:, bass.ds(at, QKV)], wl[:, bass.ds(at, QKV)], wraw[:, piece * QKV:(piece + 1) * QKV]
                    else:
                        wait(pool, ld_wo, 16 * (r + 1))
                        wait(pool, s_Y, L.unit(g - 2, NT - 1))
                        at = parity(g) * 2 * D
                        hi, lo, raw = woh[:, bass.ds(at, 2 * D)], wol[:, bass.ds(at, 2 * D)], woraw[:, :]
                    apart(pool)
                    nc.gpsimd.tensor_copy(hi, raw).then_inc(g_hi, 1)
                    wait(pool, g_hi, 3 * r + piece + 1)
                    apart(pool)
                    nc.gpsimd.tensor_tensor(lo, raw, hi, ALU.subtract).then_inc(g_w, 1)

                def step(g, s, L=L):
                    if L is LA and exists(g, s):
                        wait(pool, v_max, L.head(g, s, QM - 1))
                        wait(pool, a_es, L.unit(g, s - 2))
                        apart(pool)
                        nc.gpsimd.tensor_tensor(esin[:, s % 2, :], sink_b[:, bass.ds(g * QM, QM)],
                                                nmax[:, s % 2, :], ALU.add).then_inc(g_es, 1)
                    if L is LA and exists(g, s + 4):
                        wait(pool, v_rope, L.unit(g, s + 4))
                        wait(pool, qk_lo, L.unit(g, s + 3))
                        nc.gpsimd.tensor_tensor(qk[:, :, :], t1[:, :, :], t2[:, :, :], ALU.add).then_inc(g_add, 1)
                        wait(pool, g_add, L.unit(g, s + 4))
                        wait(pool, s_tk, L.unit(g, s + 2))
                        k2 = qk[:, QM, :].unsqueeze(1).broadcast_to([P, 2, HD])
                        apart(pool)
                        nc.gpsimd.tensor_copy(qn[:, s % 2, :, 0, :], qk[:, 0:QM, :])
                        nc.gpsimd.tensor_copy(kn[:, s % 2, 0, :, :], k2).then_inc(g_qh, 1)
                        wait(pool, g_qh, L.unit(g, s + 4))
                        nc.gpsimd.tensor_tensor(qn[:, s % 2, :, 1, :], qk[:, 0:QM, :], qn[:, s % 2, :, 0, :],
                                                ALU.subtract)
                        nc.gpsimd.tensor_tensor(kn[:, s % 2, 1, :, :], k2, kn[:, s % 2, 0, :, :],
                                                ALU.subtract).then_inc(qk_lo, 1)
                    if s in (0, 1, 2) and exists(g, NT):
                        split_piece(g + 1, s)

                for piece in range(3):
                    split_piece(0, piece)
                rounds(pool, step)

            def split_chunk(e, f):
                wait(pool, ld_m[f % 4], 16 * (2 * e + f // 4 + 1))
                wait(pool, m_dn, M_STEPS * (e - 1) + NF + f + 1)
                if isinstance(e, int) and f == 0:
                    pool.wait_ge(s_rt, NT)
                at = slice(f * EW, (f + 1) * EW)
                apart(pool)
                nc.gpsimd.tensor_copy(bufA[:, at], mraw[:, f % 4, :]).then_inc(m_wh, 1)
                wait(pool, m_wh, NF * e + f + 1)
                nc.gpsimd.tensor_tensor(bufB[:, at], mraw[:, f % 4, :], bufA[:, at], ALU.subtract).then_inc(m_w, 1)

            for f in range(NF):
                split_chunk(0, f)
            with pool.Fori(1, NE) as e:
                for f in range(NF):
                    split_chunk(e, f)

        @block.tensor
        def _(pe):
            mm = nc.tensor.matmul

            pe.wait_ge(v_cb, KC * BATCH)
            pe.wait_ge(ld_c, 32)
            for n in range(BATCH * 3):
                b, c = n // 3, n % 3
                wait(pe, v_mod, n - 1)
                for k in range(KC):
                    last = mm(psS[n % 2][:, :], cB[:, k * BATCH + b, :], wmod_s[:, k, c * 512:(c + 1) * 512],
                              start=(k == 0), stop=(k == KC - 1))
                last.then_inc(s_mod, 1)

            def to_features(phase):
                for t in range(NT):
                    n = NT * phase + t
                    pe.wait_ge(v_h, n + 1)
                    if phase == 0 and t == 0:
                        pe.wait_ge(ld_k, 16 * N_CONST)
                    wait(pe, v_htl, n + 1 - 2)
                    for k in range(KC):
                        last = nc.tensor.transpose(psX[t % 2][:, k * P:(k + 1) * P], hb[:, t % 2, k * P:(k + 1) * P],
                                                   idn[:, :])
                    last.then_inc(s_ht, 1)

            def attention(L, phase):
                def scores(g, s, j):
                    wait(pe, v_max, L.head(g, s, j) - 2)
                    if j == 0:
                        wait(pe, a_tq, L.unit(g, s))
                        wait(pe, v_tk, L.unit(g, s))
                    n = L.ntiles(s) * P
                    k0 = L.first_tile(s) * P
                    for c in range(2):
                        last = mm(psS[j % 2][:, 0:n], qT[:, s % NT, j * P:(j + 1) * P], kT[:, c, k0:k0 + n],
                                  start=(c == 0), stop=(c == 1))
                    last.then_inc(s_S, 1)

                def turn_probs(g, s, k):
                    if k == 0:
                        wait(pe, v_norm, L.head(g, s, QM - 1))
                    slot = L.kt_slot(s, k)
                    wait(pe, v_pl, L.kt(g, s, k) - 2)
                    for j in range(QM):
                        last = nc.tensor.transpose(psX[slot][:, j * P:(j + 1) * P],
                                                   probs[:, s % 2, j, k * P:(k + 1) * P], idn[:, :])
                    last.then_inc(s_X, 1)

                def values(g, s, k):
                    slot = L.kt_slot(s, k)
                    if k == 0:
                        wait(pe, v_ol, L.unit(g, s - 1))
                        wait(pe, v_vl, L.unit(g, s))
                    wait(pe, v_pl, L.kt(g, s, k))
                    kv = L.first_tile(s) + k
                    pairs = lambda p: p[:, slot, :].rearrange("p (i r q) -> p r i q", r=2, q=P)
                    n = 0
                    for v, pT in ((0, pTh), (1, pTh), (0, pTl)):
                        for r in range(2):
                            lhsT = vpad[:, v, kv, HD:3 * HD] if r == 0 else vpad[:, v, kv, 0:2 * HD]
                            last = mm(psO[:, 0:2 * P], lhsT, pairs(pT)[:, r],
                                      start=(k == 0 and n == 0), stop=(k == L.ntiles(s) - 1 and n == 5))
                            n += 1
                    last.then_inc(s_PV, 1)

                def project(g, s):
                    r = 0 if L is LA else NKV
                    wait(pe, v_vl, L.unit(g, s - 1))
                    if s % NT == 0:
                        g2 = g + s // NT
                        wait(pe, g_w, 3 * (r + g2) + 2)
                    if isinstance(g, int) and g == 0 and 0 <= s < NT:
                        pe.wait_ge(v_htl, NT * phase + s + 1)
                    at = parity(g + s // NT) * (KC * QKV)
                    t = s % NT
                    n = 0
                    for k in range(KC):
                        for a, w in ((hTh, wh), (hTl, wh), (hTh, wl)):
                            n += 1
                            last = mm(psP[:, 0:QKV], a[:, k, t * P:(t + 1) * P], w[:, bass.ds(at + k * QKV, QKV)],
                                      start=(n == 1), stop=(n == 3 * KC and L is LB))
                    if L is LA:
                        last = mm(psP[:, 0:QKV], pick[:, :], bias[:, bass.ds((g + s // NT) * QKV, QKV)],
                                  start=False, stop=True)
                    last.then_inc(s_proj, 1)

                def turn_q(g, s):
                    wait(pe, qk_lo, L.unit(g, s))
                    wait(pe, v_tk, L.unit(g, s - 1))
                    for j in range(QM):
                        last = nc.tensor.transpose(psT[:, j * P:(j + 1) * P],
                                                   qn[:, s % 2, j, :, :].rearrange("p c d -> p (c d)").bitcast(F32),
                                                   idn[:, :])
                    last.then_inc(s_tq, 1)

                def turn_k(g, s):
                    wait(pe, a_tq, L.unit(g, s))
                    for c in range(2):
                        kk = kn[:, s % 2, c, :, :].rearrange("p r d -> p (r d)").bitcast(F32)
                        last = nc.tensor.transpose(psT[:, c * P:(c + 1) * P], kk, idn[:, :])
                    last.then_inc(s_tk, 1)

                def out_project(g, s):
                    r = 0 if L is LA else NKV
                    wait(pe, v_ol, L.unit(g, s))
                    wait(pe, v_y, L.unit(g, s - 1))
                    g2 = g + s // NT
                    if s % NT == 0:
                        wait(pe, g_w, 3 * (r + g2) + 3)
                    at = parity(g2) * 2 * D
                    n = 0
                    for i in range(2):
                        for a, w in ((oh, woh), (ol, woh), (oh, wol)):
                            n += 1
                            last = mm(psY[:, 0:D], a[:, s % 2, i * P:(i + 1) * P], w[:, bass.ds(at + i * D, D)],
                                      start=(n == 1), stop=(n == 6))
                    last.then_inc(s_Y, 1)

                def step(g, s):
                    now, back, ahead = exists(g, s), exists(g, s - 1), exists(g, s + 4)
                    nk = L.ntiles(s - 1) if back else 0
                    if now:
                        scores(g, s, 0)
                        scores(g, s, 1)
                    if exists(g, s - 2):
                        out_project(g, s - 2)
                    if ahead:
                        project(g, s + 4)
                    if nk > 0:
                        turn_probs(g, s - 1, 0)
                    if now:
                        scores(g, s, 2)
                    if nk > 1:
                        turn_probs(g, s - 1, 1)
                    if nk > 0:
                        values(g, s - 1, 0)
                    if exists(g, s + 3):
                        turn_q(g, s + 3)
                    if now:
                        scores(g, s, 3)
                    if nk > 2:
                        turn_probs(g, s - 1, 2)
                    if nk > 1:
                        values(g, s - 1, 1)
                    if nk > 3:
                        turn_probs(g, s - 1, 3)
                    if nk > 2:
                        values(g, s - 1, 2)
                    if nk > 3:
                        values(g, s - 1, 3)
                    if exists(g, s + 3):
                        turn_k(g, s + 3)

                rounds(pe, step)

            to_features(0)
            attention(LA, 0)
            to_features(1)
            attention(LB, 1)
            to_features(2)

            for t in range(NT):
                pe.wait_ge(v_htl, 2 * NT + t + 1)
                if t == 0:
                    pe.wait_ge(v_gate, 1)
                n = 0
                for k in range(KC):
                    for a, w in ((hTh, gwh), (hTl, gwh), (hTh, gwl), (hTl, gwl)):
                        n += 1
                        last = mm(psY[:, t * NE:(t + 1) * NE], a[:, k, t * P:(t + 1) * P], w[:, k, :],
                                  start=(t == 0 and n == 1), stop=(n == 4 * KC), skip_group_check=True)
                last.then_inc(s_rt, 1)

            def up_gate(e, r):
                c, f = r // NF, r % NF
                q = M_STEPS * e + r
                if c == 0:
                    wait(pe, m_w, NF * e + f + 1)
                wait(pe, m_g, q - 1)
                for off, ps in ((0, psS[r % 2]), (KC * P, psX[r % 2])):
                    n = 0
                    for k in range(KC):
                        at = f * EW + off + k * P
                        for w, a in ((bufA, hTh), (bufA, hTl), (bufB, hTh)):
                            n += 1
                            last = mm(ps[:, :], w[:, at:at + P], a[:, k, c * SEQ:(c + 1) * SEQ],
                                      start=(n == 1), stop=(n == 3 * KC))
                last.then_inc(m_up, 1)

            def down(e, r):
                q = M_STEPS * e + r
                c, f = r % M_STEPS // NF, r % NF
                wait(pe, m_gl, q + 1)
                if f == 0:
                    wait(pe, m_acc, NT * (e - 1) + (c + 1) * TB)
                if isinstance(e, int) and e == 0 and r == NF:
                    pe.wait_ge(a_rt, NT)
                w2 = slice(f * EW + 2 * KC * P, (f + 1) * EW)
                for t in range(TB):
                    ps = psD[2 * c + t // 2][:, t % 2 * D:(t % 2 + 1) * D]
                    n = 0
                    for a, w in ((gTh, bufA), (gTl, bufA), (gTh, bufB)):
                        n += 1
                        last = mm(ps, a[:, r % 2, t * P:(t + 1) * P], w[:, w2],
                                  start=(f == 0 and n == 1 and t % 2 == 0), stop=(f == NF - 1 and n == 3),
                                  skip_group_check=True)
                last.then_inc(m_dn, 1)

            def moe_step(e, r):
                if not isinstance(e, int) or e < NE:
                    up_gate(e, r)
                if not isinstance(e, int) or e > 0 or r > 0:
                    down(e, r - 1)

            moe_rounds(pe, moe_step, 1)

        @block.scalar
        def _(act):
            copy = lambda o, i: nc.scalar.activation(o, i, ACT.Copy)

            act.wait_ge(ld_c, 32)
            nc.scalar.activation(cE[:, :], cS[:, :], ACT.Exp, scale=-1.0).then_inc(a_ec, 1)

            def roots(n):
                act.wait_ge(v_var, n + 1)
                nc.scalar.activation(sd[:, :], vare[:, :], ACT.Sqrt).then_inc(a_root, 1)

            def features_hi(phase):
                for t in range(NT):
                    n = NT * phase + t
                    act.wait_ge(s_ht, n + 1)
                    copy(hTh[:, :, t * P:(t + 1) * P], psX[t % 2][:, 0:D].rearrange("p (k n) -> p k n", k=KC))\
                        .then_inc(a_hth, 1)

            def attention(L):
                def exp_head(g, s, j):
                    n = L.ntiles(s) * P
                    wait(act, v_max, L.head(g, s, j))
                    if j == 0 and L is LB:
                        wait(act, v_rden, L.unit(g, s - 2))
                    if j == 0 and L is LA:
                        wait(act, v_den, L.unit(g, s - 2))
                    pj = probs[:, s % 2, j, 0:n]
                    nc.scalar.activation(pj, pj, ACT.Exp, bias=nmax[:, s % 2, j:j + 1], scale=-1.0,
                                         accum_out=sums[:, s % 2, j:j + 1]).then_inc(a_exp, 1)

                def sink_exp(g, s):
                    wait(act, g_es, L.unit(g, s))
                    wait(act, v_den, L.unit(g, s - 2))
                    nc.scalar.activation(esink[:, s % 2, :], esin[:, s % 2, :], ACT.Exp).then_inc(a_es, 1)

                def probs_hi(g, s, k):
                    slot = L.kt_slot(s, k)
                    wait(act, s_X, L.kt(g, s, k))
                    wait(act, s_PV, L.kt(g, s, k) - 2)
                    copy(pTh[:, slot, :], psX[slot][:, :]).then_inc(a_ph, 1)

                def out_hi(g, s):
                    wait(act, s_PV, L.kt_all(g, s))
                    wait(act, s_Y, L.unit(g, s - 2))
                    copy(oh[:, s % 2, :], psO[:, 0:2 * P]).then_inc(a_oh, 1)

                def project_hi(g, s):
                    wait(act, s_proj, L.unit(g, s))
                    if L is LB:
                        wait(act, s_tk, L.unit(g, s - 2))
                        copy(qn[:, s % 2, :, 0, :], psP[:, 0:HQ].rearrange("p (h d) -> p h d", d=HD))
                        copy(kn[:, s % 2, 0, :, :], psP[:, HQ:HQ + HD].unsqueeze(1).broadcast_to([P, 2, HD]))\
                            .then_inc(a_qh, 1)
                    else:
                        wait(act, v_rope, L.unit(g, s))
                    wait(act, s_PV, L.kt_all(g - 1, s % NT // TB * TB + TB - 1 + s // NT * NT))
                    copy(vpad[:, 0, s % NT, HD:2 * HD], psP[:, HQ + HD:QKV]).then_inc(a_vh, 1)

                def write_qT(g, s):
                    wait(act, s_tq, L.unit(g, s))
                    wait(act, s_S, L.head(g - 1, s, QM - 1))
                    copy(qT[:, s % NT, :], psT[:, :]).then_inc(a_tq, 1)

                def step(g, s):
                    now, back, ahead = exists(g, s), exists(g, s - 1), exists(g, s + 4)
                    nk = L.ntiles(s - 1) if back else 0
                    if L is LA and back:
                        sink_exp(g, s - 1)
                    if now:
                        exp_head(g, s, 0)
                        exp_head(g, s, 1)
                    if nk > 0:
                        probs_hi(g, s - 1, 0)
                    if now:
                        exp_head(g, s, 2)
                    if nk > 1:
                        probs_hi(g, s - 1, 1)
                    if exists(g, s + 3):
                        write_qT(g, s + 3)
                    if now:
                        exp_head(g, s, 3)
                    if nk > 2:
                        probs_hi(g, s - 1, 2)
                    if nk > 3:
                        probs_hi(g, s - 1, 3)
                    if ahead:
                        project_hi(g, s + 4)
                    if back:
                        out_hi(g, s - 1)

                if L is LA:
                    act.wait_ge(p_init, 1)
                rounds(act, step)

            roots(0)
            features_hi(0)
            attention(LA)
            roots(1)
            roots(2)
            features_hi(1)
            attention(LB)
            roots(3)
            features_hi(2)

            act.wait_ge(v_lmax, 1)
            for t in range(NT):
                nc.scalar.activation(pr[:, t, :], psY[:, t * NE:(t + 1) * NE], ACT.Exp, bias=lmax[:, t:t + 1],
                                     accum_out=prs[:, t:t + 1]).then_inc(a_rt, 1)

            def moe_step(e, r):
                q = M_STEPS * e + r
                wait(act, m_up, q + 1)
                wait(act, m_g, q - 1)
                nc.scalar.activation(relu_s[:, r % 2, :], psS[r % 2][:, :], ACT.Relu).then_inc(m_relu, 1)
                wait(act, m_g, q + 1)
                wait(act, m_dn, q - 1)
                copy(gTh[:, r % 2, :], gated[:, r % 2, :]).then_inc(m_gh, 1)

            moe_rounds(act, moe_step, 0)

        @block.vector
        def _(dve):
            V = nc.vector
            reached = {}

            def link(ins, signal=v_seq):
                reached[signal.name] = reached.get(signal.name, 0) + 1
                ins.then_inc(signal, 1)
                dve.wait_ge(signal, reached[signal.name])

            link(V.memset(biasraw[:, :], 0.0), v_zero)
            link(V.memset(bias[:, :].bitcast(F32), 0.0))
            link(V.memset(pick[:, :].bitcast(F32), 0.0))
            link(V.memset(ones[:, :], 1.0))
            for row in (0, 32):
                link(V.tensor_copy(pick[row:row + 1, :], ones[row:row + 1, :]))
            dve.wait_ge(a_ec, 1)
            link(V.tensor_scalar(cD[:, :], cE[:, :], 1.0, None, ALU.add))
            link(V.reciprocal(cR[:, :], cD[:, :]))
            link(V.tensor_tensor(cD[:, :], cS[:, :], cR[:, :], ALU.mult))
            for n in range(KC * BATCH):
                link(V.tensor_scalar(cB[:, n, :], ones[:, :], cD[:, n:n + 1], None, ALU.mult), v_cb)
            dve.wait_ge(ld_k, 16 * N_CONST)
            link(V.tensor_copy(bias[0:33, :], biasraw[:, :]))
            link(V.tensor_tensor(bias[32:33, :], biasraw[32:33, :], bias[32:33, :], ALU.subtract))
            link(V.tensor_copy(gwh[:, :, :], graw[:, :, :]))
            link(V.tensor_tensor(gwl[:, :, :], graw[:, :, :], gwh[:, :, :], ALU.subtract), v_gate)
            link(V.memset(yN[:, :, :], 0.0))
            for n in range(BATCH * 3):
                b, c = n // 3, n % 3
                dve.wait_ge(s_mod, n + 1)
                V.tensor_copy(modb[:, b, c * 512:(c + 1) * 512], psS[n % 2][:, :]).then_inc(v_mod, 1)
            dve.wait_ge(v_mod, 6)
            SA, CA, GA, SB, CB, GB = (modb[:, :, i * D:(i + 1) * D] for i in range(6))
            for m in (CA, CB):
                link(V.tensor_scalar(m, m, 1.0, None, ALU.add))
            for m in (GA, GB):
                link(V.tensor_scalar(gsign[:, :, :], m, 0.0, 2.0, ALU.is_ge, ALU.mult))
                link(V.tensor_scalar(gsign[:, :, :], gsign[:, :, :], 1.0, None, ALU.subtract))
                link(V.tensor_tensor(m, m, gsign[:, :, :], ALU.mult))
                link(V.scalar_tensor_tensor(m, m, 0.25, gsign[:, :, :], ALU.max, ALU.mult))

            def layer_norm(src, n):
                for t in range(NT):
                    V.bn_stats(stats[:, t, :], src[:, t, :]).then_inc(v_stat, 1)
                dve.wait_ge(v_stat, NT * (n + 1))
                for t in range(NT):
                    V.bn_aggr(mv[:, t, :], stats[:, t, :]).then_inc(v_aggr, 1)
                dve.wait_ge(v_aggr, NT * (n + 1))
                link(V.tensor_scalar(vare[:, :], mv[:, :, 1], EPS, None, ALU.add), v_var)

            def finish_roots(n):
                dve.wait_ge(a_root, n + 1)
                link(V.reciprocal(rs[:, :], sd[:, :]))

            def mean_square(src):
                for t in range(NT):
                    link(V.tensor_tensor_reduce(sq[:, :], src[:, t, :], src[:, t, :], 1.0 / D, 0.0, ALU.mult, ALU.add,
                                                vare[:, t:t + 1]))
                link(V.tensor_scalar(vare[:, :], vare[:, :], EPS, None, ALU.add), v_var)

            def modulate(dst, src, t, c, s):
                b = t // TB
                link(V.tensor_scalar(dst, src[:, t, :], mv[:, t, 0:1], rs[:, t:t + 1], ALU.subtract, ALU.mult))
                link(V.tensor_tensor(dst, dst, c[:, b, :], ALU.mult))
                return V.tensor_tensor(dst, dst, s[:, b, :], ALU.add)

            def features_lo(phase, t):
                n = NT * phase + t
                dve.wait_ge(a_hth, n + 1)
                V.tensor_tensor(hTl[:, :, t * P:(t + 1) * P], psX[t % 2][:, 0:D].rearrange("p (k n) -> p k n", k=KC),
                                hTh[:, :, t * P:(t + 1) * P], ALU.subtract).then_inc(v_htl, 1)

            def features(phase, make):
                for t in range(NT):
                    wait(dve, s_ht, NT * phase + t + 1 - 2)
                    make(t)
                    if t:
                        features_lo(phase, t - 1)
                features_lo(phase, NT - 1)

            def attention(L):
                def mask_max(g, s, j):
                    n = L.ntiles(s) * P
                    wait(dve, s_S, L.head(g, s, j))
                    if j == 0:
                        wait(dve, s_X, L.kt_all(g, s - 2))
                    apart(dve)
                    mask = mwin[:, 2 * P - n:] if L is LA else mcau[:, SEQ - n:]
                    V.tensor_tensor_reduce(probs[:, s % 2, j, 0:n], psS[j % 2][:, 0:n], mask, -SCALE, 3e38,
                                           ALU.add, ALU.min, nmax[:, s % 2, j:j + 1]).then_inc(v_max, 1)

                def normalise(g, s):
                    wait(dve, a_exp, L.head(g, s, QM - 1))
                    d = sums
                    if L is LA:
                        wait(dve, a_es, L.unit(g, s))
                        V.tensor_tensor(den[:, s % 2, :], sums[:, s % 2, :], esink[:, s % 2, :], ALU.add).then_inc(v_den, 1)
                        wait(dve, v_den, L.unit(g, s))
                        d = den
                    V.reciprocal(rden[:, s % 2, :], d[:, s % 2, :]).then_inc(v_rden, 1)
                    wait(dve, v_rden, L.unit(g, s))
                    n = L.ntiles(s) * P
                    for j in range(QM):
                        pj = probs[:, s % 2, j, 0:n]
                        V.tensor_scalar(pj, pj, rden[:, s % 2, j:j + 1], None, ALU.mult).then_inc(v_norm, 1)

                def probs_lo(g, s, k):
                    slot = L.kt_slot(s, k)
                    wait(dve, a_ph, L.kt(g, s, k))
                    V.tensor_tensor(pTl[:, slot, :], psX[slot][:, :], pTh[:, slot, :], ALU.subtract).then_inc(v_pl, 1)

                def out_lo(g, s):
                    wait(dve, a_oh, L.unit(g, s))
                    V.tensor_tensor(ol[:, s % 2, :], psO[:, 0:2 * P], oh[:, s % 2, :], ALU.subtract).then_inc(v_ol, 1)

                def rotate(g, s):
                    wait(dve, s_proj, L.unit(g, s))
                    qkp = psP[:, 0:HQ + HD]
                    wait(dve, g_add, L.unit(g, s - 1))
                    t = s % TB
                    heads = qkp.rearrange("p (h d) -> p h d", d=HD)
                    V.tensor_tensor(t1[:, :, :], heads, cosw[:, t, :].unsqueeze(1).broadcast_to([P, QM + 1, HD]),
                                    ALU.mult)
                    halves = qkp.rearrange("p (h r d) -> p h r d", r=2, d=HD // 2)
                    t2h = t2[:, :, :].rearrange("p h (r d) -> p h r d", r=2)
                    sinr = sinw[:, t, :].rearrange("p (r d) -> p r d", r=2)
                    for r in range(2):
                        last = V.tensor_tensor(t2h[:, :, r, :], halves[:, :, 1 - r, :],
                                               sinr[:, r, :].unsqueeze(1).broadcast_to([P, QM + 1, HD // 2]), ALU.mult)
                    last.then_inc(v_rope, 1)

                def project_lo(g, s):
                    wait(dve, a_vh, L.unit(g, s))
                    if L is LB:
                        V.tensor_tensor(qn[:, s % 2, :, 1, :], psP[:, 0:HQ].rearrange("p (h d) -> p h d", d=HD),
                                        qn[:, s % 2, :, 0, :], ALU.subtract)
                        V.tensor_tensor(kn[:, s % 2, 1, :, :], psP[:, HQ:HQ + HD].unsqueeze(1).broadcast_to([P, 2, HD]),
                                        kn[:, s % 2, 0, :, :], ALU.subtract).then_inc(qk_lo, 1)
                    V.tensor_tensor(vpad[:, 1, s % NT, HD:2 * HD], psP[:, HQ + HD:QKV], vpad[:, 0, s % NT, HD:2 * HD],
                                    ALU.subtract).then_inc(v_vl, 1)

                def write_kT(g, s):
                    wait(dve, s_tk, L.unit(g, s))
                    wait(dve, s_S, L.head(g - 1, s % NT // TB * TB + TB - 1 + s // NT * NT, QM - 1))
                    V.tensor_copy(kT[:, :, s % NT * P:(s % NT + 1) * P], psT[:, 0:2 * P].rearrange("p (c n) -> p c n", c=2))\
                     .then_inc(v_tk, 1)

                def add_y(g, s):
                    wait(dve, s_Y, L.unit(g, s))
                    yt = yN[:, s % NT, :]
                    wait(dve, v_y, L.unit(g, s - 1))
                    V.tensor_tensor(yt, psY[:, 0:D], yt, ALU.add).then_inc(v_y, 1)

                def step(g, s):
                    now, back, ahead = exists(g, s), exists(g, s - 1), exists(g, s + 4)
                    nk = L.ntiles(s - 1) if back else 0
                    if now:
                        mask_max(g, s, 0)
                    if back:
                        normalise(g, s - 1)
                    if now:
                        mask_max(g, s, 1)
                    if exists(g, s - 2):
                        add_y(g, s - 2)
                    if ahead and L is LA:
                        rotate(g, s + 4)
                    if nk > 0:
                        probs_lo(g, s - 1, 0)
                    if now:
                        mask_max(g, s, 2)
                    if nk > 1:
                        probs_lo(g, s - 1, 1)
                    if now:
                        mask_max(g, s, 3)
                    if nk > 2:
                        probs_lo(g, s - 1, 2)
                    if nk > 3:
                        probs_lo(g, s - 1, 3)
                    if exists(g, s + 3):
                        write_kT(g, s + 3)
                    if ahead:
                        project_lo(g, s + 4)
                    if back:
                        out_lo(g, s - 1)

                rounds(dve, step)

            dve.wait_ge(ld_x, 16)
            layer_norm(xN, 0)
            finish_roots(0)
            features(0, lambda t: modulate(hb[:, t % 2, :], xN, t, CA, SA).then_inc(v_h, 1))
            attention(LA)

            dve.wait_ge(v_y, LA.unit(NKV - 1, NT - 1))
            link(V.tensor_tensor(yN[:, :, :], yN[:, :, :], outb_b[:, :].unsqueeze(1).broadcast_to([P, NT, D]), ALU.add))
            for b in range(BATCH):
                at = slice(b * TB, (b + 1) * TB)
                link(V.tensor_tensor(yN[:, at, :], yN[:, at, :], GA[:, b, :].unsqueeze(1).broadcast_to([P, TB, D]), ALU.mult))
            link(V.tensor_tensor(xN[:, :, :], xN[:, :, :], yN[:, :, :], ALU.add))
            link(V.memset(yN[:, :, :], 0.0))
            layer_norm(xN, 1)
            finish_roots(1)
            for t in range(NT):
                link(modulate(uN[:, t, :], xN, t, CB, SB))
            mean_square(uN)
            finish_roots(2)
            features(1, lambda t: V.scalar_tensor_tensor(hb[:, t % 2, :], uN[:, t, :], rs[:, t:t + 1], ln1_b[:, :],
                                                         ALU.mult, ALU.mult).then_inc(v_h, 1))
            attention(LB)

            dve.wait_ge(v_y, LB.unit(NKV - 1, NT - 1))
            link(V.tensor_tensor(uN[:, :, :], uN[:, :, :], yN[:, :, :], ALU.add))
            link(V.memset(yN[:, :, :], 0.0))
            mean_square(uN)
            finish_roots(3)
            features(2, lambda t: V.scalar_tensor_tensor(hb[:, t % 2, :], uN[:, t, :], rs[:, t:t + 1], ln2_b[:, :],
                                                         ALU.mult, ALU.mult).then_inc(v_h, 1))

            dve.wait_ge(s_rt, NT)
            logits = psY[:, 0:NT * NE].rearrange("p (t e) -> p t e", e=NE)
            link(V.tensor_reduce(lmax[:, :], logits, mybir.AxisListType.X, ALU.max))
            link(V.tensor_scalar(lmax[:, :], lmax[:, :], -1.0, None, ALU.mult), v_lmax)
            dve.wait_ge(a_rt, NT)
            link(V.reciprocal(prr[:, :], prs[:, :]))
            link(V.tensor_tensor(pr[:, :, :], pr[:, :, :], prr[:, :].unsqueeze(2).broadcast_to([P, NT, NE]), ALU.mult))
            for t in range(NT):
                link(V.max(top[:, t, :], pr[:, t, :]))
                link(V.max_index(topi[:, t, :], top[:, t, :], pr[:, t, :]))
            link(V.tensor_copy(topf[:, :, :], topi[:, :, :]))
            link(V.tensor_tensor(tops[:, :], top[:, :, 0], top[:, :, 1], ALU.add))
            link(V.reciprocal(topr[:, :], tops[:, :]))
            link(V.tensor_tensor(topw[:, :, :], top[:, :, 0:2], topr[:, :].unsqueeze(2).broadcast_to([P, NT, 2]), ALU.mult))
            idb = ids[:, :].unsqueeze(1).broadcast_to([P, NT, NE])
            for i, c in ((0, c0), (1, c1)):
                link(V.tensor_tensor(c[:, :, :], idb, topf[:, :, i:i + 1].broadcast_to([P, NT, NE]), ALU.is_equal))
                link(V.tensor_tensor(c[:, :, :], c[:, :, :], topw[:, :, i:i + 1].broadcast_to([P, NT, NE]), ALU.mult))
            link(V.tensor_tensor(comb[:, :, :], c0[:, :, :], c1[:, :, :], ALU.add))

            def moe_step(e, r):
                q = M_STEPS * e + r
                if not isinstance(e, int) or e < NE:
                    wait(dve, m_relu, q + 1)
                    wait(dve, m_gh, q - 1)
                    V.tensor_tensor(gated[:, r % 2, :], psX[r % 2][:, :], relu_s[:, r % 2, :], ALU.mult).then_inc(m_g, 1)
                    wait(dve, m_gh, q + 1)
                    V.tensor_tensor(gTl[:, r % 2, :], gated[:, r % 2, :], gTh[:, r % 2, :], ALU.subtract).then_inc(m_gl, 1)
                if r % NF == 0 and (not isinstance(e, int) or q > 0):
                    c = (r - 1) % M_STEPS // NF
                    e2 = e if c == 0 else e - 1
                    wait(dve, m_dn, q)
                    for t in range(TB):
                        yt = yN[:, c * TB + t, :]
                        wait(dve, m_acc, NT * e2 + c * TB + t - 3)
                        V.scalar_tensor_tensor(yt, psD[2 * c + t // 2][:, t % 2 * D:(t % 2 + 1) * D],
                                               comb[:, c * TB + t, bass.ds(e2, 1)], yt, ALU.mult, ALU.add)\
                         .then_inc(m_acc, 1)

            moe_rounds(dve, moe_step, 1)

            dve.wait_ge(m_acc, NT * NE)
            link(V.tensor_tensor(yN[:, :, :], yN[:, :, :], uN[:, :, :], ALU.add))
            for b in range(BATCH):
                at = slice(b * TB, (b + 1) * TB)
                link(V.tensor_tensor(yN[:, at, :], yN[:, at, :], GB[:, b, :].unsqueeze(1).broadcast_to([P, TB, D]), ALU.mult))
            V.tensor_tensor(xN[:, :, :], xN[:, :, :], yN[:, :, :], ALU.add).then_inc(v_out, 1)


def _tables():
    import math
    import numpy as np

    theta, scaling, alpha, beta, icl = 150000.0, 32.0, 1.0, 32.0, 128
    half = HD // 2
    freq = theta ** (np.arange(0, HD, 2, dtype=np.float32) / HD)
    concentration = 0.1 * math.log(scaling) + 1.0
    low = half * math.log(icl / (beta * 2 * math.pi)) / math.log(theta)
    high = half * math.log(icl / (alpha * 2 * math.pi)) / math.log(theta)
    ramp = np.clip((np.arange(half, dtype=np.float32) - low) / (high - low), 0.0, 1.0)
    keep = 1.0 - ramp
    inv_freq = 1.0 / (scaling * freq) * (1.0 - keep) + 1.0 / freq * keep
    freqs = np.outer(np.arange(SEQ, dtype=np.float32), inv_freq)
    cos = (np.cos(freqs) * concentration).astype(np.float32)
    sin = (np.sin(freqs) * concentration).astype(np.float32)
    by_tile = lambda a: np.ascontiguousarray(a.reshape(TB, P, HD).transpose(1, 0, 2))
    cosw = by_tile(np.concatenate([cos, cos], 1))
    sinw = by_tile(np.concatenate([-sin, sin], 1))
    i, j = np.arange(P)[:, None], np.arange(P)[None, :]
    causal = np.where(j > i, NEG, 0.0)
    before = np.where(j <= i, NEG, 0.0)
    mask_win = np.concatenate([before, causal], 1).astype(np.float32)
    mask_causal = np.concatenate([np.zeros((P, SEQ - P)), causal], 1).astype(np.float32)
    return {"rope_cos": cosw, "rope_sin": sinw, "mask_win": mask_win, "mask_causal": mask_causal,
            "ident": np.eye(P, dtype=np.float32), "expert_ids": np.arange(NE, dtype=np.float32)}


def kernel(L0_attn_x, L0_attn_qkv_w, L0_attn_qkv_b, L0_attn_out_w, L0_attn_out_b, L0_attn_sinks,
           L0_ffn_ln1_w, L0_ffn_wq, L0_ffn_wk, L0_ffn_wv, L0_ffn_wo, L0_ffn_ln2_w, L0_ffn_gate_w,
           L0_ffn_w1, L0_ffn_w2, L0_ffn_w3, L0_c, L0_wmod):
    import numpy as np
    import concourse.bacc as bacc
    from concourse.bass_utils import run_bass_kernel_spmd

    arr = np.asarray

    def by_round(wq, wk, wv):
        a = np.concatenate([arr(wq).reshape(KC, P, NKV, HQ), arr(wk).reshape(KC, P, NKV, HD),
                            arr(wv).reshape(KC, P, NKV, HD)], 3)
        return a.transpose(2, 1, 0, 3).reshape(NKV, P, KC * QKV)

    def out_by_round(wo):
        return arr(wo).reshape(NKV, 2, P, D).transpose(0, 2, 1, 3).reshape(NKV, P, 2 * D)

    nq, nk = NKV * HQ, NKV * HD
    wt = arr(L0_attn_qkv_w).T
    b = arr(L0_attn_qkv_b)
    bias = np.concatenate([b[:nq].reshape(NKV, HQ), b[nq:nq + nk].reshape(NKV, HD), b[nq + nk:].reshape(NKV, HD)], 1)
    w13 = np.stack([arr(L0_ffn_w1), arr(L0_ffn_w3)], 1).reshape(NE, 2, KC, P, NF, P).transpose(0, 4, 3, 1, 2, 5)
    w2 = arr(L0_ffn_w2).reshape(NE, NF, P, D)
    w_moe = np.concatenate([w13.reshape(NE, NF, P, 2 * KC * P), w2], 3).reshape(NE * NF, P, EW)
    tables = _tables()
    ins = {
        "x": arr(L0_attn_x),
        "w_attn": by_round(wt[:, :nq], wt[:, nq:nq + nk], wt[:, nq + nk:]),
        "wo_attn": out_by_round(arr(L0_attn_out_w).T),
        "b_attn": bias.reshape(-1),
        "outb": arr(L0_attn_out_b),
        "sinks": arr(L0_attn_sinks),
        "w_ffn": by_round(L0_ffn_wq, L0_ffn_wk, L0_ffn_wv),
        "wo_ffn": out_by_round(L0_ffn_wo),
        "ln1": arr(L0_ffn_ln1_w),
        "ln2": arr(L0_ffn_ln2_w),
        "gate": arr(L0_ffn_gate_w).reshape(KC, P, NE).transpose(1, 0, 2),
        "w_moe": w_moe,
        "cT": arr(L0_c).T.reshape(KC, P, BATCH).transpose(1, 0, 2).reshape(P, KC * BATCH),
        "wmod": arr(L0_wmod).reshape(KC, P, NMOD).transpose(1, 0, 2),
    }
    ins.update({k: tables[k] for k in ("rope_cos", "rope_sin", "mask_win", "mask_causal", "ident", "expert_ids")})
    nc = bacc.Bacc("TRN2", target_bir_lowering=False, num_devices=1)
    arrays, args = {}, []
    for name, a in ins.items():
        arrays[f"in_{name}"] = np.ascontiguousarray(a)
        args.append(nc.dram_tensor(f"in_{name}", a.shape, mybir.dt.from_np(a.dtype), kind="ExternalInput").ap())
    args.append(nc.dram_tensor("out_x", (BATCH, SEQ, D), F32, kind="ExternalOutput").ap())
    build(nc, *args)
    r = run_bass_kernel_spmd(nc, [arrays], core_ids=[0])
    return r.results[0]["out_x"]
```

```python
from contextlib import ExitStack

import concourse.bass as bass
from concourse import mybir

F32 = mybir.dt.float32
F32R = mybir.dt.float32r
U32 = mybir.dt.uint32
I32 = mybir.dt.int32
ALU = mybir.AluOpType
ACT = mybir.ActivationFunctionType

P = 128
BATCH, SEQ, D = 2, 512, 256
NT = BATCH * SEQ // P
TB = SEQ // P
KC = D // P
HD = 64
NKV, QM = 8, 4
HQ = QM * HD
QKV = HQ + 2 * HD
VH = 3
NE, FF = 8, 1024
NF = FF // P
EW = 2 * KC * FF + NF * D
EV = EW // 2
EP = EW // 4
MAXT = 2 * NT + NE - 1
SCALE = HD ** -0.5
NEG = -1e30
EPS = 1e-5
NMOD = 6 * D


class Layer:

    def __init__(self, window, unit_base, kt_base):
        self.window = window
        self.unit_base, self.kt_base = unit_base, kt_base
        self.keys = [min(t + 1, 2) if window else t + 1 for t in range(TB)]
        self.kt_round = sum(self.keys) * BATCH

    def ntiles(self, s):
        return self.keys[s % TB]

    def first_tile(self, s):
        s %= NT
        return s - self.ntiles(s) + 1

    def unit(self, g, s):
        return self.unit_base + NT * g + s + 1

    def head(self, g, s, j):
        return QM * (self.unit(g, s) - 1) + j + 1

    def kt(self, g, s, k):
        before = sum(self.keys[i % TB] for i in range(s % NT)) + s // NT * self.kt_round
        return self.kt_base + self.kt_round * g + before + k + 1

    def kt_all(self, g, s):
        return self.kt(g, s + 1, -1)

    def kt_slot(self, s, k):
        return (sum(self.keys[i % TB] for i in range(s % NT)) + k) % 2


def exists(g, s):
    return not isinstance(g, int) or 0 <= NT * g + s < NT * NKV


def wait(eng, sem, value):
    if not isinstance(value, int) or value > 0:
        eng.wait_ge(sem, value)


def rounds(eng, step):
    for s in range(-2, NT):
        step(0, s)
    with eng.Fori(1, NKV - 1) as g:
        for s in range(NT):
            step(g, s)
    for s in range(NT + 5):
        step(NKV - 1, s)


def build(nc, x, w_attn, wo_attn, b_attn, outb, sinks, w_ffn, wo_ffn, ln1, ln2, gate, w_moe,
          cT, wmod, rope_cos, rope_sin, mask_win, mask_causal, ident, expert_ids, before, xg, yg, out):
    LA, LB = Layer(True, 0, 0), Layer(False, NT * NKV, 0)
    LB.kt_base = LA.kt_round * NKV
    ctx = ExitStack()
    with ctx:
        def sb(name, shape, dt=F32):
            return ctx.enter_context(nc.sbuf_tensor(name, shape, dt))

        of_attention = ExitStack()

        def sb_att(name, shape, dt=F32):
            return of_attention.enter_context(nc.sbuf_tensor(name, shape, dt))

        def sem(name):
            return ctx.enter_context(nc.semaphore(name))

        N_CONST = 13
        idn = sb("idn", [P, P])
        sink_b = sb("sink_b", [P, NKV * QM])
        outb_b = sb("outb_b", [P, D])
        ln1_b = sb("ln1_b", [P, D])
        ln2_b = sb("ln2_b", [P, D])
        ids = sb("ids", [P, NE])
        modb = sb("modb", [P, BATCH, NMOD])
        xN = sb("xN", [P, NT, D])
        uN = sb("uN", [P, NT, D])
        yN = sb("yN", [P, NT, D])
        hb = sb("hb", [P, 2, D])
        hTh = sb("hTh", [P, KC, NT * P], F32R)
        hTl = sb("hTl", [P, KC, NT * P], F32R)
        pick = sb("pick", [P, P], F32R)
        t1 = sb("t1", [P, QM + 1, HD])
        mrawV = sb("mrawV", [P, EV])
        biasraw = mrawV[0:33, 0:NKV * QKV]
        nmax = sb("nmax", [P, 4, QM])
        sums = sb("sums", [P, 4, QM])
        esin = sb("esin", [P, 4, QM])
        esink = sb("esink", [P, 4, QM])
        den = sb("den", [P, 4, QM])
        rden = sb("rden", [P, 4, QM])
        cS = sb("cS", [P, KC * BATCH])
        cE = sb("cE", [P, KC * BATCH])
        cD = sb("cD", [P, KC * BATCH])
        cR = sb("cR", [P, KC * BATCH])
        ones = sb("ones", [P, P])
        cB = sb("cB", [P, KC * BATCH, P])
        stats = sb("stats", [P, NT, 6])
        mv = sb("mv", [P, NT, 2])
        vare = sb("vare", [P, NT])
        sd = sb("sd", [P, NT])
        rs = sb("rs", [P, NT])
        sq = t1[:, 0:D // HD, :].rearrange("p h d -> p (h d)")
        graw = sb("graw", [P, KC, NE])
        gwh = sb("gwh", [P, KC, NE], F32R)
        gwl = sb("gwl", [P, KC, NE], F32R)

        mwin = sb_att("mwin", [P, 2 * P])
        mcau = sb_att("mcau", [P, SEQ])
        cosw = sb_att("cosw", [P, TB, HD])
        sinw = sb_att("sinw", [P, TB, HD])
        wraw = sb_att("wraw", [P, KC * QKV])
        woraw = sb_att("woraw", [P, 2 * D])
        bias = sb_att("bias", [P, NKV * QKV], F32R)
        t2 = sb_att("t2", [P, QM + 1, HD])
        qk = sb_att("qk", [P, QM + 1, HD])
        qn = sb_att("qn", [P, 2, QM, 2, HD], F32R)
        kn = sb_att("kn", [P, 2, 2, 2, HD], F32R)
        wbufs = sb_att("wbufs", [P, 4 * KC * QKV], F32R)
        wh = wbufs[:, 0:2 * KC * QKV]
        wl = wbufs[:, 2 * KC * QKV:]
        woh = sb_att("woh", [P, 2 * 2 * D], F32R)
        wol = sb_att("wol", [P, 2 * 2 * D], F32R)
        bufA = sb_att("bufA", [P, EW], F32R)
        bufB = sb_att("bufB", [P, EW], F32R)
        qT = bufA[:, 0:NT * QM * P].rearrange("p (t n) -> p t n", t=NT)
        kT = bufA[:, NT * QM * P:].rearrange("p (c n) -> p c n", c=2)
        o = 0
        vpad = bufB[:, 0:2 * NT * 3 * HD].rearrange("p (c t n) -> p c t n", c=2, t=NT)
        o = 2 * NT * 3 * HD
        pTh = bufB[:, o:o + 2 * QM * P].rearrange("p (c n) -> p c n", c=2)
        o += 2 * QM * P
        pTl = bufB[:, o:o + 2 * QM * P].rearrange("p (c n) -> p c n", c=2)
        o += 2 * QM * P
        oh = bufB[:, o:o + 2 * 2 * P].rearrange("p (c n) -> p c n", c=2)
        o += 2 * 2 * P
        ol = bufB[:, o:o + 2 * 2 * P].rearrange("p (c n) -> p c n", c=2)
        pbuf = sb_att("pbuf", [P, 4 * QM * SEQ])
        probs = pbuf[:, :].rearrange("p (c h n) -> p c h n", c=4, h=QM)
        wmod_s = pbuf[:, 0:KC * NMOD].rearrange("p (k n) -> p k n", k=KC)
        gsign = pbuf[:, KC * NMOD:KC * NMOD + BATCH * D].rearrange("p (b n) -> p b n", b=BATCH)
        of_attention.close()

        lmax = sb("lmax", [P, NT])
        pr = sb("pr", [P, NT, NE])
        prs = sb("prs", [P, NT])
        prr = sb("prr", [P, NT])
        top = sb("top", [P, NT, 8])
        topi = sb("topi", [P, NT, 8], U32)
        topf = sb("topf", [P, NT, 8])
        tops = sb("tops", [P, NT])
        topr = sb("topr", [P, NT])
        topw = sb("topw", [P, NT, 2])
        c0 = sb("c0", [P, NT, NE])
        c1 = sb("c1", [P, NT, NE])
        picked = sb("picked", [P, NT, NE])
        before_s = sb("before_s", [P, P])
        total = sb("total", [P, NT, NE])
        ahead = sb("ahead", [P, NT + 1, NE])
        slotf = sb("slotf", [P, NT, NE])
        chosen = sb("chosen", [P, 2, NT, NE])
        slotr = sb("slotr", [P, 2 * NT])
        slots = sb("slots", [P, 2 * NT], U32)
        ntil = sb("ntil", [P, NE])
        base = sb("base", [P, NE + 1])
        base_i = sb("base_i", [P, NE + 1], I32)
        wgt_hi = [sb(f"wgt_hi{i}", [P, EW], F32R) for i in range(2)]
        wgt_lo = [sb(f"wgt_lo{i}", [P, EW], F32R) for i in range(2)]
        mrawP = sb("mrawP", [P, 2, EP])
        hAll = sb("hAll", [P, NT, D])
        second = yN
        xin = sb("xin", [P, D])
        gTh, gTl = (a[:, 0, :].rearrange("p (h n) -> p h n", h=2) for a in (hTh, hTl))
        xTh, xTl = (a[:, 1, 0:KC * P].rearrange("p (k n) -> p k n", k=KC) for a in (hTh, hTl))
        relu_s = sb("relu_s", [P, 2, FF // 2])
        gated = sb("gated", [P, 2, FF // 2])
        ysb = sb("ysb", [P, D])

        def bank(name):
            return ctx.enter_context(nc.psum_tensor(name, [P, 512], F32))

        psS = [bank("psS0"), bank("psS1")]
        psX = [bank("psX0"), bank("psX1")]
        psO = bank("psO")
        psP = bank("psP")
        psT = bank("psT")
        psY = bank("psY")
        psG = [psP, psT]

        ld_c = sem("ld_c")
        ld_x = sem("ld_x")
        ld_k = sem("ld_k")
        ld_w = sem("ld_w")
        ld_wo = sem("ld_wo")
        ld_v = sem("ld_v")
        ld_p = [sem("ld_p0"), sem("ld_p1")]
        ld_xg = sem("ld_xg")
        ld_g = [sem("ld_g0"), sem("ld_g1")]
        ld_before = sem("ld_before")
        st_zero = sem("st_zero")
        st_xg = sem("st_xg")
        st_y = sem("st_y")
        st_out = sem("st_out")
        v_seq = sem("v_seq")
        v_zero = sem("v_zero")
        v_cb = sem("v_cb")
        v_mod = sem("v_mod")
        v_gate = sem("v_gate")
        v_stat = sem("v_stat")
        v_aggr = sem("v_aggr")
        v_var = sem("v_var")
        v_lmax = sem("v_lmax")
        v_out = sem("v_out")
        a_ec = sem("a_ec")
        a_root = sem("a_root")
        a_rt = sem("a_rt")
        p_init = sem("p_init")
        s_mod = sem("s_mod")
        s_ht = sem("s_ht")
        v_h = sem("v_h")
        a_hth = sem("a_hth")
        v_htl = sem("v_htl")
        g_hi = sem("g_hi")
        g_w = sem("g_w")
        s_proj = sem("s_proj")
        v_rope = sem("v_rope")
        g_add = sem("g_add")
        g_qh = sem("g_qh")
        qk_lo = sem("qk_lo")
        a_qh = sem("a_qh")
        a_vh = sem("a_vh")
        v_vl = sem("v_vl")
        s_tq = sem("s_tq")
        s_tk = sem("s_tk")
        a_tq = sem("a_tq")
        v_tk = sem("v_tk")
        s_S = sem("s_S")
        v_max = sem("v_max")
        a_exp = sem("a_exp")
        g_es = sem("g_es")
        a_es = sem("a_es")
        v_den = sem("v_den")
        v_rden = sem("v_rden")
        v_norm = sem("v_norm")
        a_norm = sem("a_norm")
        s_X = sem("s_X")
        a_ph = sem("a_ph")
        v_pl = sem("v_pl")
        s_PV = sem("s_PV")
        a_oh = sem("a_oh")
        v_ol = sem("v_ol")
        s_Y = sem("s_Y")
        v_y = sem("v_y")
        s_rt = sem("s_rt")
        v_pick = sem("v_pick")
        s_rank = sem("s_rank")
        v_slot = sem("v_slot")
        w_vh = sem("w_vh")
        w_vl = sem("w_vl")
        w_ph = sem("w_ph")
        w_pl = sem("w_pl")
        s_x = sem("s_x")
        a_x = sem("a_x")
        v_x = sem("v_x")
        m_up = sem("m_up")
        m_relu = sem("m_relu")
        m_g = sem("m_g")
        s_g = sem("s_g")
        m_gh = sem("m_gh")
        m_gl = sem("m_gl")
        m_dn = sem("m_dn")
        a_y = sem("a_y")

        block = ctx.enter_context(nc.Block())

        def apart(eng):
            eng.nop(nofuse=True)

        def first_tile_of(eng, e):
            return eng.value_load(base_i[0:1, bass.ds(e, 1)], min_val=0, max_val=MAXT)

        def experts(eng, begin, tile):
            def pair(m, more):
                for buf in range(2):
                    e = 2 * m + buf
                    begin(e, buf, buf == 0 or more)
                    if tile:
                        with eng.Fori(first_tile_of(eng, e), first_tile_of(eng, e + 1)) as i:
                            tile(i, buf)

            with eng.Fori(0, NE // 2 - 1) as m:
                pair(m, True)
            pair(NE // 2 - 1, False)

        def parity(g):
            return g % 2

        @block.sync
        def _(sp):
            sp.dma_start(cS[:, :], cT).then_inc(ld_c, 16)
            sp.dma_start(wmod_s, wmod).then_inc(ld_c, 16)
            sp.dma_start(xN[:, :, :], x.rearrange("b (t p) d -> p (b t) d", p=P)).then_inc(ld_x, 16)
            for dst, src in ((idn, ident), (mwin, mask_win), (mcau, mask_causal)):
                sp.dma_start(dst[:, :], src).then_inc(ld_k, 16)
            for dst, src in ((cosw, rope_cos), (sinw, rope_sin), (graw, gate)):
                sp.dma_start(dst[:, :, :], src).then_inc(ld_k, 16)
            for dst, src in ((sink_b, sinks), (outb_b, outb), (ln1_b, ln1), (ln2_b, ln2), (ids, expert_ids)):
                sp.dma_start(dst[:, :], src.partition_broadcast(P)).then_inc(ld_k, 16)
            sp.wait_ge(v_zero, 1)
            for row in (0, 32):
                sp.dma_start(biasraw[row:row + 1, :], b_attn.rearrange("(a n) -> a n", a=1)).then_inc(ld_k, 16)

            sp.wait_ge(v_zero, 2)
            for rows, signal in ((xg, st_zero), (yg, st_y)):
                sp.dma_start(rows.rearrange("(t p) d -> p t d", p=P), yN[:, 0:1, :].broadcast_to([P, MAXT + 2, D]))\
                  .then_inc(signal, 16)

            for n, (w_d, wo_d) in enumerate(((w_attn, wo_attn), (w_ffn, wo_ffn))):
                def load_round(g):
                    done = 3 * (NKV * n + g)
                    wait(sp, g_w, done)
                    sp.dma_start(wraw[:, :], w_d[bass.ds(g, 1)].rearrange("o p n -> (o p) n")).then_inc(ld_w, 16)
                    sp.dma_start(woraw[:, :], wo_d[bass.ds(g, 1)].rearrange("o p n -> (o p) n")).then_inc(ld_wo, 16)

                load_round(0)
                with sp.Fori(1, NKV) as g:
                    load_round(g)

            def load_expert(e):
                rows = w_moe[bass.ds(e, 1)].rearrange("o p n -> (o p) n")
                wait(sp, w_vl, 2 * e)
                sp.dma_start(mrawV[:, :], rows[:, 0:EV]).then_inc(ld_v, 16)
                for j in range(2):
                    if isinstance(e, int) and e == 0:
                        sp.wait_ge(v_h, 2 * NT + 1)
                    wait(sp, w_pl, 2 * e - 1 + j)
                    sp.dma_start(mrawP[:, j, :], rows[:, EV + j * EP:EV + (j + 1) * EP]).then_inc(ld_p[j], 16)

            sp.wait_ge(v_gate, 1)
            load_expert(0)
            sp.dma_start(before_s[:, :], before).then_inc(ld_before, 16)
            with sp.Fori(1, NE) as e:
                load_expert(e)
            for b in range(BATCH):
                sp.wait_ge(v_out, b + 1)
                sp.dma_start(out[b].rearrange("(t p) d -> p t d", p=P), xN[:, b * TB:(b + 1) * TB, :]).then_inc(st_out, 16)
            sp.wait_ge(st_out, 16 * BATCH)

        @block.gpsimd
        def _(pool):
            nc.gpsimd.memset(bufB[:, 0:2 * NT * 3 * HD].bitcast(F32), 0.0).then_inc(p_init, 1)

            for L in (LA, LB):
                n = 0 if L is LA else 1

                def split_piece(g, piece, L=L, n=n):
                    r = NKV * n + g
                    if piece < 2:
                        wait(pool, ld_w, 16 * (r + 1))
                        wait(pool, s_proj, L.unit(g - 2, NT - 1))
                        at = parity(g) * (KC * QKV) + piece * QKV
                        hi, lo, raw = wh[:, bass.ds(at, QKV)], wl[:, bass.ds(at, QKV)], wraw[:, piece * QKV:(piece + 1) * QKV]
                    else:
                        wait(pool, ld_wo, 16 * (r + 1))
                        wait(pool, s_Y, L.unit(g - 2, NT - 1))
                        at = parity(g) * 2 * D
                        hi, lo, raw = woh[:, bass.ds(at, 2 * D)], wol[:, bass.ds(at, 2 * D)], woraw[:, :]
                    apart(pool)
                    nc.gpsimd.tensor_copy(hi, raw).then_inc(g_hi, 1)
                    wait(pool, g_hi, 3 * r + piece + 1)
                    apart(pool)
                    nc.gpsimd.tensor_tensor(lo, raw, hi, ALU.subtract).then_inc(g_w, 1)

                def step(g, s, L=L):
                    if L is LA and exists(g, s):
                        wait(pool, v_max, L.head(g, s, QM - 1))
                        wait(pool, a_es, L.unit(g, s - 4))
                        apart(pool)
                        nc.gpsimd.tensor_tensor(esin[:, s % 4, :], sink_b[:, bass.ds(g * QM, QM)],
                                                nmax[:, s % 4, :], ALU.add).then_inc(g_es, 1)
                    if L is LA and exists(g, s + 2):
                        wait(pool, v_rope, L.unit(g, s + 2))
                        wait(pool, qk_lo, L.unit(g, s + 1))
                        nc.gpsimd.tensor_tensor(qk[:, :, :], t1[:, :, :], t2[:, :, :], ALU.add).then_inc(g_add, 1)
                        wait(pool, g_add, L.unit(g, s + 2))
                        wait(pool, s_tk, L.unit(g, s))
                        k2 = qk[:, QM, :].unsqueeze(1).broadcast_to([P, 2, HD])
                        apart(pool)
                        nc.gpsimd.tensor_copy(qn[:, s % 2, :, 0, :], qk[:, 0:QM, :])
                        nc.gpsimd.tensor_copy(kn[:, s % 2, 0, :, :], k2).then_inc(g_qh, 1)
                        wait(pool, g_qh, L.unit(g, s + 2))
                        nc.gpsimd.tensor_tensor(qn[:, s % 2, :, 1, :], qk[:, 0:QM, :], qn[:, s % 2, :, 0, :],
                                                ALU.subtract)
                        nc.gpsimd.tensor_tensor(kn[:, s % 2, 1, :, :], k2, kn[:, s % 2, 0, :, :],
                                                ALU.subtract).then_inc(qk_lo, 1)
                    if s in (0, 1, 2) and exists(g, NT):
                        split_piece(g + 1, s)

                for piece in range(3):
                    split_piece(0, piece)
                rounds(pool, step)

            def split_expert(e, buf):
                wait(pool, w_vh, 2 * e + 1)
                for j in range(2):
                    at = slice(EV + j * EP, EV + (j + 1) * EP)
                    wait(pool, ld_p[j], 16 * (e + 1))
                    apart(pool)
                    nc.gpsimd.tensor_copy(wgt_hi[buf][:, at], mrawP[:, j, :]).then_inc(w_ph, 1)
                    wait(pool, w_ph, 2 * e + j + 1)
                    apart(pool)
                    nc.gpsimd.tensor_tensor(wgt_lo[buf][:, at], mrawP[:, j, :], wgt_hi[buf][:, at], ALU.subtract)\
                      .then_inc(w_pl, 1)

            split_expert(0, 0)
            pool.wait_ge(v_slot, 1)
            pool.wait_ge(st_zero, 16)
            for t in range(NT):
                for i in range(2):
                    n = i * NT + t
                    nc.gpsimd.indirect_dma_start(xg[:, :], bass.IndirectOffsetOnAxis(ap=slots[:, n:n + 1], axis=0),
                                                 hAll[:, t, :], None).then_inc(st_xg, 16)

            def begin(e, buf, more):
                if more:
                    split_expert(e + 1, 1 - buf)

            experts(pool, begin, None)

            tiles = first_tile_of(pool, NE)
            pool.wait_ge(st_y, 16 * tiles + 16)
            apart(pool)
            for t in range(NT):
                for i, dst in ((0, hAll), (1, second)):
                    n = i * NT + t
                    nc.gpsimd.indirect_dma_start(dst[:, t, :], None, yg[:, :],
                                                 bass.IndirectOffsetOnAxis(ap=slots[:, n:n + 1], axis=0))\
                      .then_inc(ld_g[t // TB], 16)

        @block.tensor
        def _(pe):
            mm = nc.tensor.matmul

            pe.wait_ge(v_cb, KC * BATCH)
            pe.wait_ge(ld_c, 32)
            for n in range(BATCH * 3):
                b, c = n // 3, n % 3
                wait(pe, v_mod, n - 1)
                for k in range(KC):
                    last = mm(psS[n % 2][:, :], cB[:, k * BATCH + b, :], wmod_s[:, k, c * 512:(c + 1) * 512],
                              start=(k == 0), stop=(k == KC - 1))
                last.then_inc(s_mod, 1)

            def to_features(phase):
                for t in range(NT):
                    n = NT * phase + t
                    pe.wait_ge(v_h, n + 1)
                    if phase == 0 and t == 0:
                        pe.wait_ge(ld_k, 16 * N_CONST)
                    src = hAll[:, t, :] if phase == 2 else hb[:, t % 2, :]
                    wait(pe, v_htl, n + 1 - 2)
                    for k in range(KC):
                        last = nc.tensor.transpose(psX[t % 2][:, k * P:(k + 1) * P], src[:, k * P:(k + 1) * P],
                                                   idn[:, :])
                    last.then_inc(s_ht, 1)

            def attention(L, phase):
                def scores(g, s, j):
                    wait(pe, v_max, L.head(g, s, j) - 2)
                    if j == 0:
                        wait(pe, a_tq, L.unit(g, s))
                        wait(pe, v_tk, L.unit(g, s))
                    n = L.ntiles(s) * P
                    k0 = L.first_tile(s) * P
                    for c in range(2):
                        last = mm(psS[j % 2][:, 0:n], qT[:, s % NT, j * P:(j + 1) * P], kT[:, c, k0:k0 + n],
                                  start=(c == 0), stop=(c == 1))
                    last.then_inc(s_S, 1)

                def turn_probs(g, s, k):
                    if k == 0:
                        wait(pe, v_norm, L.unit(g, s))
                        wait(pe, a_norm, L.unit(g, s))
                    slot = L.kt_slot(s, k)
                    wait(pe, v_pl, L.kt(g, s, k) - 2)
                    for j in range(QM):
                        last = nc.tensor.transpose(psX[slot][:, j * P:(j + 1) * P],
                                                   probs[:, s % 4, j, k * P:(k + 1) * P], idn[:, :])
                    last.then_inc(s_X, 1)

                def values(g, s, k):
                    slot = L.kt_slot(s, k)
                    if k == 0:
                        wait(pe, v_ol, L.unit(g, s - 1))
                        wait(pe, v_vl, L.unit(g, s))
                    wait(pe, v_pl, L.kt(g, s, k))
                    kv = L.first_tile(s) + k
                    pairs = lambda p: p[:, slot, :].rearrange("p (i r q) -> p r i q", r=2, q=P)
                    n = 0
                    for v, pT in ((0, pTh), (1, pTh), (0, pTl)):
                        for r in range(2):
                            lhsT = vpad[:, v, kv, HD:3 * HD] if r == 0 else vpad[:, v, kv, 0:2 * HD]
                            last = mm(psO[:, 0:2 * P], lhsT, pairs(pT)[:, r],
                                      start=(k == 0 and n == 0), stop=(k == L.ntiles(s) - 1 and n == 5))
                            n += 1
                    last.then_inc(s_PV, 1)

                def project(g, s):
                    r = 0 if L is LA else NKV
                    wait(pe, v_vl, L.unit(g, s - 1))
                    if s % NT == 0:
                        g2 = g + s // NT
                        wait(pe, g_w, 3 * (r + g2) + 2)
                    if isinstance(g, int) and g == 0 and 0 <= s < NT:
                        pe.wait_ge(v_htl, NT * phase + s + 1)
                    at = parity(g + s // NT) * (KC * QKV)
                    t = s % NT
                    n = 0
                    for k in range(KC):
                        for a, w in ((hTh, wh), (hTl, wh), (hTh, wl)):
                            n += 1
                            last = mm(psP[:, 0:QKV], a[:, k, t * P:(t + 1) * P], w[:, bass.ds(at + k * QKV, QKV)],
                                      start=(n == 1), stop=(n == 3 * KC and L is LB))
                    if L is LA:
                        last = mm(psP[:, 0:QKV], pick[:, :], bias[:, bass.ds((g + s // NT) * QKV, QKV)],
                                  start=False, stop=True)
                    last.then_inc(s_proj, 1)

                def turn_q(g, s):
                    wait(pe, qk_lo, L.unit(g, s))
                    wait(pe, v_tk, L.unit(g, s - 1))
                    for j in range(QM):
                        last = nc.tensor.transpose(psT[:, j * P:(j + 1) * P],
                                                   qn[:, s % 2, j, :, :].rearrange("p c d -> p (c d)").bitcast(F32),
                                                   idn[:, :])
                    last.then_inc(s_tq, 1)

                def turn_k(g, s):
                    wait(pe, a_tq, L.unit(g, s))
                    for c in range(2):
                        kk = kn[:, s % 2, c, :, :].rearrange("p r d -> p (r d)").bitcast(F32)
                        last = nc.tensor.transpose(psT[:, c * P:(c + 1) * P], kk, idn[:, :])
                    last.then_inc(s_tk, 1)

                def out_project(g, s):
                    r = 0 if L is LA else NKV
                    wait(pe, v_ol, L.unit(g, s))
                    wait(pe, v_y, L.unit(g, s - 1))
                    g2 = g + s // NT
                    if s % NT == 0:
                        wait(pe, g_w, 3 * (r + g2) + 3)
                    at = parity(g2) * 2 * D
                    n = 0
                    for i in range(2):
                        for a, w in ((oh, woh), (ol, woh), (oh, wol)):
                            n += 1
                            last = mm(psY[:, 0:D], a[:, s % 2, i * P:(i + 1) * P], w[:, bass.ds(at + i * D, D)],
                                      start=(n == 1), stop=(n == 6))
                    last.then_inc(s_Y, 1)

                def step_window(g, s):
                    now = exists(g, s)
                    ahead = exists(g, s + 2)
                    nk = L.ntiles(s - 2) if exists(g, s - 2) else 0
                    if exists(g, s - 3):
                        values(g, s - 3, L.ntiles(s - 3) - 1)
                    if nk > 0:
                        turn_probs(g, s - 2, 0)
                    if now:
                        scores(g, s, 0)
                        scores(g, s, 1)
                    if ahead:
                        project(g, s + 2)
                    if nk > 1:
                        turn_probs(g, s - 2, 1)
                    if exists(g, s - 4):
                        out_project(g, s - 4)
                    if now:
                        scores(g, s, 2)
                        scores(g, s, 3)
                    if exists(g, s + 1):
                        turn_q(g, s + 1)
                    if nk > 1:
                        values(g, s - 2, 0)
                    if exists(g, s + 1):
                        turn_k(g, s + 1)

                def step_causal(g, s):
                    now = exists(g, s)
                    ahead = exists(g, s + 2)
                    nk = L.ntiles(s - 2) if exists(g, s - 2) else 0
                    if now:
                        scores(g, s, 0)
                    if nk > 0:
                        turn_probs(g, s - 2, 0)
                    if now:
                        scores(g, s, 1)
                    if exists(g, s - 3):
                        values(g, s - 3, L.ntiles(s - 3) - 1)
                    if nk > 1:
                        turn_probs(g, s - 2, 1)
                    if ahead:
                        project(g, s + 2)
                    if now:
                        scores(g, s, 2)
                    if exists(g, s + 1):
                        turn_q(g, s + 1)
                    if exists(g, s - 4):
                        out_project(g, s - 4)
                    if nk > 2:
                        turn_probs(g, s - 2, 2)
                    if nk > 1:
                        values(g, s - 2, 0)
                    if nk > 2:
                        values(g, s - 2, 1)
                    if exists(g, s + 1):
                        turn_k(g, s + 1)
                    if nk > 3:
                        turn_probs(g, s - 2, 3)
                    if now:
                        scores(g, s, 3)
                    if nk > 3:
                        values(g, s - 2, 2)

                rounds(pe, step_window if L is LA else step_causal)

            to_features(0)
            attention(LA, 0)
            to_features(1)
            attention(LB, 1)
            to_features(2)

            for t in range(NT):
                pe.wait_ge(v_htl, 2 * NT + t + 1)
                if t == 0:
                    pe.wait_ge(v_gate, 1)
                n = 0
                for k in range(KC):
                    for a, w in ((hTh, gwh), (hTl, gwh), (hTh, gwl), (hTl, gwl)):
                        n += 1
                        last = mm(psY[:, t * NE:(t + 1) * NE], a[:, k, t * P:(t + 1) * P], w[:, k, :],
                                  start=(t == 0 and n == 1), stop=(n == 4 * KC), skip_group_check=True)
                last.then_inc(s_rt, 1)

            pe.wait_ge(v_pick, 1)
            pe.wait_ge(ld_before, 16)
            picks = picked[:, :, :].rearrange("p t e -> p (t e)")
            mm(psO[:, 0:NT * NE], before_s[:, :], picks, start=True, stop=True)
            mm(psP[:, 0:NT * NE], ones[:, :], picks, start=True, stop=True).then_inc(s_rank, 1)

            def turn_tokens(i):
                wait(pe, ld_xg, 16 * (i + 1))
                wait(pe, v_x, i)
                for k in range(KC):
                    last = nc.tensor.transpose(psY[:, k * P:(k + 1) * P], xin[:, k * P:(k + 1) * P], idn[:, :])
                last.then_inc(s_x, 1)

            def up_gate(i, buf, h):
                if h == 0:
                    wait(pe, v_x, i + 1)
                for m, ps in ((0, psS[h]), (1, psX[h])):
                    n = 0
                    for k in range(KC):
                        at = (m * KC + k) * FF + h * 512
                        for a, w in ((xTh, wgt_hi), (xTl, wgt_hi), (xTh, wgt_lo)):
                            n += 1
                            last = mm(ps[:, :], a[:, k, :], w[buf][:, at:at + 512], start=(n == 1), stop=(n == 3 * KC))
                last.then_inc(m_up, 1)

            def turn_hidden(i, h):
                wait(pe, m_g, 2 * i + h + 1)
                for f in range(NF // 2):
                    last = nc.tensor.transpose(psG[h][:, f * P:(f + 1) * P], gated[:, h, f * P:(f + 1) * P], idn[:, :])
                last.then_inc(s_g, 1)

            def down(i, buf, h):
                wait(pe, m_gl, 2 * i + h + 1)
                n = 0
                for f in range(NF // 2):
                    at = 2 * KC * FF + (h * NF // 2 + f) * D
                    for a, w in ((gTh, wgt_hi), (gTl, wgt_hi), (gTh, wgt_lo)):
                        n += 1
                        last = mm(psO[:, 0:D], a[:, h, f * P:(f + 1) * P], w[buf][:, at:at + D],
                                  start=(h == 0 and n == 1), stop=(h == 1 and n == 3 * NF // 2))
                if h == 1:
                    last.then_inc(m_dn, 1)

            def begin(e, buf, more):
                wait(pe, w_vl, 2 * e + 2)
                wait(pe, w_pl, 2 * e + 2)
                apart(pe)

            def tile(i, buf):
                up_gate(i, buf, 0)
                up_gate(i, buf, 1)
                turn_tokens(i + 1)
                turn_hidden(i, 0)
                turn_hidden(i, 1)
                down(i, buf, 0)
                down(i, buf, 1)

            pe.wait_ge(v_slot, 1)
            turn_tokens(0)
            experts(pe, begin, tile)

        @block.scalar
        def _(act):
            copy = lambda o, i: nc.scalar.activation(o, i, ACT.Copy)

            act.wait_ge(ld_c, 32)
            nc.scalar.activation(cE[:, :], cS[:, :], ACT.Exp, scale=-1.0).then_inc(a_ec, 1)

            def roots(n):
                act.wait_ge(v_var, n + 1)
                nc.scalar.activation(sd[:, :], vare[:, :], ACT.Sqrt).then_inc(a_root, 1)

            def features_hi(phase):
                for t in range(NT):
                    n = NT * phase + t
                    act.wait_ge(s_ht, n + 1)
                    copy(hTh[:, :, t * P:(t + 1) * P], psX[t % 2][:, 0:D].rearrange("p (k n) -> p k n", k=KC))\
                        .then_inc(a_hth, 1)

            def attention(L):
                def exp_head(g, s, j):
                    n = L.ntiles(s) * P
                    wait(act, v_max, L.head(g, s, j))
                    if j == 0 and L is LB:
                        wait(act, v_rden, L.unit(g, s - 4))
                    if j == 0 and L is LA:
                        wait(act, v_den, L.unit(g, s - 4))
                    pj = probs[:, s % 4, j, 0:n]
                    nc.scalar.activation(pj, pj, ACT.Exp, bias=nmax[:, s % 4, j:j + 1], scale=-1.0,
                                         accum_out=sums[:, s % 4, j:j + 1]).then_inc(a_exp, 1)

                def normalise(g, s):
                    wait(act, v_rden, L.unit(g, s))
                    for j in range(VH, QM):
                        pj = probs[:, s % 4, j, 0:L.ntiles(s) * P]
                        last = nc.scalar.activation(pj, pj, ACT.Copy, scale=rden[:, s % 4, j:j + 1])
                    last.then_inc(a_norm, 1)

                def sink_exp(g, s):
                    wait(act, g_es, L.unit(g, s))
                    wait(act, v_den, L.unit(g, s - 4))
                    nc.scalar.activation(esink[:, s % 4, :], esin[:, s % 4, :], ACT.Exp).then_inc(a_es, 1)

                def probs_hi(g, s, k):
                    slot = L.kt_slot(s, k)
                    wait(act, s_X, L.kt(g, s, k))
                    wait(act, s_PV, L.kt(g, s, k) - 2)
                    copy(pTh[:, slot, :], psX[slot][:, :]).then_inc(a_ph, 1)

                def out_hi(g, s):
                    wait(act, s_PV, L.kt_all(g, s))
                    wait(act, s_Y, L.unit(g, s - 2))
                    copy(oh[:, s % 2, :], psO[:, 0:2 * P]).then_inc(a_oh, 1)

                def project_hi(g, s):
                    wait(act, s_proj, L.unit(g, s))
                    if L is LB:
                        wait(act, s_tk, L.unit(g, s - 2))
                        copy(qn[:, s % 2, :, 0, :], psP[:, 0:HQ].rearrange("p (h d) -> p h d", d=HD))
                        copy(kn[:, s % 2, 0, :, :], psP[:, HQ:HQ + HD].unsqueeze(1).broadcast_to([P, 2, HD]))\
                            .then_inc(a_qh, 1)
                    else:
                        wait(act, v_rope, L.unit(g, s))
                    wait(act, s_PV, L.kt_all(g - 1, s % NT // TB * TB + TB - 1 + s // NT * NT))
                    copy(vpad[:, 0, s % NT, HD:2 * HD], psP[:, HQ + HD:QKV]).then_inc(a_vh, 1)

                def write_qT(g, s):
                    wait(act, s_tq, L.unit(g, s))
                    wait(act, s_S, L.head(g - 1, s, QM - 1))
                    copy(qT[:, s % NT, :], psT[:, :]).then_inc(a_tq, 1)

                def step_window(g, s):
                    now = exists(g, s)
                    back = exists(g, s - 1)
                    ahead = exists(g, s + 2)
                    nk = L.ntiles(s - 2) if exists(g, s - 2) else 0
                    if back:
                        sink_exp(g, s - 1)
                    if nk > 0:
                        probs_hi(g, s - 2, 0)
                    if now:
                        exp_head(g, s, 0)
                    if exists(g, s - 3):
                        out_hi(g, s - 3)
                    if back:
                        normalise(g, s - 1)
                    if nk > 1:
                        probs_hi(g, s - 2, 1)
                    if now:
                        exp_head(g, s, 1)
                    if exists(g, s + 1):
                        write_qT(g, s + 1)
                    if now:
                        exp_head(g, s, 2)
                    if ahead:
                        project_hi(g, s + 2)
                    if now:
                        exp_head(g, s, 3)

                def step_causal(g, s):
                    now = exists(g, s)
                    back = exists(g, s - 1)
                    ahead = exists(g, s + 2)
                    nk = L.ntiles(s - 2) if exists(g, s - 2) else 0
                    if now:
                        exp_head(g, s, 0)
                    if nk > 0:
                        probs_hi(g, s - 2, 0)
                    if now:
                        exp_head(g, s, 1)
                    if exists(g, s - 3):
                        out_hi(g, s - 3)
                    if nk > 1:
                        probs_hi(g, s - 2, 1)
                    if back:
                        normalise(g, s - 1)
                    if exists(g, s + 1):
                        write_qT(g, s + 1)
                    if nk > 2:
                        probs_hi(g, s - 2, 2)
                    if nk > 3:
                        probs_hi(g, s - 2, 3)
                    if ahead:
                        project_hi(g, s + 2)
                    if now:
                        exp_head(g, s, 2)
                        exp_head(g, s, 3)

                if L is LA:
                    act.wait_ge(p_init, 1)
                rounds(act, step_window if L is LA else step_causal)

            roots(0)
            features_hi(0)
            attention(LA)
            roots(1)
            roots(2)
            features_hi(1)
            attention(LB)
            roots(3)
            features_hi(2)

            act.wait_ge(v_lmax, 1)
            for t in range(NT):
                nc.scalar.activation(pr[:, t, :], psY[:, t * NE:(t + 1) * NE], ACT.Exp, bias=lmax[:, t:t + 1],
                                     accum_out=prs[:, t:t + 1]).then_inc(a_rt, 1)

            def split_hi(e, buf):
                wait(act, ld_v, 16 * (e + 1))
                for j in range(2):
                    at = slice(j * EP, (j + 1) * EP)
                    copy(wgt_hi[buf][:, at], mrawV[:, at]).then_inc(w_vh, 1)

            def load_tokens(i):
                act.dma_start(xin[:, :], xg[bass.ds(i * P, P), :]).then_inc(ld_xg, 16)

            def tokens_hi(i):
                wait(act, s_x, i + 1)
                load_tokens(i + 1)
                copy(xTh[:, :, :], psY[:, 0:D].rearrange("p (k n) -> p k n", k=KC)).then_inc(a_x, 1)

            def begin(e, buf, more):
                if more:
                    split_hi(e + 1, 1 - buf)

            def tile(i, buf):
                for h in range(2):
                    wait(act, m_up, 2 * i + h + 1)
                    nc.scalar.activation(relu_s[:, h, :], psS[h][:, :], ACT.Relu).then_inc(m_relu, 1)
                tokens_hi(i + 1)
                for h in range(2):
                    wait(act, s_g, 2 * i + h + 1)
                    copy(gTh[:, h, :], psG[h][:, :]).then_inc(m_gh, 1)
                wait(act, m_dn, i + 1)
                wait(act, st_y, 16 * i + 16)
                copy(ysb[:, :], psO[:, 0:D]).then_inc(a_y, 1)
                wait(act, a_y, i + 1)
                act.dma_start(yg[bass.ds(i * P, P), :], ysb[:, :]).then_inc(st_y, 16)

            split_hi(0, 0)
            act.wait_ge(st_xg, 16 * 2 * NT)
            load_tokens(0)
            tokens_hi(0)
            experts(act, begin, tile)
            act.wait_ge(ld_xg, 16 * (first_tile_of(act, NE) + 2))
            apart(act)

        @block.vector
        def _(dve):
            V = nc.vector
            reached = {}

            def link(ins, signal=v_seq):
                reached[signal.name] = reached.get(signal.name, 0) + 1
                ins.then_inc(signal, 1)
                dve.wait_ge(signal, reached[signal.name])

            link(V.memset(biasraw[:, :], 0.0), v_zero)
            link(V.memset(yN[:, :, :], 0.0), v_zero)
            link(V.memset(bias[:, :].bitcast(F32), 0.0))
            link(V.memset(pick[:, :].bitcast(F32), 0.0))
            link(V.memset(ones[:, :], 1.0))
            for row in (0, 32):
                link(V.tensor_copy(pick[row:row + 1, :], ones[row:row + 1, :]))
            dve.wait_ge(a_ec, 1)
            link(V.tensor_scalar(cD[:, :], cE[:, :], 1.0, None, ALU.add))
            link(V.reciprocal(cR[:, :], cD[:, :]))
            link(V.tensor_tensor(cD[:, :], cS[:, :], cR[:, :], ALU.mult))
            for n in range(KC * BATCH):
                link(V.tensor_scalar(cB[:, n, :], ones[:, :], cD[:, n:n + 1], None, ALU.mult), v_cb)
            dve.wait_ge(ld_k, 16 * N_CONST)
            link(V.tensor_copy(bias[0:33, :], biasraw[:, :]))
            link(V.tensor_tensor(bias[32:33, :], biasraw[32:33, :], bias[32:33, :], ALU.subtract))
            link(V.tensor_copy(gwh[:, :, :], graw[:, :, :]))
            link(V.tensor_tensor(gwl[:, :, :], graw[:, :, :], gwh[:, :, :], ALU.subtract), v_gate)
            for n in range(BATCH * 3):
                b, c = n // 3, n % 3
                dve.wait_ge(s_mod, n + 1)
                V.tensor_copy(modb[:, b, c * 512:(c + 1) * 512], psS[n % 2][:, :]).then_inc(v_mod, 1)
            dve.wait_ge(v_mod, 6)
            SA, CA, GA, SB, CB, GB = (modb[:, :, i * D:(i + 1) * D] for i in range(6))
            for m in (CA, CB):
                link(V.tensor_scalar(m, m, 1.0, None, ALU.add))
            for m in (GA, GB):
                link(V.tensor_scalar(gsign[:, :, :], m, 0.0, 2.0, ALU.is_ge, ALU.mult))
                link(V.tensor_scalar(gsign[:, :, :], gsign[:, :, :], 1.0, None, ALU.subtract))
                link(V.tensor_tensor(m, m, gsign[:, :, :], ALU.mult))
                link(V.scalar_tensor_tensor(m, m, 0.25, gsign[:, :, :], ALU.max, ALU.mult))

            def layer_norm(src, n):
                for t in range(NT):
                    V.bn_stats(stats[:, t, :], src[:, t, :]).then_inc(v_stat, 1)
                dve.wait_ge(v_stat, NT * (n + 1))
                for t in range(NT):
                    V.bn_aggr(mv[:, t, :], stats[:, t, :]).then_inc(v_aggr, 1)
                dve.wait_ge(v_aggr, NT * (n + 1))
                link(V.tensor_scalar(vare[:, :], mv[:, :, 1], EPS, None, ALU.add), v_var)

            def finish_roots(n):
                dve.wait_ge(a_root, n + 1)
                link(V.reciprocal(rs[:, :], sd[:, :]))

            def mean_square(src):
                for t in range(NT):
                    link(V.tensor_tensor_reduce(sq, src[:, t, :], src[:, t, :], 1.0 / D, 0.0, ALU.mult, ALU.add,
                                                vare[:, t:t + 1]))
                link(V.tensor_scalar(vare[:, :], vare[:, :], EPS, None, ALU.add), v_var)

            def modulate(dst, src, t, c, s):
                b = t // TB
                link(V.tensor_scalar(dst, src[:, t, :], mv[:, t, 0:1], rs[:, t:t + 1], ALU.subtract, ALU.mult))
                link(V.tensor_tensor(dst, dst, c[:, b, :], ALU.mult))
                return V.tensor_tensor(dst, dst, s[:, b, :], ALU.add)

            def features_lo(phase, t):
                n = NT * phase + t
                dve.wait_ge(a_hth, n + 1)
                V.tensor_tensor(hTl[:, :, t * P:(t + 1) * P], psX[t % 2][:, 0:D].rearrange("p (k n) -> p k n", k=KC),
                                hTh[:, :, t * P:(t + 1) * P], ALU.subtract).then_inc(v_htl, 1)

            def features(phase, make):
                for t in range(NT):
                    if phase < 2:
                        wait(dve, s_ht, NT * phase + t + 1 - 2)
                    make(t)
                    if t:
                        features_lo(phase, t - 1)
                features_lo(phase, NT - 1)

            def attention(L):
                def mask_max(g, s, j):
                    n = L.ntiles(s) * P
                    wait(dve, s_S, L.head(g, s, j))
                    if j == 0:
                        wait(dve, s_X, L.kt_all(g, s - 4))
                    apart(dve)
                    mask = mwin[:, 2 * P - n:] if L is LA else mcau[:, SEQ - n:]
                    V.tensor_tensor_reduce(probs[:, s % 4, j, 0:n], psS[j % 2][:, 0:n], mask, -SCALE, 3e38,
                                           ALU.add, ALU.min, nmax[:, s % 4, j:j + 1]).then_inc(v_max, 1)

                def normalise(g, s):
                    wait(dve, a_exp, L.head(g, s, QM - 1))
                    d = sums
                    if L is LA:
                        wait(dve, a_es, L.unit(g, s))
                        V.tensor_tensor(den[:, s % 4, :], sums[:, s % 4, :], esink[:, s % 4, :], ALU.add).then_inc(v_den, 1)
                        wait(dve, v_den, L.unit(g, s))
                        d = den
                    V.reciprocal(rden[:, s % 4, :], d[:, s % 4, :]).then_inc(v_rden, 1)
                    wait(dve, v_rden, L.unit(g, s))
                    n = L.ntiles(s) * P
                    for j in range(VH):
                        pj = probs[:, s % 4, j, 0:n]
                        last = V.tensor_scalar(pj, pj, rden[:, s % 4, j:j + 1], None, ALU.mult)
                    last.then_inc(v_norm, 1)

                def probs_lo(g, s, k):
                    slot = L.kt_slot(s, k)
                    wait(dve, a_ph, L.kt(g, s, k))
                    V.tensor_tensor(pTl[:, slot, :], psX[slot][:, :], pTh[:, slot, :], ALU.subtract).then_inc(v_pl, 1)

                def out_lo(g, s):
                    wait(dve, a_oh, L.unit(g, s))
                    V.tensor_tensor(ol[:, s % 2, :], psO[:, 0:2 * P], oh[:, s % 2, :], ALU.subtract).then_inc(v_ol, 1)

                def rotate(g, s):
                    wait(dve, s_proj, L.unit(g, s))
                    qkp = psP[:, 0:HQ + HD]
                    wait(dve, g_add, L.unit(g, s - 1))
                    t = s % TB
                    heads = qkp.rearrange("p (h d) -> p h d", d=HD)
                    V.tensor_tensor(t1[:, :, :], heads, cosw[:, t, :].unsqueeze(1).broadcast_to([P, QM + 1, HD]),
                                    ALU.mult)
                    halves = qkp.rearrange("p (h r d) -> p h r d", r=2, d=HD // 2)
                    t2h = t2[:, :, :].rearrange("p h (r d) -> p h r d", r=2)
                    sinr = sinw[:, t, :].rearrange("p (r d) -> p r d", r=2)
                    for r in range(2):
                        last = V.tensor_tensor(t2h[:, :, r, :], halves[:, :, 1 - r, :],
                                               sinr[:, r, :].unsqueeze(1).broadcast_to([P, QM + 1, HD // 2]), ALU.mult)
                    last.then_inc(v_rope, 1)

                def project_lo(g, s):
                    wait(dve, a_vh, L.unit(g, s))
                    if L is LB:
                        V.tensor_tensor(qn[:, s % 2, :, 1, :], psP[:, 0:HQ].rearrange("p (h d) -> p h d", d=HD),
                                        qn[:, s % 2, :, 0, :], ALU.subtract)
                        V.tensor_tensor(kn[:, s % 2, 1, :, :], psP[:, HQ:HQ + HD].unsqueeze(1).broadcast_to([P, 2, HD]),
                                        kn[:, s % 2, 0, :, :], ALU.subtract).then_inc(qk_lo, 1)
                    V.tensor_tensor(vpad[:, 1, s % NT, HD:2 * HD], psP[:, HQ + HD:QKV], vpad[:, 0, s % NT, HD:2 * HD],
                                    ALU.subtract).then_inc(v_vl, 1)

                def write_kT(g, s):
                    wait(dve, s_tk, L.unit(g, s))
                    wait(dve, s_S, L.head(g - 1, s % NT // TB * TB + TB - 1 + s // NT * NT, QM - 1))
                    V.tensor_copy(kT[:, :, s % NT * P:(s % NT + 1) * P], psT[:, 0:2 * P].rearrange("p (c n) -> p c n", c=2))\
                     .then_inc(v_tk, 1)

                def add_y(g, s):
                    wait(dve, s_Y, L.unit(g, s))
                    yt = yN[:, s % NT, :]
                    wait(dve, v_y, L.unit(g, s - 1))
                    V.tensor_tensor(yt, psY[:, 0:D], yt, ALU.add).then_inc(v_y, 1)

                def step_window(g, s):
                    now = exists(g, s)
                    back = exists(g, s - 1)
                    ahead = exists(g, s + 2)
                    nk = L.ntiles(s - 2) if exists(g, s - 2) else 0
                    if back:
                        normalise(g, s - 1)
                    if now:
                        mask_max(g, s, 0)
                        mask_max(g, s, 1)
                    if nk > 0:
                        probs_lo(g, s - 2, 0)
                    if ahead:
                        rotate(g, s + 2)
                    if now:
                        mask_max(g, s, 2)
                    if exists(g, s - 3):
                        out_lo(g, s - 3)
                    if now:
                        mask_max(g, s, 3)
                    if nk > 1:
                        probs_lo(g, s - 2, 1)
                    if exists(g, s - 4):
                        add_y(g, s - 4)
                    if ahead:
                        project_lo(g, s + 2)
                    if exists(g, s + 1):
                        write_kT(g, s + 1)

                def step_causal(g, s):
                    now = exists(g, s)
                    back = exists(g, s - 1)
                    ahead = exists(g, s + 2)
                    nk = L.ntiles(s - 2) if exists(g, s - 2) else 0
                    if now:
                        mask_max(g, s, 0)
                        mask_max(g, s, 1)
                    if back:
                        normalise(g, s - 1)
                    if nk > 0:
                        probs_lo(g, s - 2, 0)
                    if exists(g, s - 3):
                        out_lo(g, s - 3)
                    if nk > 1:
                        probs_lo(g, s - 2, 1)
                    if exists(g, s - 4):
                        add_y(g, s - 4)
                    if nk > 2:
                        probs_lo(g, s - 2, 2)
                    if now:
                        mask_max(g, s, 2)
                    if exists(g, s + 1):
                        write_kT(g, s + 1)
                    if nk > 3:
                        probs_lo(g, s - 2, 3)
                    if now:
                        mask_max(g, s, 3)
                    if ahead:
                        project_lo(g, s + 2)

                rounds(dve, step_window if L is LA else step_causal)

            dve.wait_ge(ld_x, 16)
            layer_norm(xN, 0)
            finish_roots(0)
            features(0, lambda t: modulate(hb[:, t % 2, :], xN, t, CA, SA).then_inc(v_h, 1))
            dve.wait_ge(st_zero, 16)
            dve.wait_ge(st_y, 16)
            attention(LA)

            dve.wait_ge(v_y, LA.unit(NKV - 1, NT - 1))
            link(V.tensor_tensor(yN[:, :, :], yN[:, :, :], outb_b[:, :].unsqueeze(1).broadcast_to([P, NT, D]), ALU.add))
            for b in range(BATCH):
                at = slice(b * TB, (b + 1) * TB)
                link(V.tensor_tensor(yN[:, at, :], yN[:, at, :], GA[:, b, :].unsqueeze(1).broadcast_to([P, TB, D]), ALU.mult))
            link(V.tensor_tensor(xN[:, :, :], xN[:, :, :], yN[:, :, :], ALU.add))
            link(V.memset(yN[:, :, :], 0.0))
            layer_norm(xN, 1)
            finish_roots(1)
            for t in range(NT):
                link(modulate(uN[:, t, :], xN, t, CB, SB))
            mean_square(uN)
            finish_roots(2)
            features(1, lambda t: V.scalar_tensor_tensor(hb[:, t % 2, :], uN[:, t, :], rs[:, t:t + 1], ln1_b[:, :],
                                                         ALU.mult, ALU.mult).then_inc(v_h, 1))
            attention(LB)

            dve.wait_ge(v_y, LB.unit(NKV - 1, NT - 1))
            link(V.tensor_tensor(uN[:, :, :], uN[:, :, :], yN[:, :, :], ALU.add))
            mean_square(uN)
            finish_roots(3)
            features(2, lambda t: V.scalar_tensor_tensor(hAll[:, t, :], uN[:, t, :], rs[:, t:t + 1], ln2_b[:, :],
                                                         ALU.mult, ALU.mult).then_inc(v_h, 1))

            dve.wait_ge(s_rt, NT)
            logits = psY[:, 0:NT * NE].rearrange("p (t e) -> p t e", e=NE)
            link(V.tensor_reduce(lmax[:, :], logits, mybir.AxisListType.X, ALU.max))
            link(V.tensor_scalar(lmax[:, :], lmax[:, :], -1.0, None, ALU.mult), v_lmax)
            dve.wait_ge(a_rt, NT)
            link(V.reciprocal(prr[:, :], prs[:, :]))
            link(V.tensor_tensor(pr[:, :, :], pr[:, :, :], prr[:, :].unsqueeze(2).broadcast_to([P, NT, NE]), ALU.mult))
            for t in range(NT):
                link(V.max(top[:, t, :], pr[:, t, :]))
                link(V.max_index(topi[:, t, :], top[:, t, :], pr[:, t, :]))
            link(V.tensor_copy(topf[:, :, :], topi[:, :, :]))
            link(V.tensor_tensor(tops[:, :], top[:, :, 0], top[:, :, 1], ALU.add))
            link(V.reciprocal(topr[:, :], tops[:, :]))
            link(V.tensor_tensor(topw[:, :, :], top[:, :, 0:2], topr[:, :].unsqueeze(2).broadcast_to([P, NT, 2]), ALU.mult))
            idb = ids[:, :].unsqueeze(1).broadcast_to([P, NT, NE])
            for i, c in ((0, c0), (1, c1)):
                link(V.tensor_tensor(c[:, :, :], idb, topf[:, :, i:i + 1].broadcast_to([P, NT, NE]), ALU.is_equal))
            link(V.tensor_tensor(picked[:, :, :], c0[:, :, :], c1[:, :, :], ALU.add), v_pick)

            link(V.memset(ahead[:, 0, :], 0.0))
            link(V.memset(base[:, 0:1], 0.0))
            link(V.memset(ntil[:, :], 1.0))
            dve.wait_ge(s_rank, 1)
            link(V.tensor_copy(total[:, :, :], psP[:, 0:NT * NE].rearrange("p (t e) -> p t e", e=NE)))
            for t in range(NT):
                link(V.tensor_tensor(ahead[:, t + 1, :], ahead[:, t, :], total[:, t, :], ALU.add))
            link(V.tensor_tensor(slotf[:, :, :], psO[:, 0:NT * NE].rearrange("p (t e) -> p t e", e=NE),
                                 ahead[:, 0:NT, :], ALU.add))
            for k in range(1, NT):
                link(V.scalar_tensor_tensor(ntil[:, :], ahead[:, NT, :], float(k * P), ntil[:, :], ALU.is_gt, ALU.add))
            for e in range(NE):
                link(V.tensor_tensor(base[:, e + 1:e + 2], base[:, e:e + 1], ntil[:, e:e + 1], ALU.add))
            link(V.tensor_copy(base_i[:, :], base[:, :]))
            link(V.scalar_tensor_tensor(slotf[:, :, :], base[:, 0:NE].unsqueeze(1).broadcast_to([P, NT, NE]), float(P),
                                        slotf[:, :, :], ALU.mult, ALU.add))
            for i, c in ((0, c0), (1, c1)):
                link(V.tensor_tensor(chosen[:, i, :, :], slotf[:, :, :], c[:, :, :], ALU.mult))
                link(V.tensor_reduce(slotr[:, i * NT:(i + 1) * NT], chosen[:, i, :, :], mybir.AxisListType.X, ALU.add))
            link(V.tensor_copy(slots[:, :], slotr[:, :]), v_slot)

            def split_lo(e, buf):
                for j in range(2):
                    at = slice(j * EP, (j + 1) * EP)
                    wait(dve, w_vh, 2 * e + j + 1)
                    V.tensor_tensor(wgt_lo[buf][:, at], mrawV[:, at], wgt_hi[buf][:, at], ALU.subtract).then_inc(w_vl, 1)

            def tokens_lo(i):
                wait(dve, a_x, i + 1)
                V.tensor_tensor(xTl[:, :, :], psY[:, 0:D].rearrange("p (k n) -> p k n", k=KC), xTh[:, :, :],
                                ALU.subtract).then_inc(v_x, 1)

            def begin(e, buf, more):
                if more:
                    split_lo(e + 1, 1 - buf)

            def tile(i, buf):
                for h in range(2):
                    wait(dve, m_relu, 2 * i + h + 1)
                    V.tensor_tensor(gated[:, h, :], psX[h][:, :], relu_s[:, h, :], ALU.mult).then_inc(m_g, 1)
                tokens_lo(i + 1)
                for h in range(2):
                    wait(dve, m_gh, 2 * i + h + 1)
                    V.tensor_tensor(gTl[:, h, :], psG[h][:, :], gTh[:, h, :], ALU.subtract).then_inc(m_gl, 1)

            split_lo(0, 0)
            tokens_lo(0)
            experts(dve, begin, tile)

            for b in range(BATCH):
                dve.wait_ge(ld_g[b], 16 * 2 * TB)
                at = slice(b * TB, (b + 1) * TB)
                for t in range(b * TB, (b + 1) * TB):
                    link(V.scalar_tensor_tensor(uN[:, t, :], hAll[:, t, :], topw[:, t, 0:1], uN[:, t, :], ALU.mult, ALU.add))
                    link(V.scalar_tensor_tensor(uN[:, t, :], second[:, t, :], topw[:, t, 1:2], uN[:, t, :], ALU.mult, ALU.add))
                link(V.tensor_tensor(uN[:, at, :], uN[:, at, :], GB[:, b, :].unsqueeze(1).broadcast_to([P, TB, D]), ALU.mult))
                V.tensor_tensor(xN[:, at, :], xN[:, at, :], uN[:, at, :], ALU.add).then_inc(v_out, 1)


def _tables():
    import math
    import numpy as np

    theta, scaling, alpha, beta, icl = 150000.0, 32.0, 1.0, 32.0, 128
    half = HD // 2
    freq = theta ** (np.arange(0, HD, 2, dtype=np.float32) / HD)
    concentration = 0.1 * math.log(scaling) + 1.0
    low = half * math.log(icl / (beta * 2 * math.pi)) / math.log(theta)
    high = half * math.log(icl / (alpha * 2 * math.pi)) / math.log(theta)
    ramp = np.clip((np.arange(half, dtype=np.float32) - low) / (high - low), 0.0, 1.0)
    keep = 1.0 - ramp
    inv_freq = 1.0 / (scaling * freq) * (1.0 - keep) + 1.0 / freq * keep
    freqs = np.outer(np.arange(SEQ, dtype=np.float32), inv_freq)
    cos = (np.cos(freqs) * concentration).astype(np.float32)
    sin = (np.sin(freqs) * concentration).astype(np.float32)
    by_tile = lambda a: np.ascontiguousarray(a.reshape(TB, P, HD).transpose(1, 0, 2))
    cosw = by_tile(np.concatenate([cos, cos], 1))
    sinw = by_tile(np.concatenate([-sin, sin], 1))
    i, j = np.arange(P)[:, None], np.arange(P)[None, :]
    causal = np.where(j > i, NEG, 0.0)
    before = np.where(j <= i, NEG, 0.0)
    mask_win = np.concatenate([before, causal], 1).astype(np.float32)
    mask_causal = np.concatenate([np.zeros((P, SEQ - P)), causal], 1).astype(np.float32)
    return {"rope_cos": cosw, "rope_sin": sinw, "mask_win": mask_win, "mask_causal": mask_causal,
            "ident": np.eye(P, dtype=np.float32), "expert_ids": np.arange(NE, dtype=np.float32),
            "before": np.triu(np.ones((P, P), np.float32), 1)}


def kernel(L0_attn_x, L0_attn_qkv_w, L0_attn_qkv_b, L0_attn_out_w, L0_attn_out_b, L0_attn_sinks,
           L0_ffn_ln1_w, L0_ffn_wq, L0_ffn_wk, L0_ffn_wv, L0_ffn_wo, L0_ffn_ln2_w, L0_ffn_gate_w,
           L0_ffn_w1, L0_ffn_w2, L0_ffn_w3, L0_c, L0_wmod):
    import numpy as np
    import concourse.bacc as bacc
    from concourse.bass_utils import run_bass_kernel_spmd

    arr = np.asarray

    def by_round(wq, wk, wv):
        a = np.concatenate([arr(wq).reshape(KC, P, NKV, HQ), arr(wk).reshape(KC, P, NKV, HD),
                            arr(wv).reshape(KC, P, NKV, HD)], 3)
        return a.transpose(2, 1, 0, 3).reshape(NKV, P, KC * QKV)

    def out_by_round(wo):
        return arr(wo).reshape(NKV, 2, P, D).transpose(0, 2, 1, 3).reshape(NKV, P, 2 * D)

    nq, nk = NKV * HQ, NKV * HD
    wt = arr(L0_attn_qkv_w).T
    b = arr(L0_attn_qkv_b)
    bias = np.concatenate([b[:nq].reshape(NKV, HQ), b[nq:nq + nk].reshape(NKV, HD), b[nq + nk:].reshape(NKV, HD)], 1)
    by_rows = lambda w: arr(w).reshape(NE, -1, P, arr(w).shape[2]).transpose(0, 2, 1, 3).reshape(NE, P, -1)
    w_moe = np.concatenate([by_rows(L0_ffn_w1), by_rows(L0_ffn_w3), by_rows(L0_ffn_w2)], 2)
    tables = _tables()
    ins = {
        "x": arr(L0_attn_x),
        "w_attn": by_round(wt[:, :nq], wt[:, nq:nq + nk], wt[:, nq + nk:]),
        "wo_attn": out_by_round(arr(L0_attn_out_w).T),
        "b_attn": bias.reshape(-1),
        "outb": arr(L0_attn_out_b),
        "sinks": arr(L0_attn_sinks),
        "w_ffn": by_round(L0_ffn_wq, L0_ffn_wk, L0_ffn_wv),
        "wo_ffn": out_by_round(L0_ffn_wo),
        "ln1": arr(L0_ffn_ln1_w),
        "ln2": arr(L0_ffn_ln2_w),
        "gate": arr(L0_ffn_gate_w).reshape(KC, P, NE).transpose(1, 0, 2),
        "w_moe": w_moe,
        "cT": arr(L0_c).T.reshape(KC, P, BATCH).transpose(1, 0, 2).reshape(P, KC * BATCH),
        "wmod": arr(L0_wmod).reshape(KC, P, NMOD).transpose(1, 0, 2),
    }
    ins.update({k: tables[k] for k in ("rope_cos", "rope_sin", "mask_win", "mask_causal", "ident", "expert_ids",
                                     "before")})
    nc = bacc.Bacc("TRN2", target_bir_lowering=False, num_devices=1)
    arrays, args = {}, []
    for name, a in ins.items():
        arrays[f"in_{name}"] = np.ascontiguousarray(a)
        args.append(nc.dram_tensor(f"in_{name}", a.shape, mybir.dt.from_np(a.dtype), kind="ExternalInput").ap())
    for name in ("xg", "yg"):
        args.append(nc.dram_tensor(name, ((MAXT + 2) * P, D), F32, kind="Internal").ap())
    args.append(nc.dram_tensor("out_x", (BATCH, SEQ, D), F32, kind="ExternalOutput").ap())
    build(nc, *args)
    r = run_bass_kernel_spmd(nc, [arrays], core_ids=[0])
    return r.results[0]["out_x"]
```

```python
from contextlib import ExitStack

import concourse.bass as bass
from concourse import mybir

F32 = mybir.dt.float32
F32R = mybir.dt.float32r
U32 = mybir.dt.uint32
I32 = mybir.dt.int32
ALU = mybir.AluOpType
ACT = mybir.ActivationFunctionType

P = 128
BATCH, SEQ, D = 2, 512, 256
NT = BATCH * SEQ // P
TB = SEQ // P
KC = D // P
HD = 64
NKV, QM = 8, 4
HQ = QM * HD
QKV = HQ + 2 * HD
NE, FF = 8, 1024
NF = FF // P
EW = 2 * KC * FF + NF * D
EV = EW // 2
EP = EW // 4
MAXT = 2 * NT + NE - 1
SCALE = HD ** -0.5
NEG = -1e30
EPS = 1e-5
NMOD = 6 * D


class Layer:

    def __init__(self, window, unit_base, kt_base, by_vector):
        self.window = window
        self.by_vector = by_vector
        self.unit_base, self.kt_base = unit_base, kt_base
        self.keys = [min(t + 1, 2) if window else t + 1 for t in range(TB)]
        self.kt_round = sum(self.keys) * BATCH

    def ntiles(self, s):
        return self.keys[s % TB]

    def first_tile(self, s):
        s %= NT
        return s - self.ntiles(s) + 1

    def unit(self, g, s):
        return self.unit_base + NT * g + s + 1

    def head(self, g, s, j):
        return QM * (self.unit(g, s) - 1) + j + 1

    def kt(self, g, s, k):
        before = sum(self.keys[i % TB] for i in range(s % NT)) + s // NT * self.kt_round
        return self.kt_base + self.kt_round * g + before + k + 1

    def kt_all(self, g, s):
        return self.kt(g, s + 1, -1)

    def kt_slot(self, s, k):
        return (sum(self.keys[i % TB] for i in range(s % NT)) + k) % 2


def exists(g, s):
    return not isinstance(g, int) or 0 <= NT * g + s < NT * NKV


def wait(eng, sem, value):
    if not isinstance(value, int) or value > 0:
        eng.wait_ge(sem, value)


def rounds(eng, step):
    for s in range(-2, NT):
        step(0, s)
    with eng.Fori(1, NKV - 1) as g:
        for s in range(NT):
            step(g, s)
    for s in range(NT + 5):
        step(NKV - 1, s)


def build(nc, x, w_attn, wo_attn, b_attn, outb, sinks, w_ffn, wo_ffn, ln1, ln2, gate, w_moe,
          cT, wmod, rope_cos, rope_sin, mask_win, mask_causal, ident, expert_ids, before, xg, yg, out):
    LA, LB = Layer(True, 0, 0, 3), Layer(False, NT * NKV, 0, 3)
    LB.kt_base = LA.kt_round * NKV
    ctx = ExitStack()
    with ctx:
        def sb(name, shape, dt=F32):
            return ctx.enter_context(nc.sbuf_tensor(name, shape, dt))

        of_attention = ExitStack()

        def sb_att(name, shape, dt=F32):
            return of_attention.enter_context(nc.sbuf_tensor(name, shape, dt))

        def sem(name):
            return ctx.enter_context(nc.semaphore(name))

        N_CONST = 12
        idn = sb("idn", [P, P])
        sink_b = sb("sink_b", [P, NKV * QM])
        outb_b = sb("outb_b", [P, D])
        ln1_b = sb("ln1_b", [P, D])
        ln2_b = sb("ln2_b", [P, D])
        ids = sb("ids", [P, NE])
        modb = sb("modb", [P, BATCH, NMOD])
        xN = sb("xN", [P, NT, D])
        uN = sb("uN", [P, NT, D])
        yN = sb("yN", [P, NT, D])
        hb = sb("hb", [P, 2, D])
        hTh = sb("hTh", [P, KC, NT * P], F32R)
        hTl = sb("hTl", [P, KC, NT * P], F32R)
        pick = sb("pick", [33, P], F32R)
        t1 = sb("t1", [P, QM + 1, HD])
        mrawV = sb("mrawV", [P, EV])
        biasraw = mrawV[0:33, 0:NKV * QKV]
        nmax = sb("nmax", [P, 4, QM])
        sums = sb("sums", [P, 4, QM])
        esin = sb("esin", [P, 4, QM])
        esink = sb("esink", [P, 4, QM])
        den = sb("den", [P, 4, QM])
        rden = sb("rden", [P, 4, QM])
        cS = sb("cS", [P, KC * BATCH])
        cE = sb("cE", [P, KC * BATCH])
        cD = sb("cD", [P, KC * BATCH])
        cR = sb("cR", [P, KC * BATCH])
        ones = sb("ones", [P, P])
        cB = sb("cB", [P, KC * BATCH, P])
        stats = sb("stats", [P, NT, 6])
        mv = sb("mv", [P, NT, 2])
        vare = sb("vare", [P, NT])
        ssq = sb("ssq", [P, NT])
        sd = sb("sd", [P, NT])
        rs = sb("rs", [P, NT])
        graw = sb("graw", [P, KC, NE])
        gw = sb("gw", [P, KC, 2 * NE], F32R)

        mwin = sb_att("mwin", [P, 2 * P])
        mcau = sb_att("mcau", [P, SEQ])
        cosw = sb_att("cosw", [P, TB, HD])
        sinw = sb_att("sinw", [P, TB, HD])
        wraw = sb_att("wraw", [P, KC * QKV])
        woraw = sb_att("woraw", [P, 2 * D])
        bias = sb_att("bias", [33, NKV * QKV], F32R)
        t2 = sb_att("t2", [P, QM + 1, HD])
        qk = sb_att("qk", [P, QM + 1, HD])
        qn = sb_att("qn", [P, 2, QM, 2, HD], F32R)
        kn = sb_att("kn", [P, 2, 2, 2, HD], F32R)
        wbufs = sb_att("wbufs", [P, 4 * KC * QKV], F32R)
        wh = wbufs[:, 0:2 * KC * QKV]
        wl = wbufs[:, 2 * KC * QKV:]
        woh = sb_att("woh", [P, 2 * 2 * D], F32R)
        wol = sb_att("wol", [P, 2 * 2 * D], F32R)
        bufA = sb_att("bufA", [P, EW], F32R)
        bufB = sb_att("bufB", [P, EW], F32R)
        qT = bufA[:, 0:NT * QM * P].rearrange("p (t n) -> p t n", t=NT)
        kT = bufA[:, NT * QM * P:].rearrange("p (c n) -> p c n", c=2)
        o = 0
        vpad = bufB[:, 0:2 * NT * 3 * HD].rearrange("p (c t n) -> p c t n", c=2, t=NT)
        o = 2 * NT * 3 * HD
        pTh = bufB[:, o:o + 2 * QM * P].rearrange("p (c n) -> p c n", c=2)
        o += 2 * QM * P
        pTl = bufB[:, o:o + 2 * QM * P].rearrange("p (c n) -> p c n", c=2)
        o += 2 * QM * P
        oh = bufB[:, o:o + 2 * 2 * P].rearrange("p (c n) -> p c n", c=2)
        o += 2 * 2 * P
        ol = bufB[:, o:o + 2 * 2 * P].rearrange("p (c n) -> p c n", c=2)
        pbuf = sb_att("pbuf", [P, 4 * QM * SEQ])
        probs = pbuf[:, :].rearrange("p (c h n) -> p c h n", c=4, h=QM)
        wmod_s = pbuf[:, 0:KC * NMOD].rearrange("p (k n) -> p k n", k=KC)
        of_attention.close()

        lmax = sb("lmax", [P, NT])
        logit = sb("logit", [P, NT, NE])
        pr = sb("pr", [P, NT, NE])
        prs = sb("prs", [P, NT])
        prr = sb("prr", [P, NT])
        top = sb("top", [P, NT, 8])
        topi = sb("topi", [P, NT, 8], U32)
        topf = sb("topf", [P, NT, 8])
        tops = sb("tops", [P, NT])
        topr = sb("topr", [P, NT])
        topw = sb("topw", [P, NT, 2])
        c0 = sb("c0", [P, NT, NE])
        c1 = sb("c1", [P, NT, NE])
        picked = sb("picked", [P, NT, NE])
        before_s = sb("before_s", [P, P])
        total = sb("total", [P, NT, NE])
        ahead = sb("ahead", [P, NT + 1, NE])
        slotf = sb("slotf", [P, NT, NE])
        chosen = sb("chosen", [P, 2, NT, NE])
        slotr = sb("slotr", [P, 2 * NT])
        slots = sb("slots", [P, 2 * NT], U32)
        slots_out = sb("slots_out", [P, 2 * NT], U32)
        order = sb("order", [P, 2, NT])
        share = sb("share", [P, 2, NT])
        bound = sb("bound", [P, NT])
        above = sb("above", [P, NE, NT])
        ntil = sb("ntil", [P, NE])
        base = sb("base", [P, NE + 1])
        base_i = sb("base_i", [P, NE + 1], I32)
        wgt_hi = [sb(f"wgt_hi{i}", [P, EW], F32R) for i in range(2)]
        wgt_lo = [sb(f"wgt_lo{i}", [P, EW], F32R) for i in range(2)]
        mrawP = sb("mrawP", [P, 2, EP])
        hAll = sb("hAll", [P, NT, D])
        second = uN
        xin = sb("xin", [P, D])
        gTh, gTl = (a[:, 0, :].rearrange("p (h n) -> p h n", h=2) for a in (hTh, hTl))
        xTh, xTl = (a[:, 1, 0:KC * P].rearrange("p (k n) -> p k n", k=KC) for a in (hTh, hTl))
        relu_s = sb("relu_s", [P, 2, FF // 2])
        gated = sb("gated", [P, 2, FF // 2])
        ysb = sb("ysb", [P, D])

        def bank(name):
            return ctx.enter_context(nc.psum_tensor(name, [P, 512], F32))

        psS = [bank("psS0"), bank("psS1")]
        psX = [bank("psX0"), bank("psX1")]
        psO = bank("psO")
        psP = bank("psP")
        psT = bank("psT")
        psY = bank("psY")
        psG = [psP, psT]

        ld_c = sem("ld_c")
        ld_x = sem("ld_x")
        ld_k = sem("ld_k")
        ld_w = sem("ld_w")
        ld_wo = sem("ld_wo")
        ld_v = sem("ld_v")
        ld_p = [sem("ld_p0"), sem("ld_p1")]
        ld_xg = sem("ld_xg")
        ld_g = [[sem(f"ld_g{i}_{t}") for t in range(NT)] for i in range(2)]
        ld_before = sem("ld_before")
        st_zero = sem("st_zero")
        st_xg = sem("st_xg")
        st_y = sem("st_y")
        st_out = sem("st_out")
        v_seq = sem("v_seq")
        a_sq = sem("a_sq")
        v_u = sem("v_u")
        a_bias = sem("a_bias")
        a_yi = sem("a_yi")
        g_seq = sem("g_seq")
        g_zero = sem("g_zero")
        g_x = sem("g_x")
        v_cb = sem("v_cb")
        v_mod = sem("v_mod")
        v_gate = sem("v_gate")
        v_stat = sem("v_stat")
        v_aggr = sem("v_aggr")
        v_var = sem("v_var")
        v_lmax = sem("v_lmax")
        v_out = sem("v_out")
        a_ec = sem("a_ec")
        a_root = sem("a_root")
        a_rt = sem("a_rt")
        p_init = sem("p_init")
        s_mod = sem("s_mod")
        s_ht = sem("s_ht")
        v_h = sem("v_h")
        a_hth = sem("a_hth")
        v_htl = sem("v_htl")
        g_hi = sem("g_hi")
        g_w = sem("g_w")
        s_proj = sem("s_proj")
        v_rope = sem("v_rope")
        g_add = sem("g_add")
        g_qh = sem("g_qh")
        qk_lo = sem("qk_lo")
        a_qh = sem("a_qh")
        a_vh = sem("a_vh")
        v_vl = sem("v_vl")
        s_tq = sem("s_tq")
        s_tk = sem("s_tk")
        a_tq = sem("a_tq")
        v_tk = sem("v_tk")
        s_S = sem("s_S")
        v_max = sem("v_max")
        a_exp = sem("a_exp")
        g_es = sem("g_es")
        a_es = sem("a_es")
        v_den = sem("v_den")
        v_rden = sem("v_rden")
        v_norm = sem("v_norm")
        a_norm = sem("a_norm")
        s_X = sem("s_X")
        a_ph = sem("a_ph")
        v_pl = sem("v_pl")
        s_PV = sem("s_PV")
        a_oh = sem("a_oh")
        v_ol = sem("v_ol")
        s_Y = sem("s_Y")
        v_y = sem("v_y")
        s_rt = sem("s_rt")
        v_pick = sem("v_pick")
        s_rank = sem("s_rank")
        v_slot = sem("v_slot")
        w_vh = sem("w_vh")
        w_vl = sem("w_vl")
        w_ph = sem("w_ph")
        w_pl = sem("w_pl")
        s_x = sem("s_x")
        a_x = sem("a_x")
        v_x = sem("v_x")
        m_up = sem("m_up")
        m_gate = sem("m_gate")
        m_relu = sem("m_relu")
        m_g = sem("m_g")
        s_g = sem("s_g")
        m_gh = sem("m_gh")
        m_gl = sem("m_gl")
        m_dn = sem("m_dn")
        a_y = sem("a_y")

        block = ctx.enter_context(nc.Block())

        def apart(eng):
            eng.nop(nofuse=True)

        def first_tile_of(eng, e):
            return eng.value_load(base_i[0:1, bass.ds(e, 1)], min_val=0, max_val=MAXT)

        def experts(eng, begin, tile):
            def pair(m, more):
                for buf in range(2):
                    e = 2 * m + buf
                    begin(e, buf, buf == 0 or more)
                    if tile:
                        with eng.Fori(first_tile_of(eng, e), first_tile_of(eng, e + 1)) as i:
                            tile(i, buf)

            with eng.Fori(0, NE // 2 - 1) as m:
                pair(m, True)
            pair(NE // 2 - 1, False)

        def parity(g):
            return g % 2

        @block.sync
        def _(sp):
            sp.dma_start(cS[:, :], cT).then_inc(ld_c, 16)
            sp.dma_start(wmod_s, wmod).then_inc(ld_c, 16)
            sp.dma_start(xN[:, :, :], x.rearrange("b (t p) d -> p (b t) d", p=P)).then_inc(ld_x, 16)
            sp.dma_start(wraw[:, :], w_attn[0]).then_inc(ld_w, 16)
            sp.dma_start(woraw[:, :], wo_attn[0]).then_inc(ld_wo, 16)
            for dst, src in ((idn, ident), (mwin, mask_win), (mcau, mask_causal)):
                sp.dma_start(dst[:, :], src).then_inc(ld_k, 16)
            for dst, src in ((cosw, rope_cos), (sinw, rope_sin), (graw, gate)):
                sp.dma_start(dst[:, :, :], src).then_inc(ld_k, 16)
            for dst, src in ((sink_b, sinks), (outb_b, outb), (ln1_b, ln1), (ln2_b, ln2), (ids, expert_ids)):
                sp.dma_start(dst[:, :], src.partition_broadcast(P)).then_inc(ld_k, 16)
            sp.dma_start(biasraw, b_attn.partition_broadcast(33)).then_inc(ld_k, 16)

            for n, (w_d, wo_d) in enumerate(((w_attn, wo_attn), (w_ffn, wo_ffn))):
                def load_round(g):
                    done = 3 * (NKV * n + g)
                    wait(sp, g_w, done)
                    sp.dma_start(wraw[:, :], w_d[bass.ds(g, 1)].rearrange("o p n -> (o p) n")).then_inc(ld_w, 16)
                    sp.dma_start(woraw[:, :], wo_d[bass.ds(g, 1)].rearrange("o p n -> (o p) n")).then_inc(ld_wo, 16)

                if n > 0:
                    load_round(0)
                else:
                    sp.wait_ge(g_zero, 1)
                    for rows, signal in ((xg, st_zero), (yg, st_y)):
                        sp.dma_start(rows.rearrange("(t p) d -> p t d", p=P),
                                     uN[:, 0:1, :].broadcast_to([P, MAXT + 2, D])).then_inc(signal, 16)
                with sp.Fori(1, NKV) as g:
                    load_round(g)

            def load_expert(e):
                rows = w_moe[bass.ds(e, 1)].rearrange("o p n -> (o p) n")
                wait(sp, w_vl, 2 * e)
                sp.dma_start(mrawV[:, :], rows[:, 0:EV]).then_inc(ld_v, 16)
                for j in range(2):
                    if isinstance(e, int) and e == 0:
                        sp.wait_ge(v_h, 2 * NT + 1)
                    wait(sp, w_pl, 2 if isinstance(e, int) and e == 1 else 2 * e - 1 + j)
                    sp.dma_start(mrawP[:, j, :], rows[:, EV + j * EP:EV + (j + 1) * EP]).then_inc(ld_p[j], 16)

            sp.wait_ge(v_gate, 1)
            load_expert(0)
            sp.dma_start(before_s[:, :], before).then_inc(ld_before, 16)
            load_expert(1)
            with sp.Fori(2, NE) as e:
                load_expert(e)
            for t in range(NT):
                sp.wait_ge(v_out, t + 1)
                sp.dma_start(out[t // TB, t % TB * P:(t % TB + 1) * P, :], xN[:, t, :]).then_inc(st_out, 16)
            sp.wait_ge(st_out, 16 * NT)

        @block.gpsimd
        def _(pool):
            G = nc.gpsimd
            GA, GB = modb[:, :, 2 * D:3 * D], modb[:, :, 5 * D:6 * D]
            gsign = cB[:, :, :].rearrange("p n q -> p (n q)").rearrange("p (b d) -> p b d", b=BATCH)
            done = [0]

            def link(ins):
                done[0] += 1
                ins.then_inc(g_seq, 1)
                pool.wait_ge(g_seq, done[0])

            def gate_rows(m):
                link(G.tensor_scalar(gsign, m, 0.0, 2.0, ALU.is_ge, ALU.mult))
                link(G.tensor_scalar(gsign, gsign, 1.0, None, ALU.subtract))
                link(G.tensor_tensor(m, m, gsign, ALU.mult))
                link(G.tensor_scalar(m, m, 0.25, None, ALU.max))
                link(G.tensor_tensor(m, m, gsign, ALU.mult))

            G.memset(uN[:, 0, :], 0.0).then_inc(g_zero, 1)
            G.memset(bufB[:, 0:2 * NT * 3 * HD].bitcast(F32), 0.0).then_inc(p_init, 1)

            for L in (LA, LB):
                n = 0 if L is LA else 1

                def split_piece(g, piece, L=L, n=n):
                    r = NKV * n + g
                    if piece < 2:
                        wait(pool, ld_w, 16 * (r + 1))
                        wait(pool, s_proj, L.unit(g - 2, NT - 1))
                        at = parity(g) * (KC * QKV) + piece * QKV
                        hi, lo, raw = wh[:, bass.ds(at, QKV)], wl[:, bass.ds(at, QKV)], wraw[:, piece * QKV:(piece + 1) * QKV]
                    else:
                        wait(pool, ld_wo, 16 * (r + 1))
                        wait(pool, s_Y, L.unit(g - 2, NT - 1))
                        at = parity(g) * 2 * D
                        hi, lo, raw = woh[:, bass.ds(at, 2 * D)], wol[:, bass.ds(at, 2 * D)], woraw[:, :]
                    apart(pool)
                    nc.gpsimd.tensor_copy(hi, raw).then_inc(g_hi, 1)
                    wait(pool, g_hi, 3 * r + piece + 1)
                    apart(pool)
                    nc.gpsimd.tensor_tensor(lo, raw, hi, ALU.subtract).then_inc(g_w, 1)

                def step(g, s, L=L):
                    if L is LA and exists(g, s):
                        wait(pool, v_max, L.head(g, s, QM - 1))
                        wait(pool, a_es, L.unit(g, s - 4))
                        apart(pool)
                        nc.gpsimd.tensor_tensor(esin[:, s % 4, :], sink_b[:, bass.ds(g * QM, QM)],
                                                nmax[:, s % 4, :], ALU.add).then_inc(g_es, 1)
                    if L is LA and exists(g, s + 2):
                        wait(pool, v_rope, L.unit(g, s + 2))
                        wait(pool, qk_lo, L.unit(g, s + 1))
                        nc.gpsimd.tensor_tensor(qk[:, :, :], t1[:, :, :], t2[:, :, :], ALU.add).then_inc(g_add, 1)
                        wait(pool, g_add, L.unit(g, s + 2))
                        wait(pool, s_tk, L.unit(g, s))
                        k2 = qk[:, QM, :].unsqueeze(1).broadcast_to([P, 2, HD])
                        apart(pool)
                        nc.gpsimd.tensor_copy(qn[:, s % 2, :, 0, :], qk[:, 0:QM, :])
                        nc.gpsimd.tensor_copy(kn[:, s % 2, 0, :, :], k2).then_inc(g_qh, 1)
                        wait(pool, g_qh, L.unit(g, s + 2))
                        nc.gpsimd.tensor_tensor(qn[:, s % 2, :, 1, :], qk[:, 0:QM, :], qn[:, s % 2, :, 0, :],
                                                ALU.subtract)
                        nc.gpsimd.tensor_tensor(kn[:, s % 2, 1, :, :], k2, kn[:, s % 2, 0, :, :],
                                                ALU.subtract).then_inc(qk_lo, 1)
                    if s in (0, 1, 2) and exists(g, NT):
                        split_piece(g + 1, s)

                for piece in range(3):
                    split_piece(0, piece)
                pool.wait_ge(v_mod, 2 * BATCH if L is LA else 3 * BATCH)
                pool.wait_ge(s_mod, 3 * BATCH)
                gate_rows(GA if L is LA else GB)
                rounds(pool, step)
                if L is LA:
                    for t in range(NT):
                        pool.wait_ge(v_y, LA.unit(NKV - 1, t))
                        link(G.tensor_tensor(yN[:, t, :], yN[:, t, :], GA[:, t // TB, :], ALU.mult))
                        G.tensor_tensor(xN[:, t, :], xN[:, t, :], yN[:, t, :], ALU.add).then_inc(g_x, 1)

            def split_expert(e, buf, used):
                wait(pool, m_dn, used + 1)
                for j in range(2):
                    at = slice(EV + j * EP, EV + (j + 1) * EP)
                    wait(pool, ld_p[j], 16 * (e + 1))
                    apart(pool)
                    nc.gpsimd.tensor_copy(wgt_hi[buf][:, at], mrawP[:, j, :]).then_inc(w_ph, 1)
                    wait(pool, w_ph, 2 * e + j + 1)
                    apart(pool)
                    nc.gpsimd.tensor_tensor(wgt_lo[buf][:, at], mrawP[:, j, :], wgt_hi[buf][:, at], ALU.subtract)\
                      .then_inc(w_pl, 1)

            pool.wait_ge(v_slot, 1)
            pool.wait_ge(st_zero, 16)
            for t in range(NT):
                for i in range(2):
                    n = i * NT + t
                    nc.gpsimd.indirect_dma_start(xg[:, :], bass.IndirectOffsetOnAxis(ap=slots[:, n:n + 1], axis=0),
                                                 hAll[:, t, :], None).then_inc(st_xg, 16)

            def begin(e, buf, more):
                if more:
                    split_expert(e + 1, 1 - buf, first_tile_of(pool, e))

            experts(pool, begin, None)

            pool.wait_ge(v_slot, 2)
            for i, dst in ((0, hAll), (1, second)):
                pool.wait_ge(st_y, 16 * first_tile_of(pool, NE - 1 + i) + 32)
                apart(pool)
                for t in range(NT):
                    n = i * NT + t
                    nc.gpsimd.indirect_dma_start(dst[:, t, :], None, yg[:, :],
                                                 bass.IndirectOffsetOnAxis(ap=slots_out[:, n:n + 1], axis=0))\
                      .then_inc(ld_g[i][t], 16)

        @block.tensor
        def _(pe):
            mm = nc.tensor.matmul

            pe.wait_ge(v_cb, KC * BATCH)
            pe.wait_ge(ld_c, 32)
            for n in range(BATCH * 3):
                c, b = n // BATCH, n % BATCH
                wait(pe, v_mod, n - 1)
                for k in range(KC):
                    last = mm(psS[n % 2][:, :], cB[:, k * BATCH + b, :], wmod_s[:, k, c * 512:(c + 1) * 512],
                              start=(k == 0), stop=(k == KC - 1))
                last.then_inc(s_mod, 1)

            def to_features(phase, behind=None):
                for t in range(NT):
                    n = NT * phase + t
                    pe.wait_ge(v_h, n + 1)
                    if phase == 0 and t == 0:
                        pe.wait_ge(ld_k, 16 * N_CONST)
                    src = hAll[:, t, :] if phase == 2 else hb[:, t % 2, :]
                    wait(pe, v_htl, n + 1 - 2)
                    for k in range(KC):
                        last = nc.tensor.transpose(psX[t % 2][:, k * P:(k + 1) * P], src[:, k * P:(k + 1) * P],
                                                   idn[:, :])
                    last.then_inc(s_ht, 1)
                    if behind and t >= 2:
                        behind(t - 2)

            def attention(L, phase):
                def scores(g, s, j):
                    wait(pe, v_max, L.head(g, s, j) - 2)
                    if j == 0:
                        wait(pe, a_tq, L.unit(g, s))
                        wait(pe, v_tk, L.unit(g, s))
                    n = L.ntiles(s) * P
                    k0 = L.first_tile(s) * P
                    for c in range(2):
                        last = mm(psS[j % 2][:, 0:n], qT[:, s % NT, j * P:(j + 1) * P], kT[:, c, k0:k0 + n],
                                  start=(c == 0), stop=(c == 1))
                    last.then_inc(s_S, 1)

                def turn_probs(g, s, k):
                    if k == 0:
                        wait(pe, v_norm, L.unit(g, s))
                        wait(pe, a_norm, L.unit(g, s))
                    slot = L.kt_slot(s, k)
                    wait(pe, v_pl, L.kt(g, s, k) - 2)
                    for j in range(QM):
                        last = nc.tensor.transpose(psX[slot][:, j * P:(j + 1) * P],
                                                   probs[:, s % 4, j, k * P:(k + 1) * P], idn[:, :])
                    last.then_inc(s_X, 1)

                def values(g, s, k):
                    slot = L.kt_slot(s, k)
                    if k == 0:
                        wait(pe, v_ol, L.unit(g, s - 1))
                        wait(pe, v_vl, L.unit(g, s))
                    wait(pe, v_pl, L.kt(g, s, k))
                    kv = L.first_tile(s) + k
                    pairs = lambda p: p[:, slot, :].rearrange("p (i r q) -> p r i q", r=2, q=P)
                    n = 0
                    for v, pT in ((0, pTh), (1, pTh), (0, pTl)):
                        for r in range(2):
                            lhsT = vpad[:, v, kv, HD:3 * HD] if r == 0 else vpad[:, v, kv, 0:2 * HD]
                            last = mm(psO[:, 0:2 * P], lhsT, pairs(pT)[:, r],
                                      start=(k == 0 and n == 0), stop=(k == L.ntiles(s) - 1 and n == 5))
                            n += 1
                    last.then_inc(s_PV, 1)

                def project(g, s):
                    r = 0 if L is LA else NKV
                    wait(pe, v_vl, L.unit(g, s - 1))
                    if s % NT == 0:
                        g2 = g + s // NT
                        wait(pe, g_w, 3 * (r + g2) + 2)
                    if isinstance(g, int) and g == 0 and 0 <= s < NT:
                        pe.wait_ge(v_htl, NT * phase + s + 1)
                    at = parity(g + s // NT) * (KC * QKV)
                    t = s % NT
                    n = 0
                    for k in range(KC):
                        for a, w in ((hTh, wh), (hTl, wh), (hTh, wl)):
                            n += 1
                            last = mm(psP[:, 0:QKV], a[:, k, t * P:(t + 1) * P], w[:, bass.ds(at + k * QKV, QKV)],
                                      start=(n == 1), stop=(n == 3 * KC and L is LB))
                    if L is LA:
                        last = mm(psP[:, 0:QKV], pick[:, :], bias[:, bass.ds((g + s // NT) * QKV, QKV)],
                                  start=False, stop=True)
                    last.then_inc(s_proj, 1)

                def turn_q(g, s):
                    wait(pe, qk_lo, L.unit(g, s))
                    wait(pe, v_tk, L.unit(g, s - 1))
                    for j in range(QM):
                        last = nc.tensor.transpose(psT[:, j * P:(j + 1) * P],
                                                   qn[:, s % 2, j, :, :].rearrange("p c d -> p (c d)").bitcast(F32),
                                                   idn[:, :])
                    last.then_inc(s_tq, 1)

                def turn_k(g, s):
                    wait(pe, a_tq, L.unit(g, s))
                    for c in range(2):
                        kk = kn[:, s % 2, c, :, :].rearrange("p r d -> p (r d)").bitcast(F32)
                        last = nc.tensor.transpose(psT[:, c * P:(c + 1) * P], kk, idn[:, :])
                    last.then_inc(s_tk, 1)

                def out_project(g, s):
                    r = 0 if L is LA else NKV
                    wait(pe, v_ol, L.unit(g, s))
                    wait(pe, v_y, L.unit(g, s - 1))
                    g2 = g + s // NT
                    if s % NT == 0:
                        wait(pe, g_w, 3 * (r + g2) + 3)
                    at = parity(g2) * 2 * D
                    n = 0
                    for i in range(2):
                        for a, w in ((oh, woh), (ol, woh), (oh, wol)):
                            n += 1
                            last = mm(psY[:, 0:D], a[:, s % 2, i * P:(i + 1) * P], w[:, bass.ds(at + i * D, D)],
                                      start=(n == 1), stop=(n == 6))
                    last.then_inc(s_Y, 1)

                def step_window(g, s):
                    now = exists(g, s)
                    ahead = exists(g, s + 2)
                    nk = L.ntiles(s - 2) if exists(g, s - 2) else 0
                    if nk > 0:
                        turn_probs(g, s - 2, 0)
                    if exists(g, s - 3):
                        values(g, s - 3, L.ntiles(s - 3) - 1)
                    if now:
                        scores(g, s, 0)
                        scores(g, s, 1)
                    if ahead:
                        project(g, s + 2)
                    if nk > 1:
                        turn_probs(g, s - 2, 1)
                    if exists(g, s - 4):
                        out_project(g, s - 4)
                    if now:
                        scores(g, s, 2)
                        scores(g, s, 3)
                    if exists(g, s + 1):
                        turn_q(g, s + 1)
                    if nk > 1:
                        values(g, s - 2, 0)
                    if exists(g, s + 1):
                        turn_k(g, s + 1)

                def step_causal(g, s):
                    now = exists(g, s)
                    ahead = exists(g, s + 2)
                    nk = L.ntiles(s - 2) if exists(g, s - 2) else 0
                    if now:
                        scores(g, s, 0)
                    if nk > 0:
                        turn_probs(g, s - 2, 0)
                    if now:
                        scores(g, s, 1)
                    if nk > 1:
                        turn_probs(g, s - 2, 1)
                    if exists(g, s - 3):
                        values(g, s - 3, L.ntiles(s - 3) - 1)
                    if exists(g, s + 1):
                        turn_q(g, s + 1)
                    if ahead:
                        project(g, s + 2)
                    if exists(g, s - 4):
                        out_project(g, s - 4)
                    if nk > 2:
                        turn_probs(g, s - 2, 2)
                    if now:
                        scores(g, s, 2)
                    if nk > 1:
                        values(g, s - 2, 0)
                    if exists(g, s + 1):
                        turn_k(g, s + 1)
                    if nk > 3:
                        turn_probs(g, s - 2, 3)
                    if nk > 2:
                        values(g, s - 2, 1)
                    if now:
                        scores(g, s, 3)
                    if nk > 3:
                        values(g, s - 2, 2)

                rounds(pe, step_window if L is LA else step_causal)

            to_features(0)
            attention(LA, 0)
            to_features(1)
            attention(LB, 1)

            def logits(t):
                pe.wait_ge(v_htl, 2 * NT + t + 1)
                if t == 0:
                    pe.wait_ge(v_gate, 1)
                n = 0
                for k in range(KC):
                    for a in (hTh, hTl):
                        n += 1
                        last = mm(psY[:, t * 2 * NE:(t + 1) * 2 * NE], a[:, k, t * P:(t + 1) * P], gw[:, k, :],
                                  start=(t == 0 and n == 1), stop=(n == 2 * KC), skip_group_check=True)
                last.then_inc(s_rt, 1)

            to_features(2, logits)
            logits(NT - 2)
            logits(NT - 1)

            pe.wait_ge(v_pick, 1)
            pe.wait_ge(ld_before, 16)
            picks = picked[:, :, :].rearrange("p t e -> p (t e)")
            mm(psO[:, 0:NT * NE], before_s[:, :], picks, start=True, stop=True)
            mm(psP[:, 0:NT * NE], ones[:, :], picks, start=True, stop=True).then_inc(s_rank, 1)

            def turn_tokens(i, signal=None):
                wait(pe, ld_xg, 16 * (i + 1))
                wait(pe, v_x, i)
                for k in range(KC):
                    last = nc.tensor.transpose(psY[:, k * P:(k + 1) * P], xin[:, k * P:(k + 1) * P], idn[:, :])
                    if k == 0 and signal:
                        last.then_inc(signal, 1)
                last.then_inc(s_x, 1)

            def tokens_times(buf, m, h, ps):
                n = 0
                for k in range(KC):
                    at = (m * KC + k) * FF + h * 512
                    for a, w in ((xTh, wgt_hi), (xTl, wgt_hi), (xTh, wgt_lo)):
                        n += 1
                        last = mm(ps[:, :], a[:, k, :], w[buf][:, at:at + 512], start=(n == 1), stop=(n == 3 * KC))
                return last

            def turn_hidden(i, h):
                wait(pe, m_g, 2 * i + h + 1)
                for f in range(NF // 2):
                    last = nc.tensor.transpose(psG[h][:, f * P:(f + 1) * P], gated[:, h, f * P:(f + 1) * P], idn[:, :])
                last.then_inc(s_g, 1)

            def down(buf, h, chunks):
                for f in chunks:
                    at = 2 * KC * FF + (h * NF // 2 + f) * D
                    for n, (a, w) in enumerate(((gTh, wgt_hi), (gTl, wgt_hi), (gTh, wgt_lo))):
                        last = mm(psO[:, 0:D], a[:, h, f * P:(f + 1) * P], w[buf][:, at:at + D],
                                  start=(h == 0 and f == 0 and n == 0),
                                  stop=(h == 1 and f == NF // 2 - 1 and n == 2))
                return last

            def begin(e, buf, more):
                wait(pe, w_vl, 2 * e + 2)
                wait(pe, w_pl, 2 * e + 2)
                apart(pe)

            def tile(i, buf):
                wait(pe, v_x, i + 1)
                tokens_times(buf, 0, 0, psS[0]).then_inc(m_up, 1)
                tokens_times(buf, 1, 0, psX[0]).then_inc(m_gate, 1)
                tokens_times(buf, 0, 1, psS[1]).then_inc(m_up, 1)
                turn_hidden(i, 0)
                tokens_times(buf, 1, 1, psX[1]).then_inc(m_gate, 1)
                wait(pe, m_gl, 2 * i + 1)
                down(buf, 0, (0, 1))
                turn_hidden(i, 1)
                turn_tokens(i + 1)
                down(buf, 0, (2, 3))
                wait(pe, m_gl, 2 * i + 2)
                down(buf, 1, range(4)).then_inc(m_dn, 1)

            pe.wait_ge(v_slot, 1)
            turn_tokens(0, m_dn)
            experts(pe, begin, tile)

        @block.scalar
        def _(act):
            copy = lambda o, i: nc.scalar.activation(o, i, ACT.Copy)

            act.wait_ge(ld_c, 32)
            nc.scalar.activation(cE[:, :], cS[:, :], ACT.Exp, scale=-1.0).then_inc(a_ec, 1)

            def roots(n):
                act.wait_ge(v_var, n + 1)
                nc.scalar.activation(sd[:, :], vare[:, :], ACT.Sqrt).then_inc(a_root, 1)

            def features_hi(phase):
                for t in range(NT):
                    n = NT * phase + t
                    act.wait_ge(s_ht, n + 1)
                    copy(hTh[:, :, t * P:(t + 1) * P], psX[t % 2][:, 0:D].rearrange("p (k n) -> p k n", k=KC))\
                        .then_inc(a_hth, 1)

            def attention(L):
                def exp_head(g, s, j):
                    n = L.ntiles(s) * P
                    wait(act, v_max, L.head(g, s, j))
                    if j == 0 and L is LB:
                        wait(act, v_rden, L.unit(g, s - 4))
                    if j == 0 and L is LA:
                        wait(act, v_den, L.unit(g, s - 4))
                    pj = probs[:, s % 4, j, 0:n]
                    nc.scalar.activation(pj, pj, ACT.Exp, bias=nmax[:, s % 4, j:j + 1], scale=-1.0,
                                         accum_out=sums[:, s % 4, j:j + 1]).then_inc(a_exp, 1)

                def normalise(g, s):
                    wait(act, v_rden, L.unit(g, s))
                    for j in range(L.by_vector, QM):
                        pj = probs[:, s % 4, j, 0:L.ntiles(s) * P]
                        last = nc.scalar.activation(pj, pj, ACT.Copy, scale=rden[:, s % 4, j:j + 1])
                    last.then_inc(a_norm, 1)

                def sink_exp(g, s):
                    wait(act, g_es, L.unit(g, s))
                    wait(act, v_den, L.unit(g, s - 4))
                    nc.scalar.activation(esink[:, s % 4, :], esin[:, s % 4, :], ACT.Exp).then_inc(a_es, 1)

                def probs_hi(g, s, k):
                    slot = L.kt_slot(s, k)
                    wait(act, s_X, L.kt(g, s, k))
                    wait(act, s_PV, L.kt(g, s, k) - 2)
                    copy(pTh[:, slot, :], psX[slot][:, :]).then_inc(a_ph, 1)

                def out_hi(g, s):
                    wait(act, s_PV, L.kt_all(g, s))
                    wait(act, s_Y, L.unit(g, s - 2))
                    copy(oh[:, s % 2, :], psO[:, 0:2 * P]).then_inc(a_oh, 1)

                def project_hi(g, s):
                    wait(act, s_proj, L.unit(g, s))
                    if L is LB:
                        wait(act, s_tk, L.unit(g, s - 2))
                        copy(qn[:, s % 2, :, 0, :], psP[:, 0:HQ].rearrange("p (h d) -> p h d", d=HD))
                        copy(kn[:, s % 2, 0, :, :], psP[:, HQ:HQ + HD].unsqueeze(1).broadcast_to([P, 2, HD]))\
                            .then_inc(a_qh, 1)
                    else:
                        wait(act, v_rope, L.unit(g, s))
                    wait(act, s_PV, L.kt_all(g - 1, s % NT // TB * TB + TB - 1 + s // NT * NT))
                    copy(vpad[:, 0, s % NT, HD:2 * HD], psP[:, HQ + HD:QKV]).then_inc(a_vh, 1)

                def write_qT(g, s):
                    wait(act, s_tq, L.unit(g, s))
                    wait(act, s_S, L.head(g - 1, s, QM - 1))
                    copy(qT[:, s % NT, :], psT[:, :]).then_inc(a_tq, 1)

                def step_window(g, s):
                    now = exists(g, s)
                    back = exists(g, s - 1)
                    ahead = exists(g, s + 2)
                    nk = L.ntiles(s - 2) if exists(g, s - 2) else 0
                    if back:
                        sink_exp(g, s - 1)
                    if nk > 0:
                        probs_hi(g, s - 2, 0)
                    if now:
                        exp_head(g, s, 0)
                    if exists(g, s - 3):
                        out_hi(g, s - 3)
                    if nk > 1:
                        probs_hi(g, s - 2, 1)
                    if now:
                        exp_head(g, s, 1)
                    if back:
                        normalise(g, s - 1)
                    if exists(g, s + 1):
                        write_qT(g, s + 1)
                    if now:
                        exp_head(g, s, 2)
                    if ahead:
                        project_hi(g, s + 2)
                    if now:
                        exp_head(g, s, 3)

                def step_causal(g, s):
                    now = exists(g, s)
                    back = exists(g, s - 1)
                    ahead = exists(g, s + 2)
                    nk = L.ntiles(s - 2) if exists(g, s - 2) else 0
                    if now:
                        exp_head(g, s, 0)
                    if nk > 0:
                        probs_hi(g, s - 2, 0)
                    if exists(g, s - 3):
                        out_hi(g, s - 3)
                    if exists(g, s + 1):
                        write_qT(g, s + 1)
                    if back:
                        normalise(g, s - 1)
                    if nk > 1:
                        probs_hi(g, s - 2, 1)
                    if now:
                        exp_head(g, s, 1)
                    if nk > 2:
                        probs_hi(g, s - 2, 2)
                    if nk > 3:
                        probs_hi(g, s - 2, 3)
                    if ahead:
                        project_hi(g, s + 2)
                    if now:
                        exp_head(g, s, 2)
                        exp_head(g, s, 3)

                if L is LA:
                    act.wait_ge(p_init, 1)
                rounds(act, step_window if L is LA else step_causal)

            act.wait_ge(ld_k, 16 * N_CONST)
            copy(bias[:, :], biasraw).then_inc(a_bias, 1)
            copy(yN[:, :, :], outb_b[:, :].unsqueeze(1).broadcast_to([P, NT, D])).then_inc(a_yi, 1)

            def squares(ready):
                for t in range(NT):
                    act.wait_ge(*ready(t))
                    nc.scalar.activation(uN[:, t, :], yN[:, t, :], ACT.Square, accum_out=ssq[:, t:t + 1]).then_inc(a_sq, 1)

            roots(0)
            features_hi(0)
            attention(LA)
            roots(1)
            squares(lambda t: (v_u, t + 1))
            roots(2)
            features_hi(1)
            attention(LB)
            squares(lambda t: (v_y, LB.unit(NKV - 1, t)))
            roots(3)
            features_hi(2)

            act.wait_ge(v_lmax, 1)
            nc.scalar.activation(pr[:, :, :], logit[:, :, :], ACT.Exp).then_inc(a_rt, 1)

            def split_hi(e, buf):
                wait(act, ld_v, 16 * (e + 1))
                for j in range(2):
                    at = slice(j * EP, (j + 1) * EP)
                    copy(wgt_hi[buf][:, at], mrawV[:, at]).then_inc(w_vh, 1)

            def load_tokens(i):
                act.dma_start(xin[:, :], xg[bass.ds(i * P, P), :]).then_inc(ld_xg, 16)

            def tokens_hi(i):
                wait(act, s_x, i + 1)
                load_tokens(i + 1)
                copy(xTh[:, :, :], psY[:, 0:D].rearrange("p (k n) -> p k n", k=KC)).then_inc(a_x, 1)

            def begin(e, buf, more):
                if more:
                    split_hi(e + 1, 1 - buf)

            def output(i):
                wait(act, m_dn, i + 1)
                wait(act, st_y, 16 * i + 16)
                copy(ysb[:, :], psO[:, 0:D]).then_inc(a_y, 1)
                wait(act, a_y, i + 1)
                act.dma_start(yg[bass.ds(i * P, P), :], ysb[:, :]).then_inc(st_y, 16)

            def tile(i, buf):
                output(i)
                for h in range(2):
                    wait(act, m_up, 2 * i + h + 1)
                    nc.scalar.activation(relu_s[:, h, :], psS[h][:, :], ACT.Relu).then_inc(m_relu, 1)
                    if h == 0:
                        hidden_hi(i, 0)
                hidden_hi(i, 1)
                tokens_hi(i + 1)

            def hidden_hi(i, h):
                wait(act, s_g, 2 * i + h + 1)
                copy(gTh[:, h, :], psG[h][:, :]).then_inc(m_gh, 1)

            split_hi(0, 0)
            for j in range(2):
                act.wait_ge(ld_p[j], 16)
                copy(wgt_hi[0][:, EV + j * EP:EV + (j + 1) * EP], mrawP[:, j, :]).then_inc(w_ph, 1)
            act.wait_ge(st_xg, 16 * 2 * NT)
            load_tokens(0)
            tokens_hi(0)
            experts(act, begin, tile)
            tiles = first_tile_of(act, NE)
            output(tiles)
            act.wait_ge(ld_xg, 16 * (tiles + 2))
            apart(act)

        @block.vector
        def _(dve):
            V = nc.vector
            reached = {}

            def link(ins, signal=v_seq):
                reached[signal.name] = reached.get(signal.name, 0) + 1
                ins.then_inc(signal, 1)
                dve.wait_ge(signal, reached[signal.name])

            def layer_norm(src, n):
                for t in range(NT):
                    if n:
                        dve.wait_ge(g_x, t + 1)
                    V.bn_stats(stats[:, t, :], src[:, t, :]).then_inc(v_stat, 1)
                dve.wait_ge(v_stat, NT * (n + 1))
                for t in range(NT):
                    V.bn_aggr(mv[:, t, :], stats[:, t, :]).then_inc(v_aggr, 1)
                dve.wait_ge(v_aggr, NT * (n + 1))
                link(V.tensor_scalar(vare[:, :], mv[:, :, 1], EPS, None, ALU.add), v_var)

            link(V.memset(pick[:, :].bitcast(F32), 0.0))
            link(V.memset(ones[:, :], 1.0))
            for row in (0, 32):
                link(V.tensor_copy(pick[row:row + 1, :], ones[row:row + 1, :]))
            dve.wait_ge(a_ec, 1)
            link(V.tensor_scalar(cD[:, :], cE[:, :], 1.0, None, ALU.add))
            link(V.reciprocal(cR[:, :], cD[:, :]))
            link(V.tensor_tensor(cD[:, :], cS[:, :], cR[:, :], ALU.mult))
            for n in range(KC * BATCH):
                link(V.tensor_scalar(cB[:, n, :], ones[:, :], cD[:, n:n + 1], None, ALU.mult), v_cb)

            def modulation_rows(n):
                c, b = n // BATCH, n % BATCH
                dve.wait_ge(s_mod, n + 1)
                V.tensor_copy(modb[:, b, c * 512:(c + 1) * 512], psS[n % 2][:, :]).then_inc(v_mod, 1)

            dve.wait_ge(ld_x, 16)
            modulation_rows(0)
            modulation_rows(1)
            layer_norm(xN, 0)
            modulation_rows(2)
            dve.wait_ge(ld_k, 16 * N_CONST)
            dve.wait_ge(a_bias, 1)
            modulation_rows(3)
            link(V.tensor_tensor(bias[32:33, :], biasraw[32:33, :], bias[32:33, :], ALU.subtract))
            SA, CA, GA, SB, CB, GB = (modb[:, :, i * D:(i + 1) * D] for i in range(6))
            dve.wait_ge(v_mod, 4)
            link(V.tensor_scalar(CA, CA, 1.0, None, ALU.add))

            def first_features(t):
                modulate(hb[:, t % 2, :], xN, t, CA, SA).then_inc(v_h, 1)
                if t < BATCH:
                    modulation_rows(2 * BATCH + t)
                if t == BATCH:
                    dve.wait_ge(v_mod, 6)
                    link(V.tensor_scalar(CB, CB, 1.0, None, ALU.add))
                    link(V.tensor_copy(gw[:, :, 0:NE], graw[:, :, :]))
                    link(V.tensor_tensor(gw[:, :, NE:2 * NE], graw[:, :, :], gw[:, :, 0:NE], ALU.subtract), v_gate)

            def finish_roots(n):
                dve.wait_ge(a_root, n + 1)
                link(V.reciprocal(rs[:, :], sd[:, :]))

            def mean_square(n):
                dve.wait_ge(a_sq, NT * (n + 1))
                link(V.tensor_scalar(vare[:, :], ssq[:, :], 1.0 / D, EPS, ALU.mult, ALU.add), v_var)

            def modulate(dst, src, t, c, s):
                b = t // TB
                link(V.scalar_tensor_tensor(dst, src[:, t, :], mv[:, t, 0:1], c[:, b, :], ALU.subtract, ALU.mult))
                return V.scalar_tensor_tensor(dst, dst, rs[:, t:t + 1], s[:, b, :], ALU.mult, ALU.add)

            def features_lo(phase, t):
                n = NT * phase + t
                dve.wait_ge(a_hth, n + 1)
                V.tensor_tensor(hTl[:, :, t * P:(t + 1) * P], psX[t % 2][:, 0:D].rearrange("p (k n) -> p k n", k=KC),
                                hTh[:, :, t * P:(t + 1) * P], ALU.subtract).then_inc(v_htl, 1)

            def features(phase, make):
                for t in range(NT):
                    if phase < 2:
                        wait(dve, s_ht, NT * phase + t + 1 - 2)
                    make(t)
                    if t:
                        features_lo(phase, t - 1)
                features_lo(phase, NT - 1)

            def attention(L):
                def mask_max(g, s, j):
                    n = L.ntiles(s) * P
                    wait(dve, s_S, L.head(g, s, j))
                    if j == 0:
                        wait(dve, s_X, L.kt_all(g, s - 4))
                    apart(dve)
                    mask = mwin[:, 2 * P - n:] if L is LA else mcau[:, SEQ - n:]
                    V.tensor_tensor_reduce(probs[:, s % 4, j, 0:n], psS[j % 2][:, 0:n], mask, -SCALE, 3e38,
                                           ALU.add, ALU.min, nmax[:, s % 4, j:j + 1]).then_inc(v_max, 1)

                def normalise(g, s):
                    wait(dve, a_exp, L.head(g, s, QM - 1))
                    d = sums
                    if L is LA:
                        wait(dve, a_es, L.unit(g, s))
                        V.tensor_tensor(den[:, s % 4, :], sums[:, s % 4, :], esink[:, s % 4, :], ALU.add).then_inc(v_den, 1)
                        wait(dve, v_den, L.unit(g, s))
                        d = den
                    V.reciprocal(rden[:, s % 4, :], d[:, s % 4, :]).then_inc(v_rden, 1)
                    wait(dve, v_rden, L.unit(g, s))
                    n = L.ntiles(s) * P
                    for j in range(L.by_vector):
                        pj = probs[:, s % 4, j, 0:n]
                        last = V.tensor_scalar(pj, pj, rden[:, s % 4, j:j + 1], None, ALU.mult)
                    last.then_inc(v_norm, 1)

                def probs_lo(g, s, k):
                    slot = L.kt_slot(s, k)
                    wait(dve, a_ph, L.kt(g, s, k))
                    V.tensor_tensor(pTl[:, slot, :], psX[slot][:, :], pTh[:, slot, :], ALU.subtract).then_inc(v_pl, 1)

                def out_lo(g, s):
                    wait(dve, a_oh, L.unit(g, s))
                    V.tensor_tensor(ol[:, s % 2, :], psO[:, 0:2 * P], oh[:, s % 2, :], ALU.subtract).then_inc(v_ol, 1)

                def rotate(g, s):
                    wait(dve, s_proj, L.unit(g, s))
                    qkp = psP[:, 0:HQ + HD]
                    wait(dve, g_add, L.unit(g, s - 1))
                    t = s % TB
                    heads = qkp.rearrange("p (h d) -> p h d", d=HD)
                    V.tensor_tensor(t1[:, :, :], heads, cosw[:, t, :].unsqueeze(1).broadcast_to([P, QM + 1, HD]),
                                    ALU.mult)
                    halves = qkp.rearrange("p (h r d) -> p h r d", r=2, d=HD // 2)
                    t2h = t2[:, :, :].rearrange("p h (r d) -> p h r d", r=2)
                    sinr = sinw[:, t, :].rearrange("p (r d) -> p r d", r=2)
                    for r in range(2):
                        last = V.tensor_tensor(t2h[:, :, r, :], halves[:, :, 1 - r, :],
                                               sinr[:, r, :].unsqueeze(1).broadcast_to([P, QM + 1, HD // 2]), ALU.mult)
                    last.then_inc(v_rope, 1)

                def project_lo(g, s):
                    wait(dve, a_vh, L.unit(g, s))
                    if L is LB:
                        V.tensor_tensor(qn[:, s % 2, :, 1, :], psP[:, 0:HQ].rearrange("p (h d) -> p h d", d=HD),
                                        qn[:, s % 2, :, 0, :], ALU.subtract)
                        V.tensor_tensor(kn[:, s % 2, 1, :, :], psP[:, HQ:HQ + HD].unsqueeze(1).broadcast_to([P, 2, HD]),
                                        kn[:, s % 2, 0, :, :], ALU.subtract).then_inc(qk_lo, 1)
                    V.tensor_tensor(vpad[:, 1, s % NT, HD:2 * HD], psP[:, HQ + HD:QKV], vpad[:, 0, s % NT, HD:2 * HD],
                                    ALU.subtract).then_inc(v_vl, 1)

                def write_kT(g, s):
                    wait(dve, s_tk, L.unit(g, s))
                    wait(dve, s_S, L.head(g - 1, s % NT // TB * TB + TB - 1 + s // NT * NT, QM - 1))
                    V.tensor_copy(kT[:, :, s % NT * P:(s % NT + 1) * P], psT[:, 0:2 * P].rearrange("p (c n) -> p c n", c=2))\
                     .then_inc(v_tk, 1)

                def add_y(g, s):
                    wait(dve, s_Y, L.unit(g, s))
                    yt = yN[:, s % NT, :]
                    wait(dve, v_y, L.unit(g, s - 1))
                    V.tensor_tensor(yt, psY[:, 0:D], yt, ALU.add).then_inc(v_y, 1)

                def step_window(g, s):
                    now = exists(g, s)
                    back = exists(g, s - 1)
                    ahead = exists(g, s + 2)
                    nk = L.ntiles(s - 2) if exists(g, s - 2) else 0
                    if back:
                        normalise(g, s - 1)
                    if now:
                        mask_max(g, s, 0)
                        mask_max(g, s, 1)
                    if nk > 0:
                        probs_lo(g, s - 2, 0)
                    if ahead:
                        rotate(g, s + 2)
                    if exists(g, s - 3):
                        out_lo(g, s - 3)
                    if now:
                        mask_max(g, s, 2)
                        mask_max(g, s, 3)
                    if nk > 1:
                        probs_lo(g, s - 2, 1)
                    if exists(g, s - 4):
                        add_y(g, s - 4)
                    if ahead:
                        project_lo(g, s + 2)
                    if exists(g, s + 1):
                        write_kT(g, s + 1)

                def step_causal(g, s):
                    now = exists(g, s)
                    back = exists(g, s - 1)
                    ahead = exists(g, s + 2)
                    nk = L.ntiles(s - 2) if exists(g, s - 2) else 0
                    if now:
                        mask_max(g, s, 0)
                    if back:
                        normalise(g, s - 1)
                    if now:
                        mask_max(g, s, 1)
                    if nk > 0:
                        probs_lo(g, s - 2, 0)
                    if exists(g, s - 3):
                        out_lo(g, s - 3)
                    if nk > 1:
                        probs_lo(g, s - 2, 1)
                    if exists(g, s - 4):
                        add_y(g, s - 4)
                    if now:
                        mask_max(g, s, 2)
                    if exists(g, s + 1):
                        write_kT(g, s + 1)
                    if nk > 2:
                        probs_lo(g, s - 2, 2)
                    if now:
                        mask_max(g, s, 3)
                    if nk > 3:
                        probs_lo(g, s - 2, 3)
                    if ahead:
                        project_lo(g, s + 2)

                rounds(dve, step_window if L is LA else step_causal)

            finish_roots(0)
            dve.wait_ge(a_yi, 1)
            features(0, first_features)
            attention(LA)

            layer_norm(xN, 1)
            finish_roots(1)
            for t in range(NT):
                modulate(yN[:, t, :], xN, t, CB, SB).then_inc(v_u, 1)
            mean_square(0)
            finish_roots(2)
            features(1, lambda t: V.scalar_tensor_tensor(hb[:, t % 2, :], yN[:, t, :], rs[:, t:t + 1], ln1_b[:, :],
                                                         ALU.mult, ALU.mult).then_inc(v_h, 1))
            attention(LB)

            mean_square(1)
            finish_roots(3)
            features(2, lambda t: V.scalar_tensor_tensor(hAll[:, t, :], yN[:, t, :], rs[:, t:t + 1], ln2_b[:, :],
                                                         ALU.mult, ALU.mult).then_inc(v_h, 1))

            dve.wait_ge(s_rt, NT)
            parts = psY[:, 0:NT * 2 * NE].rearrange("p (t c e) -> p t c e", c=2, e=NE)
            link(V.tensor_copy(logit[:, :, :], parts[:, :, 0, :]))
            link(V.tensor_tensor(logit[:, :, :], logit[:, :, :], parts[:, :, 1, :], ALU.add))
            link(V.tensor_reduce(lmax[:, :], logit[:, :, :], mybir.AxisListType.X, ALU.max))
            link(V.tensor_tensor(logit[:, :, :], logit[:, :, :], lmax[:, :].unsqueeze(2).broadcast_to([P, NT, NE]),
                                 ALU.subtract), v_lmax)
            dve.wait_ge(a_rt, 1)
            link(V.tensor_reduce(prs[:, :], pr[:, :, :], mybir.AxisListType.X, ALU.add))
            link(V.reciprocal(prr[:, :], prs[:, :]))
            link(V.tensor_tensor(pr[:, :, :], pr[:, :, :], prr[:, :].unsqueeze(2).broadcast_to([P, NT, NE]), ALU.mult))
            for t in range(NT):
                last = V.max(top[:, t, :], pr[:, t, :])
            link(last)
            for t in range(NT):
                last = V.max_index(topi[:, t, :], top[:, t, :], pr[:, t, :])
            link(last)
            link(V.tensor_copy(topf[:, :, :], topi[:, :, :]))
            link(V.tensor_tensor(tops[:, :], top[:, :, 0], top[:, :, 1], ALU.add))
            link(V.reciprocal(topr[:, :], tops[:, :]))
            link(V.tensor_tensor(topw[:, :, :], top[:, :, 0:2], topr[:, :].unsqueeze(2).broadcast_to([P, NT, 2]), ALU.mult))
            idb = ids[:, :].unsqueeze(1).broadcast_to([P, NT, NE])
            for i, c in ((0, c0), (1, c1)):
                link(V.tensor_tensor(c[:, :, :], idb, topf[:, :, i:i + 1].broadcast_to([P, NT, NE]), ALU.is_equal))
            link(V.tensor_tensor(picked[:, :, :], c0[:, :, :], c1[:, :, :], ALU.add), v_pick)

            link(V.memset(ahead[:, 0, :], 0.0))
            link(V.memset(base[:, 0:1], 0.0))
            link(V.memset(bound[:, 0:1], -1.0))
            for k in range(1, NT):
                last = V.memset(bound[:, k:k + 1], float(k * P))
            link(last)
            dve.wait_ge(s_rank, 1)
            link(V.tensor_copy(total[:, :, :], psP[:, 0:NT * NE].rearrange("p (t e) -> p t e", e=NE)))
            for t in range(NT):
                link(V.tensor_tensor(ahead[:, t + 1, :], ahead[:, t, :], total[:, t, :], ALU.add))
            link(V.tensor_tensor(slotf[:, :, :], psO[:, 0:NT * NE].rearrange("p (t e) -> p t e", e=NE),
                                 ahead[:, 0:NT, :], ALU.add))
            link(V.tensor_tensor(above[:, :, :], ahead[:, NT, :].unsqueeze(2).broadcast_to([P, NE, NT]),
                                 bound[:, :].unsqueeze(1).broadcast_to([P, NE, NT]), ALU.is_gt))
            link(V.tensor_reduce(ntil[:, :], above[:, :, :], mybir.AxisListType.X, ALU.add))
            for e in range(NE):
                link(V.tensor_tensor(base[:, e + 1:e + 2], base[:, e:e + 1], ntil[:, e:e + 1], ALU.add))
            link(V.tensor_copy(base_i[:, :], base[:, :]))
            link(V.scalar_tensor_tensor(slotf[:, :, :], base[:, 0:NE].unsqueeze(1).broadcast_to([P, NT, NE]), float(P),
                                        slotf[:, :, :], ALU.mult, ALU.add))
            for i, c in ((0, c0), (1, c1)):
                link(V.tensor_tensor(chosen[:, i, :, :], slotf[:, :, :], c[:, :, :], ALU.mult))
                link(V.tensor_reduce(slotr[:, i * NT:(i + 1) * NT], chosen[:, i, :, :], mybir.AxisListType.X, ALU.add))
            link(V.tensor_copy(slots[:, :], slotr[:, :]), v_slot)
            s0, s1 = slotr[:, 0:NT], slotr[:, NT:2 * NT]
            link(V.tensor_tensor(order[:, 0, :], s0, s1, ALU.min))
            link(V.tensor_tensor(order[:, 1, :], s0, s1, ALU.max))
            link(V.tensor_scalar(slots_out[:, :], order[:, :, :].rearrange("p i t -> p (i t)"), float(P), None, ALU.add),
                 v_slot)
            link(V.tensor_tensor(order[:, 0, :], s0, s1, ALU.is_lt))
            link(V.tensor_tensor(order[:, 1, :], s0, s1, ALU.is_gt))
            for i in range(2):
                link(V.tensor_tensor(share[:, i, :], topw[:, :, 0], order[:, i, :], ALU.mult))
                link(V.tensor_tensor(slotr[:, 0:NT], topw[:, :, 1], order[:, 1 - i, :], ALU.mult))
                link(V.tensor_tensor(share[:, i, :], share[:, i, :], slotr[:, 0:NT], ALU.add))

            def split_lo(e, buf):
                for j in range(2):
                    at = slice(j * EP, (j + 1) * EP)
                    wait(dve, w_vh, 2 * e + j + 1)
                    V.tensor_tensor(wgt_lo[buf][:, at], mrawV[:, at], wgt_hi[buf][:, at], ALU.subtract).then_inc(w_vl, 1)

            def tokens_lo(i):
                wait(dve, a_x, i + 1)
                V.tensor_tensor(xTl[:, :, :], psY[:, 0:D].rearrange("p (k n) -> p k n", k=KC), xTh[:, :, :],
                                ALU.subtract).then_inc(v_x, 1)

            def begin(e, buf, more):
                if more:
                    split_lo(e + 1, 1 - buf)

            def tile(i, buf):
                def gate(h):
                    wait(dve, m_gate, 2 * i + h + 1)
                    wait(dve, m_relu, 2 * i + h + 1)
                    V.tensor_tensor(gated[:, h, :], psX[h][:, :], relu_s[:, h, :], ALU.mult).then_inc(m_g, 1)

                def hidden_lo(h):
                    wait(dve, m_gh, 2 * i + h + 1)
                    V.tensor_tensor(gTl[:, h, :], psG[h][:, :], gTh[:, h, :], ALU.subtract).then_inc(m_gl, 1)

                gate(0)
                hidden_lo(0)
                gate(1)
                hidden_lo(1)
                tokens_lo(i + 1)

            split_lo(0, 0)
            for j in range(2):
                at = slice(EV + j * EP, EV + (j + 1) * EP)
                dve.wait_ge(w_ph, j + 1)
                V.tensor_tensor(wgt_lo[0][:, at], mrawP[:, j, :], wgt_hi[0][:, at], ALU.subtract).then_inc(w_pl, 1)
            tokens_lo(0)
            experts(dve, begin, tile)

            for t in range(NT):
                dve.wait_ge(ld_g[0][t], 16)
                link(V.scalar_tensor_tensor(yN[:, t, :], hAll[:, t, :], share[:, 0, t:t + 1], yN[:, t, :], ALU.mult, ALU.add))
            for t in range(NT):
                b = t // TB
                dve.wait_ge(ld_g[1][t], 16)
                link(V.scalar_tensor_tensor(yN[:, t, :], second[:, t, :], share[:, 1, t:t + 1], yN[:, t, :], ALU.mult, ALU.add))
                link(V.tensor_tensor(yN[:, t, :], yN[:, t, :], GB[:, b, :], ALU.mult))
                V.tensor_tensor(xN[:, t, :], xN[:, t, :], yN[:, t, :], ALU.add).then_inc(v_out, 1)


def _tables():
    import math
    import numpy as np

    theta, scaling, alpha, beta, icl = 150000.0, 32.0, 1.0, 32.0, 128
    half = HD // 2
    freq = theta ** (np.arange(0, HD, 2, dtype=np.float32) / HD)
    concentration = 0.1 * math.log(scaling) + 1.0
    low = half * math.log(icl / (beta * 2 * math.pi)) / math.log(theta)
    high = half * math.log(icl / (alpha * 2 * math.pi)) / math.log(theta)
    ramp = np.clip((np.arange(half, dtype=np.float32) - low) / (high - low), 0.0, 1.0)
    keep = 1.0 - ramp
    inv_freq = 1.0 / (scaling * freq) * (1.0 - keep) + 1.0 / freq * keep
    freqs = np.outer(np.arange(SEQ, dtype=np.float32), inv_freq)
    cos = (np.cos(freqs) * concentration).astype(np.float32)
    sin = (np.sin(freqs) * concentration).astype(np.float32)
    by_tile = lambda a: np.ascontiguousarray(a.reshape(TB, P, HD).transpose(1, 0, 2))
    cosw = by_tile(np.concatenate([cos, cos], 1))
    sinw = by_tile(np.concatenate([-sin, sin], 1))
    i, j = np.arange(P)[:, None], np.arange(P)[None, :]
    causal = np.where(j > i, NEG, 0.0)
    before = np.where(j <= i, NEG, 0.0)
    mask_win = np.concatenate([before, causal], 1).astype(np.float32)
    mask_causal = np.concatenate([np.zeros((P, SEQ - P)), causal], 1).astype(np.float32)
    return {"rope_cos": cosw, "rope_sin": sinw, "mask_win": mask_win, "mask_causal": mask_causal,
            "ident": np.eye(P, dtype=np.float32), "expert_ids": np.arange(NE, dtype=np.float32),
            "before": np.triu(np.ones((P, P), np.float32), 1)}


def kernel(L0_attn_x, L0_attn_qkv_w, L0_attn_qkv_b, L0_attn_out_w, L0_attn_out_b, L0_attn_sinks,
           L0_ffn_ln1_w, L0_ffn_wq, L0_ffn_wk, L0_ffn_wv, L0_ffn_wo, L0_ffn_ln2_w, L0_ffn_gate_w,
           L0_ffn_w1, L0_ffn_w2, L0_ffn_w3, L0_c, L0_wmod):
    import numpy as np
    import concourse.bacc as bacc
    from concourse.bass_utils import run_bass_kernel_spmd

    arr = np.asarray

    def by_round(wq, wk, wv):
        a = np.concatenate([arr(wq).reshape(KC, P, NKV, HQ), arr(wk).reshape(KC, P, NKV, HD),
                            arr(wv).reshape(KC, P, NKV, HD)], 3)
        return a.transpose(2, 1, 0, 3).reshape(NKV, P, KC * QKV)

    def out_by_round(wo):
        return arr(wo).reshape(NKV, 2, P, D).transpose(0, 2, 1, 3).reshape(NKV, P, 2 * D)

    nq, nk = NKV * HQ, NKV * HD
    wt = arr(L0_attn_qkv_w).T
    b = arr(L0_attn_qkv_b)
    bias = np.concatenate([b[:nq].reshape(NKV, HQ), b[nq:nq + nk].reshape(NKV, HD), b[nq + nk:].reshape(NKV, HD)], 1)
    by_rows = lambda w: arr(w).reshape(NE, -1, P, arr(w).shape[2]).transpose(0, 2, 1, 3).reshape(NE, P, -1)
    w_moe = np.concatenate([by_rows(L0_ffn_w1), by_rows(L0_ffn_w3), by_rows(L0_ffn_w2)], 2)
    tables = _tables()
    ins = {
        "x": arr(L0_attn_x),
        "w_attn": by_round(wt[:, :nq], wt[:, nq:nq + nk], wt[:, nq + nk:]),
        "wo_attn": out_by_round(arr(L0_attn_out_w).T),
        "b_attn": bias.reshape(-1),
        "outb": arr(L0_attn_out_b),
        "sinks": arr(L0_attn_sinks),
        "w_ffn": by_round(L0_ffn_wq, L0_ffn_wk, L0_ffn_wv),
        "wo_ffn": out_by_round(L0_ffn_wo),
        "ln1": arr(L0_ffn_ln1_w),
        "ln2": arr(L0_ffn_ln2_w),
        "gate": arr(L0_ffn_gate_w).reshape(KC, P, NE).transpose(1, 0, 2),
        "w_moe": w_moe,
        "cT": arr(L0_c).T.reshape(KC, P, BATCH).transpose(1, 0, 2).reshape(P, KC * BATCH),
        "wmod": arr(L0_wmod).reshape(KC, P, NMOD).transpose(1, 0, 2),
    }
    ins.update({k: tables[k] for k in ("rope_cos", "rope_sin", "mask_win", "mask_causal", "ident", "expert_ids",
                                     "before")})
    nc = bacc.Bacc("TRN2", target_bir_lowering=False, num_devices=1)
    arrays, args = {}, []
    for name, a in ins.items():
        arrays[f"in_{name}"] = np.ascontiguousarray(a)
        args.append(nc.dram_tensor(f"in_{name}", a.shape, mybir.dt.from_np(a.dtype), kind="ExternalInput").ap())
    for name in ("xg", "yg"):
        args.append(nc.dram_tensor(name, ((MAXT + 2) * P, D), F32, kind="Internal").ap())
    args.append(nc.dram_tensor("out_x", (BATCH, SEQ, D), F32, kind="ExternalOutput").ap())
    build(nc, *args)
    r = run_bass_kernel_spmd(nc, [arrays], core_ids=[0])
    return r.results[0]["out_x"]
```
